# Optimizing a Trainium2 kernel written in Bass

```python
import numpy as np
import jax
import jax.numpy as jnp

def _softmax(x, axis=-1):
    return jax.nn.softmax(x, axis=axis)

def _gelu(x):
    return jax.nn.gelu(x, approximate=True)

def _silu(x):
    return jax.nn.silu(x)

def _sigmoid(x):
    return jax.nn.sigmoid(x)

def _layernorm(x, axis=-1, eps=1e-05):
    m = jnp.mean(x, axis=axis, keepdims=True)
    v = jnp.var(x, axis=axis, keepdims=True)
    return (x - m) / jnp.sqrt(v + eps)

def _scatter_add(tgt, idx, src, axis=0):
    return tgt.at[idx].add(src)

def _segment_sum(src, seg, n):
    return jax.ops.segment_sum(src, seg, n)
kernel_name = 'mk_seq_preln_d1_jaxref_r4_cf9b87'

def setup_inputs(seed: int=0):
    np.random.seed(seed)
    _w = jnp.asarray

    def _L0_attn_setup():
        import jax, jax.numpy as jnp
        import numpy as np
        D_MODEL = 256
        STATE = 64
        HEADS = 8
        EXPAND = 2
        INNER = EXPAND * D_MODEL
        HEAD_DIM = INNER // HEADS
        PROJ_OUT = 2 * INNER + 2 * STATE + HEADS
        BATCH, SEQ = (2, 256)
        EPS = 1e-05

        def _layer_norm(x, gamma, beta):
            mu = jnp.mean(x, axis=-1, keepdims=True)
            xc = x - mu
            var = jnp.mean(xc * xc, axis=-1, keepdims=True)
            return xc * jax.lax.rsqrt(var + EPS) * gamma + beta

        def _mamba2(u, W_in, b_in, A_log, D_skip, dt_bias, W_out, b_out):
            B, L, _ = u.shape
            zxbcdt = u @ W_in + b_in
            z = zxbcdt[..., :INNER]
            xs = zxbcdt[..., INNER:2 * INNER].reshape(B, L, HEADS, HEAD_DIM)
            Bm = zxbcdt[..., 2 * INNER:2 * INNER + STATE]
            Cm = zxbcdt[..., 2 * INNER + STATE:2 * INNER + 2 * STATE]
            dt = jax.nn.softplus(zxbcdt[..., 2 * INNER + 2 * STATE:] + dt_bias)
            A = -jnp.exp(A_log)
            decay = jnp.exp(dt * A)
            dtx = dt[..., None] * xs

            def step(h, inp):
                dec_t, dtx_t, B_t, C_t = inp
                h = dec_t[:, :, None, None] * h + dtx_t[..., None] * B_t[:, None, None, :]
                y = jnp.einsum('bhpn,bn->bhp', h, C_t)
                return (h, y)
            h0 = jnp.zeros((B, HEADS, HEAD_DIM, STATE), u.dtype)
            scan_in = (jnp.moveaxis(decay, 1, 0), jnp.moveaxis(dtx, 1, 0), jnp.moveaxis(Bm, 1, 0), jnp.moveaxis(Cm, 1, 0))
            _, ys = jax.lax.scan(step, h0, scan_in)
            y = jnp.moveaxis(ys, 0, 1)
            y = y + D_skip[None, None, :, None] * xs
            y = y.reshape(B, L, INNER) * jax.nn.silu(z)
            return y @ W_out + b_out
        key = jax.random.key(seed)
        ks = jax.random.split(key, 6)
        g = lambda k, shape, sc: jax.random.normal(k, shape, jnp.float32) * sc
        return {'input_tensor': jax.random.normal(ks[0], (BATCH, SEQ, D_MODEL), jnp.float32), 'ln_gamma': jnp.ones((D_MODEL,), jnp.float32), 'ln_beta': jnp.zeros((D_MODEL,), jnp.float32), 'W_in': g(ks[1], (D_MODEL, PROJ_OUT), 0.02), 'b_in': jnp.zeros((PROJ_OUT,), jnp.float32), 'A_log': jnp.log(jnp.arange(1, HEADS + 1, dtype=jnp.float32)), 'D_skip': jnp.ones((HEADS,), jnp.float32), 'dt_bias': g(ks[2], (HEADS,), 0.1), 'W_out': g(ks[3], (INNER, D_MODEL), 0.02), 'b_out': jnp.zeros((D_MODEL,), jnp.float32)}
    _L0_attn_in = _L0_attn_setup()

    def _L0_ffn_setup():
        import jax, jax.numpy as jnp
        import numpy as np
        D, H, N, K = (256, 512, 8, 2)
        B, S = (4, 512)
        key = jax.random.key(seed)
        ks = jax.random.split(key, 4)
        x = jax.random.normal(ks[0], (B, S, D), dtype=jnp.float32)
        Wr = jax.random.normal(ks[1], (N, D), dtype=jnp.float32) / np.sqrt(D)
        br = jnp.zeros((N,), jnp.float32)
        Wl1 = jax.random.normal(ks[2], (N, D, 2 * H), dtype=jnp.float32) / np.sqrt(D)
        bl1 = jnp.zeros((N, 2 * H), jnp.float32)
        Wl2 = jax.random.normal(ks[3], (N, H, D), dtype=jnp.float32) / np.sqrt(H)
        bl2 = jnp.zeros((N, D), jnp.float32)
        biases_N = jnp.zeros((N,), jnp.float32)
        return {'x': x, 'Wr': Wr, 'br': br, 'Wl1': Wl1, 'bl1': bl1, 'Wl2': Wl2, 'bl2': bl2, 'biases_N': biases_N}
    _L0_ffn_in = _L0_ffn_setup()
    _d = {'L0_attn_input_tensor': _L0_attn_in['input_tensor'], 'L0_attn_ln_gamma': _L0_attn_in['ln_gamma'], 'L0_attn_ln_beta': _L0_attn_in['ln_beta'], 'L0_attn_W_in': _L0_attn_in['W_in'], 'L0_attn_b_in': _L0_attn_in['b_in'], 'L0_attn_A_log': _L0_attn_in['A_log'], 'L0_attn_D_skip': _L0_attn_in['D_skip'], 'L0_attn_dt_bias': _L0_attn_in['dt_bias'], 'L0_attn_W_out': _L0_attn_in['W_out'], 'L0_attn_b_out': _L0_attn_in['b_out'], 'L0_ffn_Wr': _L0_ffn_in['Wr'], 'L0_ffn_br': _L0_ffn_in['br'], 'L0_ffn_Wl1': _L0_ffn_in['Wl1'], 'L0_ffn_bl1': _L0_ffn_in['bl1'], 'L0_ffn_Wl2': _L0_ffn_in['Wl2'], 'L0_ffn_bl2': _L0_ffn_in['bl2'], 'L0_ffn_biases_N': _L0_ffn_in['biases_N']}
    _x0 = _d['L0_attn_input_tensor']
    _d['L0_attn_input_tensor'] = jax.random.normal(jax.random.fold_in(jax.random.key(seed), 1), (4, 1024, 256), dtype=_x0.dtype)
    del _x0
    return _d

def reference(L0_attn_input_tensor, L0_attn_ln_gamma, L0_attn_ln_beta, L0_attn_W_in, L0_attn_b_in, L0_attn_A_log, L0_attn_D_skip, L0_attn_dt_bias, L0_attn_W_out, L0_attn_b_out, L0_ffn_Wr, L0_ffn_br, L0_ffn_Wl1, L0_ffn_bl1, L0_ffn_Wl2, L0_ffn_bl2, L0_ffn_biases_N):

    def _L0_attn_ref(input_tensor, ln_gamma, ln_beta, W_in, b_in, A_log, D_skip, dt_bias, W_out, b_out):
        import jax, jax.numpy as jnp
        import numpy as np
        D_MODEL = 256
        STATE = 64
        HEADS = 8
        EXPAND = 2
        INNER = EXPAND * D_MODEL
        HEAD_DIM = INNER // HEADS
        PROJ_OUT = 2 * INNER + 2 * STATE + HEADS
        BATCH, SEQ = (2, 256)
        EPS = 1e-05

        def _layer_norm(x, gamma, beta):
            mu = jnp.mean(x, axis=-1, keepdims=True)
            xc = x - mu
            var = jnp.mean(xc * xc, axis=-1, keepdims=True)
            return xc * jax.lax.rsqrt(var + EPS) * gamma + beta

        def _mamba2(u, W_in, b_in, A_log, D_skip, dt_bias, W_out, b_out):
            B, L, _ = u.shape
            zxbcdt = u @ W_in + b_in
            z = zxbcdt[..., :INNER]
            xs = zxbcdt[..., INNER:2 * INNER].reshape(B, L, HEADS, HEAD_DIM)
            Bm = zxbcdt[..., 2 * INNER:2 * INNER + STATE]
            Cm = zxbcdt[..., 2 * INNER + STATE:2 * INNER + 2 * STATE]
            dt = jax.nn.softplus(zxbcdt[..., 2 * INNER + 2 * STATE:] + dt_bias)
            A = -jnp.exp(A_log)
            decay = jnp.exp(dt * A)
            dtx = dt[..., None] * xs

            def step(h, inp):
                dec_t, dtx_t, B_t, C_t = inp
                h = dec_t[:, :, None, None] * h + dtx_t[..., None] * B_t[:, None, None, :]
                y = jnp.einsum('bhpn,bn->bhp', h, C_t)
                return (h, y)
            h0 = jnp.zeros((B, HEADS, HEAD_DIM, STATE), u.dtype)
            scan_in = (jnp.moveaxis(decay, 1, 0), jnp.moveaxis(dtx, 1, 0), jnp.moveaxis(Bm, 1, 0), jnp.moveaxis(Cm, 1, 0))
            _, ys = jax.lax.scan(step, h0, scan_in)
            y = jnp.moveaxis(ys, 0, 1)
            y = y + D_skip[None, None, :, None] * xs
            y = y.reshape(B, L, INNER) * jax.nn.silu(z)
            return y @ W_out + b_out
        normed = _layer_norm(input_tensor, ln_gamma, ln_beta)
        out = _mamba2(normed, W_in, b_in, A_log, D_skip, dt_bias, W_out, b_out)
        return input_tensor + out

    def _L0_ffn_ref(x, Wr, br, Wl1, bl1, Wl2, bl2, biases_N):
        import jax, jax.numpy as jnp
        import numpy as np
        D, H, N, K = (256, 512, 8, 2)
        B, S = (4, 512)
        Bb, Ss, Dd = x.shape
        scores_BSN = jnp.einsum('bsd,nd->bsn', x, Wr) + br
        w_BSN = jax.nn.softmax(scores_BSN, axis=-1)
        _, idx_BSK = jax.lax.top_k(scores_BSN + biases_N[None, None, :], K)
        val_BSK = jnp.take_along_axis(w_BSN, idx_BSK, axis=-1)
        val_BSK = val_BSK / jnp.sum(val_BSK, axis=-1, keepdims=True)
        M = Bb * Ss
        x_MD = x.reshape(M, Dd)
        idx_MK = idx_BSK.reshape(M, K)
        val_MK = val_BSK.reshape(M, K)
        h_NM2H = jnp.einsum('md,ndh->nmh', x_MD, Wl1) + bl1[:, None, :]
        a_NMH, b_NMH = (h_NM2H[..., :H], h_NM2H[..., H:])
        y_NMD = jnp.einsum('nmh,nhd->nmd', jax.nn.silu(a_NMH) * b_NMH, Wl2) + bl2[:, None, :]
        ew_MN = jnp.zeros((M, N), x.dtype)
        ew_MN = ew_MN.at[jnp.arange(M)[:, None], idx_MK].set(val_MK)
        y_MD = jnp.einsum('mn,nmd->md', ew_MN, y_NMD)
        return y_MD.reshape(Bb, Ss, Dd)
    x = L0_attn_input_tensor
    x = x + _L0_attn_ref(_layernorm(x, axis=-1), L0_attn_ln_gamma, L0_attn_ln_beta, L0_attn_W_in, L0_attn_b_in, L0_attn_A_log, L0_attn_D_skip, L0_attn_dt_bias, L0_attn_W_out, L0_attn_b_out)
    x = x + _L0_ffn_ref(_layernorm(x, axis=-1), L0_ffn_Wr, L0_ffn_br, L0_ffn_Wl1, L0_ffn_bl1, L0_ffn_Wl2, L0_ffn_bl2, L0_ffn_biases_N)
    return x

_drawn_inputs = setup_inputs


def setup_inputs(seed=0):
    import zlib

    import numpy as np

    out = dict(_drawn_inputs(seed))
    spreads = {'L0_attn_ln_gamma': (1.0, 0.6),
     'L0_attn_ln_beta': (0.0, 0.8),
     'L0_attn_b_in': (0.0, 0.4),
     'L0_attn_D_skip': (1.0, 0.6),
     'L0_attn_b_out': (0.0, 0.1),
     'L0_ffn_br': (0.0, 0.1),
     'L0_ffn_bl1': (0.0, 0.1),
     'L0_ffn_bl2': (0.0, 0.1),
     'L0_ffn_biases_N': (0.0, 0.1)}
    factors = {'L0_attn_A_log': 8.0, 'L0_attn_dt_bias': 8.0}
    for name, (base, spread) in spreads.items():
        noise = np.random.default_rng([zlib.crc32(name.encode()), seed]).standard_normal(out[name].shape)
        drawn = base * np.exp(spread * noise) if base else spread * noise
        out[name] = jnp.asarray(drawn.astype(out[name].dtype))
    for name, factor in factors.items():
        out[name] = (out[name] * factor).astype(out[name].dtype)
    return out
```

```python
from contextlib import ExitStack

import concourse.bass as bass
from concourse import mybir

ALU = mybir.AluOpType
ACT = mybir.ActivationFunctionType
F32 = mybir.dt.float32
BF16 = mybir.dt.bfloat16
I32 = mybir.dt.int32
U32 = mybir.dt.uint32
AX_X = mybir.AxisListType.X

P = 128
D = 256
DK = D // P
INNER = 512
FB = INNER // P
HEADS = 8
HD = INNER // HEADS
STATE = 64
PROJ = 2 * INNER + 2 * STATE + HEADS
BATCH, SEQ = 4, 1024
TOKENS = BATCH * SEQ
CHUNKS = TOKENS // P
CPS = SEQ // P
GC = 4
GT_ = GC * P
EPS = 1e-5
NE = 8
HID = 512
TOPK = 2
CHOICES = TOPK * CHUNKS
TILES = (TOPK * TOKENS + NE * (P - 1)) // P + 1
EB = 2 * HID + D
UNROLL = 4
AHEAD = 3
TPAD = TILES + AHEAD + 1
RING = 10
GROUP_PRODUCTS = ["u0", "u1", "bd", "bt", "ct", "cum", "z0", "z1", "z2", "z3"]


class Steps:

    def __init__(self, eng, sem, base=0, per_round=0, r=0):
        self.eng, self.sem, self.base, self.per_round, self.r, self.n = eng, sem, base, per_round, r, 0

    def did(self, ins):
        self.n += 1
        ins.then_inc(self.sem, 1)
        return self.n

    def wait(self, n=None):
        n = self.n if n is None else n
        self.eng.wait_ge(self.sem, self.per_round * self.r + (self.base + n) if self.per_round else self.base + n)

    def link(self, ins):
        self.wait(self.did(ins))


def wait_here(eng, scratch):
    eng.tensor_tensor(scratch[:, 0:1], scratch[:, 1:2], scratch[:, 1:2], ALU.add)


def build(nc, x, win, wout, gam, bet, bz, bbc, bx, bdt, alog, dskip, dtb, bout, wr, br, bn, w1, w2, eb, out):
    xf_dram = nc.dram_tensor("xf_dram", (TOKENS, D), F32, kind="Internal").ap()
    with ExitStack() as ctx:
        def sb(name, shape, dt=F32, c=ctx):
            return c.enter_context(nc.sbuf_tensor(name, shape, dt))

        consts = {
            "ident": sb("ident", [P, P]), "le": sb("le", [P, P]), "gt": sb("gt", [P, P]),
            "lt": sb("lt", [P, P]), "ones": sb("ones", [P, P]), "half": sb("half", [P, 8]),
        }
        scores = sb("scores", [P, CHUNKS, NE])
        w1s = sb("w1s", [P, NE, DK, 2 * HID])
        with ExitStack() as c:
            mamba(nc, c, consts, scores, w1s, xf_dram, x, win, wout, gam, bet, bz, bbc, bx, bdt, alog, dskip, dtb,
                  bout, wr, br, w1, out)
        w2s = sb("w2s", [P, NE, FB, D])
        b3 = sb("b3", [3, NE * EB], BF16)
        tab = {
            "gather": sb("gather", [P, TPAD], U32), "scatter": sb("scatter", [P, TILES], U32),
            "weight": sb("weight", [P, TILES]), "expert": sb("expert", [1, TPAD], I32),
        }
        with ExitStack() as c:
            route(nc, c, consts, scores, tab, w2s, b3, w2, eb, bn)
        with ExitStack() as c:
            experts(nc, c, consts, tab, w1s, w2s, b3, xf_dram, out)


def mamba(nc, ctx, consts, scores, w1s, xf_dram, x, win, wout, gam, bet, bz, bbc, bx, bdt, alog, dskip, dtb, bout,
          wr, br, w1, out):
    def sb(name, shape, dt=F32):
        return ctx.enter_context(nc.sbuf_tensor(name, shape, dt))

    def sem(name):
        return ctx.enter_context(nc.semaphore(name))

    def bank(name):
        return ctx.enter_context(nc.psum_tensor(name, [P, 512], F32))

    ident, le, gt, lt, ones, half = (consts[k] for k in ("ident", "le", "gt", "lt", "ones", "half"))
    wins = sb("wins", [P, DK, PROJ])
    wouts = sb("wouts", [P, FB, D])
    wrs = sb("wrs", [P, DK, NE])
    gams, bets = sb("gams", [P, DK]), sb("bets", [P, DK])
    bzs, bzh = sb("bzs", [P, FB]), sb("bzh", [P, FB])
    bbcs = sb("bbcs", [STATE, 2])
    bxs = sb("bxs", [P, INNER])
    bdts = sb("bdts", [2, STATE + HEADS])
    brs = sb("brs", [1, NE])
    alogs, nega, dsk = sb("alogs", [P, HEADS]), sb("nega", [P, HEADS]), sb("dsk", [P, HEADS])
    bouts = sb("bouts", [P, D])
    scratch, scratched = sb("scratch", [1, 2]), sem("scratched")
    xi, xr = sb("xi", [P, 2, GC, D]), sb("xr", [P, 2, GC, D])
    x1, u0 = sb("x1", [P, GC, D]), sb("u0", [P, GC, D])
    st = sb("st", [P, GC, 6])
    mv1, mv2 = sb("mv1", [P, GC, 2]), sb("mv2", [P, GC, 2])
    ve1, ve2, rs1, rs2 = (sb(n, [P, GC]) for n in ("ve1", "ve2", "rs1", "rs2"))
    ut = sb("ut", [P, 2, DK, GT_])
    zh, th = sb("zh", [P, 2, GT_]), sb("th", [P, 2, GT_])
    sil = sb("sil", [P, 2, FB, GT_])
    bt, ct = sb("bt", [STATE, 2, GT_]), sb("ct", [STATE, 2, GT_])
    btok = sb("btok", [P, 2, GC, STATE])
    spa, spe, spl, spr = (sb(n, [P, GC, HEADS]) for n in ("spa", "spe", "spl", "spr"))
    dt, aa = sb("dt", [P, 2, GC, HEADS]), sb("aa", [P, 2, GC, HEADS])
    ex = sb("ex", [P, 2, 3, GC, HEADS])
    xs, dtx, wx, dxs, y, gT = (sb(n, [P, 2, INNER]) for n in ("xs", "dtx", "wx", "dxs", "y", "gT"))
    segr, lm = sb("segr", [P, 2, HEADS, P]), sb("lm", [P, 2, HEADS, P])
    gm = sb("gm", [P, 2, P])
    hst = sb("hst", [STATE, 2, INNER])
    xp, xf, xft = sb("xp", [P, 2, D]), sb("xf", [P, 2, D]), sb("xft", [P, 2, DK, P])
    st3, mv3, ve3, rs3 = sb("st3", [P, 6]), sb("mv3", [P, 2]), sb("ve3", [P, 1]), sb("rs3", [P, 1])

    pa = [bank("pa0"), bank("pa1")]
    ps = [bank("ps0"), bank("ps1")]
    px, pg, py, po = bank("px"), bank("pg"), bank("py"), bank("po")

    c_const, c_load, c_w1, masks = sem("c_const"), sem("c_load"), sem("c_w1"), sem("masks")
    cleared, nega_ready = sem("cleared"), sem("nega_ready")
    x_in, xp_stored, xf_stored = ([sem(f"{n}{k}") for k in range(2)] for n in ("x_in", "xp_stored", "xf_stored"))
    stats1, rstd1, x1_ready, xr_ready, stats2, rstd2, u0_ready = (
        sem(n) for n in ("stats1", "rstd1", "x1_ready", "xr_ready", "stats2", "rstd2", "u0_ready"))
    a_full, a_free, sp_ready, a_ready, sil_ready = (
        sem(n) for n in ("a_full", "a_free", "sp_ready", "a_ready", "sil_ready"))
    segr_ready, seg_full, l_ready, g_full, gm_ready, m_ready = (
        sem(n) for n in ("segr_ready", "seg_full", "l_ready", "g_full", "gm_ready", "m_ready"))
    x_full, xs_ready, dtx_ready, wx_ready, dxs_ready = (
        sem(n) for n in ("x_full", "xs_ready", "dtx_ready", "wx_ready", "dxs_ready"))
    n_full, st_ready, yi_full, ye_full, y_ready, yt_full, gate_ready, o_full, xp_ready = (
        sem(n) for n in ("n_full", "st_ready", "yi_full", "ye_full", "y_ready", "yt_full", "gate_ready", "o_full",
                         "xp_ready"))
    stats3, rstd3, xf_ready, xft_full, xft_ready, sc_full, sc_ready = (
        sem(n) for n in ("stats3", "rstd3", "xf_ready", "xft_full", "xft_ready", "sc_full", "sc_ready"))
    dve_did, act_did, pool_did = sem("dve_did"), sem("act_did"), sem("pool_did")

    xg_dram = x.rearrange("(g c p) d -> g p c d", p=P, c=GC)
    zero_rows = out[TOKENS:TOKENS + P, :]
    NLOADS = 17

    def par(c):
        return c % 2

    def gpar(c):
        return (c // GC) % 2, c % GC

    def cnt(s, c):
        return s * CPS + (c + 1)

    def gcnt(s, g, per=1):
        return s * (2 * per) + per * (g + 1)

    block = ctx.enter_context(nc.Block())

    @block.sync
    def _(sp):
        def load_x(g_dram, half_):
            sp.dma_start(xi[:, half_], g_dram).then_inc(x_in[half_], 16)

        def row(a):
            return a.partition_broadcast(P)

        load_x(xg_dram[0], 0)
        sp.wait_ge(cleared, 1)
        for dst, src in ((gams[:], gam), (bets[:], bet), (wins[:, :, 0:PROJ], win), (bzs[:], bz), (bbcs[:], bbc),
                         (bdts[0:1, :], bdt), (bdts[1:2, STATE:], dtb), (bxs[:], row(bx[0])),
                         (alogs[:], row(alog[0])), (dsk[:], row(dskip[0])), (bouts[:], row(bout[0])),
                         (brs[:], br), (wrs[:], wr), (wouts[:], wout)):
            sp.dma_start(dst, src).then_inc(c_load, 16)
        load_x(xg_dram[1], 1)
        sp.wait_ge(cleared, 2)
        sp.dma_start(zero_rows, wx[:, 0, 0:D]).then_inc(c_const, 16)
        for e in range(NE):
            sp.dma_start(w1s[:, e], w1[:, e]).then_inc(c_w1, 16)

        def body(s, last):
            for c in range(CPS + 2):
                if c % GC == 0 and c < CPS and not last:
                    g = c // GC
                    sp.wait_ge(xr_ready, gcnt(s, g))
                    load_x(xg_dram[bass.ds(2 * s + (g + 2), 1)].rearrange("a p c d -> (a p) c d"), g)
                if 1 <= c <= CPS:
                    n = c - 1
                    sp.wait_ge(xp_ready, cnt(s, n))
                    sp.dma_start(out[bass.ds(s * SEQ + n * P, P), :], xp[:, par(n)]) \
                        .then_inc(xp_stored[par(n)], 16)
                    sp.wait_ge(xf_ready, cnt(s, n))
                    sp.dma_start(xf_dram[bass.ds(s * SEQ + n * P, P), :], xf[:, par(n)]) \
                        .then_inc(xf_stored[par(n)], 16)

        with sp.Fori(0, BATCH - 1) as s:
            body(s, False)
        body(BATCH - 1, True)
        for k in range(2):
            sp.wait_ge(xp_stored[k], 16 * (CHUNKS // 2 + 1))
            sp.wait_ge(xf_stored[k], 16 * (CHUNKS // 2 + 1))
        sp.wait_ge(c_const, 16)
        sp.wait_ge(c_w1, 16 * NE)

    @block.gpsimd
    def _(pool):
        pool.memset(bdts[:], 0.0).then_inc(cleared, 1)
        steps0 = Steps(pool, masks)
        pool.memset(wx[:, 0, 0:D], 0.0).then_inc(cleared, 1)
        for t, v in ((ident, 0.0), (le, 1.0), (gt, 1.0), (lt, 1.0), (ones, 1.0), (half, -0.5)):
            steps0.did(pool.memset(t[:], v))
        steps0.wait()
        for t, op, base, mult, step, fill in ((ident, ALU.not_equal, 0, 1, -1, 1.0), (le, ALU.is_ge, 0, -1, 1, 0.0),
                                              (gt, ALU.is_gt, 0, 1, -1, 0.0), (lt, ALU.is_gt, 0, -1, 1, 0.0)):
            steps0.did(pool.affine_select(out=t[:], in_=t[:], compare_op=op, fill=fill, base=base,
                                          pattern=[[step, P]], channel_multiplier=mult))
        steps0.wait()

        def rstd(dst, src, n, ready, value, done):
            pool.wait_ge(ready, value)
            pool.tensor_tensor(dst, src, half[:, 0:n], ALU.pow).then_inc(done, 1)

        def residual(s, g, steps):
            h = g % 2
            pool.wait_ge(x1_ready, gcnt(s, g))
            steps.link(pool.tensor_tensor(xr[:, h], xi[:, h], x1[:], ALU.add))
            pool.tensor_tensor(xr[:, h], xr[:, h], bouts[:].unsqueeze(1).to_broadcast([P, GC, D]), ALU.add) \
                .then_inc(xr_ready, 1)

        def segment(s, n):
            h, k = gpar(n)
            pool.wait_ge(a_ready, gcnt(s, n // GC))
            if n:
                pool.wait_ge(seg_full, cnt(s, n - 1))
            pool.tensor_tensor(segr[:, par(n)], le[:].unsqueeze(1).to_broadcast([P, HEADS, P]),
                               aa[:, h, k].unsqueeze(2).to_broadcast([P, HEADS, P]), ALU.mult) \
                .then_inc(segr_ready, 1)

        def heads(t):
            return t.rearrange("p (h d) -> p h d", h=HEADS)

        def per_head(t):
            return t.unsqueeze(2).to_broadcast([P, HEADS, HD])

        def scaled(s, n):
            h, k = gpar(n)
            pool.wait_ge(xs_ready, cnt(s, n))
            pool.tensor_tensor(heads(dtx[:, par(n)]), heads(xs[:, par(n)]), per_head(dt[:, h, k]), ALU.mult) \
                .then_inc(dtx_ready, 1)
            pool.tensor_tensor(heads(dxs[:, par(n)]), heads(xs[:, par(n)]), per_head(dsk[:]), ALU.mult) \
                .then_inc(dxs_ready, 1)
            pool.wait_ge(a_free, gcnt(s, n // GC - 1, RING) + (GROUP_PRODUCTS.index("cum") + 3))
            pool.wait_ge(dtx_ready, cnt(s, n))
            pool.tensor_tensor(heads(wx[:, par(n)]), heads(dtx[:, par(n)]), per_head(ex[:, h, 1, k]), ALU.mult) \
                .then_inc(wx_ready, 1)

        POOL_LINKS = 2
        steps = Steps(pool, pool_did)
        rstd(rs1[:], ve1[:], GC, stats1, 1, rstd1)
        pool.wait_ge(c_load, 16 * 14)
        residual(0, 0, steps)
        rstd(rs2[:], ve2[:], GC, stats2, 1, rstd2)
        segment(0, 0)
        pool.wait_ge(c_const, 16)
        scaled(0, 0)

        def body(s, nxt):
            steps = Steps(pool, pool_did, base=1, per_round=POOL_LINKS, r=s)
            for c in range(CPS + 1):
                ahead = c < CPS - 1 or (nxt and c == CPS - 1)
                g = c // GC + 1
                prepares = c < CPS and (g == 1 or nxt)
                if prepares and c % GC == 0:
                    rstd(rs1[:], ve1[:], GC, stats1, gcnt(s, g), rstd1)
                if ahead:
                    segment(s, c + 1)
                if c:
                    rstd(rs3[:], ve3[:], 1, stats3, cnt(s, c - 1), rstd3)
                if prepares and c % GC == 0:
                    rstd(rs2[:], ve2[:], GC, stats2, gcnt(s, g), rstd2)
                if ahead:
                    scaled(s, c + 1)
                if prepares and c % GC == 0:
                    residual(s, g, steps)

        with pool.Fori(0, BATCH - 1) as s:
            body(s, True)
        body(BATCH - 1, False)

    @block.scalar
    def _(act):
        act.sem_inc(a_free, 2)
        act.sem_inc(xft_ready, 1)
        act.sem_inc(sc_ready, 1)
        for k in range(2):
            act.sem_inc(xp_stored[k], 16)
            act.sem_inc(xf_stored[k], 16)
        act.wait_ge(c_load, 16 * 14)
        act.mul(bzh[:], bzs[:], 0.5).then_inc(act_did, 1)
        act.activation(nega[:], alogs[:], ACT.Exp).then_inc(nega_ready, 1)
        act.wait_ge(act_did, 1)

        def group(s, g, parts):
            h = g % 2
            for k, what in enumerate(GROUP_PRODUCTS):
                if what not in parts:
                    continue
                src = pa[k % 2]
                act.wait_ge(a_full, gcnt(s, g - 1, RING) + (k + 1))
                if what in ("u0", "u1"):
                    d = int(what[1])
                    act.activation(ut[:, h, d], src[:], ACT.Identity, bias=bets[:, d:d + 1],
                                   scale=gams[:, d:d + 1]).then_inc(a_free, 1)
                elif what == "bd":
                    v = src[:, 0:GC * (STATE + HEADS)].rearrange("p (c n) -> p c n", c=GC)
                    act.activation(btok[:, h], v[:, :, 0:STATE], ACT.Identity)
                    act.activation(spa[:], v[:, :, STATE:], ACT.Abs).then_inc(act_did, 1)
                    act.activation(spr[:], v[:, :, STATE:], ACT.Relu).then_inc(a_free, 1)
                    act.wait_ge(act_did, gcnt(s, g - 1, 2) + 2)
                    act.activation(spe[:], spa[:], ACT.Exp, scale=-1.0).then_inc(act_did, 1)
                    act.wait_ge(act_did, gcnt(s, g - 1, 2) + 3)
                    act.activation(spl[:], spe[:], ACT.Ln, bias=1.0).then_inc(sp_ready, 1)
                elif what in ("bt", "ct"):
                    j = int(what == "ct")
                    act.activation((bt, ct)[j][:, h], src[0:STATE, :], ACT.Identity, bias=bbcs[:, j:j + 1]) \
                        .then_inc(a_free, 1)
                elif what == "cum":
                    act.activation(ex[:, h].rearrange("p a c n -> p (a c n)"), src[:, 0:3 * GC * HEADS], ACT.Exp) \
                        .then_inc(a_free, 1)
                else:
                    f = int(what[1])
                    act.wait_ge(sil_ready, gcnt(s, g - 1, FB) + (f + 1))
                    act.activation(zh[:, f % 2], src[:], ACT.Identity, bias=bzh[:, f:f + 1], scale=0.5)
                    act.activation(th[:, f % 2], src[:], ACT.Tanh, bias=bzh[:, f:f + 1], scale=0.5) \
                        .then_inc(a_free, 1)

        def decay(s, n):
            act.wait_ge(seg_full, cnt(s, n))
            act.activation(lm[:, par(n), 0:4], ps[0][:].rearrange("p (h i) -> p h i", h=4), ACT.Exp)
            act.activation(lm[:, par(n), 4:8], ps[1][:].rearrange("p (h i) -> p h i", h=4), ACT.Exp) \
                .then_inc(l_ready, 1)

        def router(s, n):
            act.wait_ge(xft_full, cnt(s, n))
            act.activation(xft[:, par(n)].rearrange("p d t -> p (d t)"), ps[0][:, 0:D], ACT.Identity) \
                .then_inc(xft_ready, 1)
            act.wait_ge(sc_full, cnt(s, n))
            act.activation(scores[:, bass.ds(s * CPS + n, 1)], ps[1][:, 0:NE].unsqueeze(1), ACT.Identity) \
                .then_inc(sc_ready, 1)

        group(0, 0, GROUP_PRODUCTS)
        decay(0, 0)

        def body(s, nxt):
            for c in range(CPS):
                if c < CPS - 1 or nxt:
                    decay(s, c + 1)
                if c >= 2:
                    router(s, c - 2)
                g, k = c // GC + 1, c % GC
                if g == 1 or nxt:
                    group(s, g, STAGES[k])
            router(s, CPS - 2)
            router(s, CPS - 1)

        with act.Fori(0, BATCH - 1) as s:
            body(s, True)
        body(BATCH - 1, False)

    @block.vector
    def _(dve):
        dve.memset(scratch[:], 0.0).then_inc(scratched, 1)
        dve.wait_ge(scratched, 1)
        dve.sem_inc(sil_ready, 2)
        dve.wait_ge(nega_ready, 1)
        dve.wait_ge(masks, 10)

        def stats(src, ve, mv, steps, done):
            n = [steps.did(dve.bn_stats(st[:, k], src[:, k])) for k in range(GC)]
            steps.wait(n[-1])
            wait_here(dve, scratch)
            for k in range(GC):
                m = steps.did(dve.bn_aggr(mv[:, k], st[:, k]))
            steps.wait(m)
            dve.tensor_scalar(ve[:], mv[:, :, 1], EPS, None, ALU.add).then_inc(done, 1)

        def normalise(dst, src, mv, rs, done):
            for k in range(GC):
                ins = dve.tensor_scalar(dst[:, k], src[:, k], mv[:, k, 0:1], rs[:, k:k + 1], ALU.subtract, ALU.mult)
            ins.then_inc(done, 1)

        def first_stats(s, g, steps):
            dve.wait_ge(x_in[g % 2], 16 * s + 16 * (g // 2 + 1))
            stats(xi[:, g % 2], ve1, mv1, steps, stats1)

        def first_norm(s, g, steps):
            dve.wait_ge(rstd1, gcnt(s, g))
            if not (isinstance(s, int) and 2 * s + g == 0):
                dve.wait_ge(xr_ready, gcnt(s, g - 1))
            normalise(x1, xi[:, g % 2], mv1, rs1, x1_ready)
            dve.wait_ge(x1_ready, gcnt(s, g))
            stats(x1, ve2, mv2, steps, stats2)

        def second_norm(s, g):
            dve.wait_ge(rstd2, gcnt(s, g))
            if not (isinstance(s, int) and 2 * s + g == 0):
                dve.wait_ge(a_full, gcnt(s, g - 2, RING) + 2)
            normalise(u0, x1, mv2, rs2, u0_ready)

        def steps_dt(s, g, steps):
            h = g % 2
            dve.wait_ge(sp_ready, gcnt(s, g))
            steps.link(dve.tensor_tensor(dt[:, h], spr[:], spl[:], ALU.add))
            dve.scalar_tensor_tensor(aa[:, h], dt[:, h], -1.0, nega[:].unsqueeze(1).to_broadcast([P, GC, HEADS]),
                                     ALU.mult, ALU.mult).then_inc(a_ready, 1)

        def silu(s, g):
            for f in range(FB):
                dve.wait_ge(a_free, gcnt(s, g - 1, RING) + (GROUP_PRODUCTS.index(f"z{f}") + 3))
                dve.scalar_tensor_tensor(sil[:, g % 2, f], th[:, f % 2], 1.0, zh[:, f % 2], ALU.add, ALU.mult) \
                    .then_inc(sil_ready, 1)

        def inner_x(s, n):
            dve.wait_ge(x_full, cnt(s, n))
            dve.tensor_tensor(xs[:, par(n)], px[:], bxs[:], ALU.add).then_inc(xs_ready, 1)

        def mixing(s, n):
            dve.wait_ge(g_full, cnt(s, n))
            dve.tensor_tensor(gm[:, par(n)], pg[:, 0:P], le[:], ALU.mult).then_inc(gm_ready, 1)
            dve.wait_ge(gm_ready, cnt(s, n))
            dve.wait_ge(l_ready, cnt(s, n))
            dve.tensor_tensor(lm[:, par(n)], lm[:, par(n)],
                              gm[:, par(n)].unsqueeze(1).to_broadcast([P, HEADS, P]), ALU.mult).then_inc(m_ready, 1)

        def state(s, n, steps):
            h, k = gpar(n)
            dve.wait_ge(n_full, s * (CPS - 1) + (n + 1))
            if n == 0:
                dve.tensor_copy(hst[:, 1], pg[0:STATE, :]).then_inc(st_ready, 1)
                return
            new = hst[:, par(n + 1)]
            dve.wait_ge(st_ready, s * (CPS - 1) + n)
            steps.link(dve.tensor_tensor(new.rearrange("p (h d) -> p h d", h=HEADS),
                                         hst[:, par(n)].rearrange("p (h d) -> p h d", h=HEADS),
                                         ex[0:STATE, h, 2, k].unsqueeze(2).to_broadcast([STATE, HEADS, HD]), ALU.mult))
            dve.tensor_tensor(new, new, pg[0:STATE, :], ALU.add).then_inc(st_ready, 1)

        def gate(s, n):
            h, k = gpar(n)
            dve.wait_ge(yt_full, cnt(s, n))
            dve.wait_ge(sil_ready, gcnt(s, n // GC, FB) + 2)
            dve.tensor_tensor(gT[:, par(n)].rearrange("p (f t) -> p f t", f=FB),
                              py[:].rearrange("p (f t) -> p f t", f=FB), sil[:, h, :, k * P:(k + 1) * P], ALU.mult) \
                .then_inc(gate_ready, 1)

        def residual(s, n, steps):
            h, k = gpar(n)
            dve.wait_ge(o_full, cnt(s, n))
            dve.wait_ge(xp_stored[par(n)], s * (8 * CPS) + 16 * (n // 2 + 1))
            dve.tensor_tensor(xp[:, par(n)], po[:, 0:D], xr[:, h, k], ALU.add).then_inc(xp_ready, 1)
            dve.wait_ge(xp_ready, cnt(s, n))
            a = steps.did(dve.bn_stats(st3[:], xp[:, par(n)]))
            steps.wait(a)
            wait_here(dve, scratch)
            steps.link(dve.bn_aggr(mv3[:], st3[:]))
            dve.tensor_scalar(ve3[:], mv3[:, 1:2], EPS, None, ALU.add).then_inc(stats3, 1)

        def last_norm(s, n):
            dve.wait_ge(rstd3, cnt(s, n))
            dve.wait_ge(xf_stored[par(n)], s * (8 * CPS) + 16 * (n // 2 + 1))
            dve.tensor_scalar(xf[:, par(n)], xp[:, par(n)], mv3[:, 0:1], rs3[:], ALU.subtract, ALU.mult) \
                .then_inc(xf_ready, 1)

        def output(s, n, steps):
            h, k = gpar(n)
            dve.wait_ge(yi_full, cnt(s, n))
            dve.wait_ge(dxs_ready, cnt(s, n))
            yy = y[:, par(n)]
            if n:
                dve.wait_ge(ye_full, s * (CPS - 1) + n)
                steps.link(dve.tensor_tensor(yy.rearrange("p (h d) -> p h d", h=HEADS),
                                             po[:].rearrange("p (h d) -> p h d", h=HEADS),
                                             ex[:, h, 0, k].unsqueeze(2).to_broadcast([P, HEADS, HD]), ALU.mult))
                steps.link(dve.tensor_tensor(yy, py[:], yy, ALU.add))
                dve.tensor_tensor(yy, yy, dxs[:, par(n)], ALU.add).then_inc(y_ready, 1)
            else:
                dve.tensor_tensor(yy, py[:], dxs[:, par(n)], ALU.add).then_inc(y_ready, 1)

        steps = Steps(dve, dve_did)
        first_stats(0, 0, steps)
        first_norm(0, 0, steps)
        second_norm(0, 0)
        steps_dt(0, 0, steps)
        silu(0, 0)
        inner_x(0, 0)
        mixing(0, 0)
        base = steps.n

        def body(s, nxt, per_round):
            steps = Steps(dve, dve_did, base=base, per_round=per_round, r=s)
            for c in range(CPS):
                ahead = c < CPS - 1 or nxt
                g, k = c // GC + 1, c % GC
                prepares = g == 1 or nxt
                if c < CPS - 1:
                    state(s, c, steps)
                if c:
                    gate(s, c - 1)
                if prepares and k == 1:
                    second_norm(s, g)
                if ahead:
                    inner_x(s, c + 1)
                if prepares and k == 0:
                    first_stats(s, g, steps)
                if prepares and k == 2:
                    steps_dt(s, g, steps)
                if c:
                    residual(s, c - 1, steps)
                output(s, c, steps)
                if c:
                    last_norm(s, c - 1)
                if prepares and k == 0:
                    first_norm(s, g, steps)
                if ahead:
                    mixing(s, c + 1)
                if prepares and k == 3:
                    silu(s, g)
            gate(s, CPS - 1)
            residual(s, CPS - 1, steps)
            last_norm(s, CPS - 1)
            return steps.n

        DVE_STEPS = 2 * (4 * GC + 1) + (CPS - 2) + 2 * CPS + 2 * (CPS - 1)
        with dve.Fori(0, BATCH - 1) as s:
            assert body(s, True, DVE_STEPS) == DVE_STEPS
        body(BATCH - 1, False, DVE_STEPS)

    @block.tensor
    def _(pe):
        pe.wait_ge(masks, 10)
        pe.wait_ge(c_load, 16 * 14)

        def group(s, g, parts):
            h = g % 2
            for k, what in enumerate(GROUP_PRODUCTS):
                if what not in parts:
                    continue
                dst = pa[k % 2]
                pe.wait_ge(a_free, gcnt(s, g - 1, RING) + (k + 1))
                if what in ("u0", "u1"):
                    d = int(what[1])
                    pe.wait_ge(u0_ready, gcnt(s, g))
                    for c in range(GC):
                        ins = pe.transpose(dst[:, c * P:(c + 1) * P], u0[:, c, d * P:(d + 1) * P], ident[:])
                elif what == "bd":
                    pe.wait_ge(a_free, gcnt(s, g - 1, RING) + 4)
                    n0 = STATE + HEADS
                    for c in range(GC):
                        o = c * n0
                        for d in range(DK):
                            lhs = ut[:, h, d, c * P:(c + 1) * P]
                            pe.matmul(dst[:, o:o + STATE], lhs, wins[:, d, 2 * INNER:2 * INNER + STATE],
                                      start=d == 0, stop=False, skip_group_check=True)
                        for d in range(DK):
                            lhs = ut[:, h, d, c * P:(c + 1) * P]
                            pe.matmul(dst[:, o + STATE:o + n0], lhs, wins[:, d, PROJ - HEADS:PROJ],
                                      start=False, stop=False, skip_group_check=True)
                        ins = pe.matmul(dst[:, o:o + n0], ones[0:2, :], bdts[:], start=False, stop=True,
                                        skip_group_check=True)
                elif what in ("bt", "ct"):
                    j = 2 * INNER + STATE * int(what == "ct")
                    for d in range(DK):
                        ins = pe.matmul(dst[0:STATE, :], wins[:, d, j:j + STATE], ut[:, h, d], start=d == 0,
                                        stop=d == DK - 1)
                elif what == "cum":
                    pe.wait_ge(a_ready, gcnt(s, g))
                    n = GC * HEADS
                    for j, m in enumerate((le, gt, ones)):
                        ins = pe.matmul(dst[:, j * n:(j + 1) * n], m[:], aa[:, h].rearrange("p c n -> p (c n)"),
                                        start=True, stop=True)
                else:
                    f = int(what[1])
                    for d in range(DK):
                        ins = pe.matmul(dst[:], wins[:, d, f * P:(f + 1) * P], ut[:, h, d], start=d == 0,
                                        stop=d == DK - 1)
                ins.then_inc(a_full, 1)

        def inner_x(s, n):
            h, k = gpar(n)
            if n:
                pe.wait_ge(xs_ready, cnt(s, n - 1))
            for d in range(DK):
                ins = pe.matmul(px[:], ut[:, h, d, k * P:(k + 1) * P], wins[:, d, INNER:2 * INNER], start=d == 0,
                                stop=d == DK - 1)
            ins.then_inc(x_full, 1)

        def scores_cb(s, n):
            h, k = gpar(n)
            pe.wait_ge(a_free, gcnt(s, n // GC - 1, RING) + (GROUP_PRODUCTS.index("ct") + 3))
            if n == CPS:
                pe.wait_ge(gm_ready, cnt(s, n - 1))
            elif n:
                pe.wait_ge(st_ready, s * (CPS - 1) + n)
            pe.matmul(pg[:, 0:P], bt[:, h, k * P:(k + 1) * P], ct[:, h, k * P:(k + 1) * P], start=True, stop=True) \
                .then_inc(g_full, 1)
            pe.wait_ge(segr_ready, cnt(s, n))
            if n:
                pe.wait_ge(xft_ready, s * CPS + (max(n - 3, 0) + 1))
                pe.wait_ge(sc_ready, s * CPS + (max(n - 3, 0) + 1))
            for j in range(2):
                ins = pe.matmul(ps[j][:], gt[:], segr[:, par(n), 4 * j:4 * j + 4].rearrange("p h i -> p (h i)"),
                                start=True, stop=True)
            ins.then_inc(seg_full, 1)

        def new_state(s, n):
            h, k = gpar(n)
            pe.wait_ge(wx_ready, cnt(s, n))
            pe.wait_ge(gm_ready, cnt(s, n))
            pe.matmul(pg[0:STATE, :], btok[:, h, k], wx[:, par(n)], start=True, stop=True).then_inc(n_full, 1)

        def transposed(s, n):
            pe.wait_ge(y_ready, cnt(s, n))
            for f in range(FB):
                ins = pe.transpose(py[:, f * P:(f + 1) * P], y[:, par(n), f * P:(f + 1) * P], ident[:])
            ins.then_inc(yt_full, 1)

        def out_proj(s, n):
            pe.wait_ge(gate_ready, cnt(s, n))
            for f in range(FB):
                ins = pe.matmul(po[:, 0:D], gT[:, par(n), f * P:(f + 1) * P], wouts[:, f], start=f == 0,
                                stop=f == FB - 1)
            ins.then_inc(o_full, 1)

        def within(s, n):
            pe.wait_ge(m_ready, cnt(s, n))
            pe.wait_ge(dtx_ready, cnt(s, n))
            for hh in range(HEADS):
                ins = pe.matmul(py[:, hh * HD:(hh + 1) * HD], lm[:, par(n), hh], dtx[:, par(n), hh * HD:(hh + 1) * HD],
                                start=True, stop=True)
            ins.then_inc(yi_full, 1)

        def across(s, n):
            h, k = gpar(n)
            pe.wait_ge(st_ready, s * (CPS - 1) + n)
            pe.wait_ge(xp_ready, cnt(s, n - 1))
            pe.matmul(po[:], ct[:, h, k * P:(k + 1) * P], hst[:, par(n)], start=True, stop=True).then_inc(ye_full, 1)

        def router(s, n):
            pe.wait_ge(xf_ready, cnt(s, n))
            pe.wait_ge(l_ready, cnt(s, min(n + 3, CPS - 1)))
            pe.wait_ge(sc_ready, s * CPS + (n + 1))
            for d in range(DK):
                ins = pe.transpose(ps[0][:, d * P:(d + 1) * P], xf[:, par(n), d * P:(d + 1) * P], ident[:])
            ins.then_inc(xft_full, 1)
            pe.wait_ge(xft_ready, s * CPS + (n + 2))
            for d in range(DK):
                pe.matmul(ps[1][:, 0:NE], xft[:, par(n), d], wrs[:, d], start=d == 0, stop=False)
            pe.matmul(ps[1][:, 0:NE], ones[0:1, :], brs[:], start=False, stop=True).then_inc(sc_full, 1)

        group(0, 0, GROUP_PRODUCTS)
        inner_x(0, 0)
        scores_cb(0, 0)

        def body(s, nxt):
            for c in range(CPS):
                ahead = c < CPS - 1 or nxt
                if c < CPS - 1:
                    new_state(s, c)
                if c:
                    transposed(s, c - 1)
                if ahead:
                    inner_x(s, c + 1)
                    scores_cb(s, c + 1)
                if c:
                    out_proj(s, c - 1)
                within(s, c)
                if c:
                    across(s, c)
                if c >= 2:
                    if c == CPS - 1 and nxt:
                        pe.wait_ge(l_ready, cnt(s, CPS))
                    router(s, c - 2)
                g, k = c // GC + 1, c % GC
                if g == 1 or nxt:
                    group(s, g, STAGES[k])
            transposed(s, CPS - 1)
            out_proj(s, CPS - 1)
            router(s, CPS - 2)
            router(s, CPS - 1)

        with pe.Fori(0, BATCH - 1) as s:
            body(s, True)
        body(BATCH - 1, False)


STAGES = [[], ["u0", "u1", "bd"], ["bt", "ct", "cum"], ["z0", "z1", "z2", "z3"]]


def route(nc, ctx, consts, scores, tab, w2s, b3, w2, eb, bn):
    def sb(name, shape, dt=F32):
        return ctx.enter_context(nc.sbuf_tensor(name, shape, dt))

    def sem(name):
        return ctx.enter_context(nc.semaphore(name))

    lt, ones = consts["lt"], consts["ones"]
    te = [P, CHUNKS, NE]
    bns = sb("bns", [P, NE])
    ebs, eb_rest, eb3 = sb("ebs", [P, NE * EB // P]), sb("eb_rest", [P, NE * EB // P]), \
        sb("eb3", [P, 3, NE * EB // P], BF16)
    top, wts, biased, cand = sb("top", [P, CHUNKS]), sb("wts", te), sb("biased", te), sb("cand", te)
    pick = sb("pick", [P, TOPK, CHUNKS, NE])
    order = sb("order", [P, NE])
    val = sb("val", [P, TOPK, CHUNKS])
    total = sb("total", [P, CHUNKS])
    chosen = sb("chosen", te)
    before = [sb("before0", te), sb("before1", te)]
    many, iota_k = sb("many", [P, NE, CHUNKS]), sb("iota_k", [P, CHUNKS])
    tiles = sb("tiles", [P, NE])
    upto = [sb("upto0", [P, NE]), sb("upto1", [P, NE])]
    base = sb("base", [P, NE])
    slot, slots = sb("slot", te), sb("slots", [P, TOPK, CHUNKS])
    slot_i, tile_i, row_i = (sb(n, [P, CHOICES], I32) for n in ("slot_i", "tile_i", "row_i"))
    tile_f, row_f = sb("tile_f", [P, CHOICES]), sb("row_f", [P, CHOICES])
    iota_r, iota_t = sb("iota_r", [P, P]), sb("iota_t", [P, TILES])
    token1 = sb("token1", [P, TOPK, CHUNKS])
    spare = sb("spare", [P, 1])
    hot_t = sb("hot_t", [P, CHOICES, 2, TILES])
    RINGS = 4
    hot_r = sb("hot_r", [P, RINGS, P])
    named = sb("named", [P, 2, TILES])
    empty, dest = sb("empty", [P, TILES]), sb("dest", [P, TILES])
    ex_t, ex_f = sb("ex_t", [1, TILES, NE]), sb("ex_f", [1, TILES])
    pr = ctx.enter_context(nc.psum_tensor("pr", [P, 512], F32))
    pt = ctx.enter_context(nc.psum_tensor("pt", [P, 512], F32))

    loaded, w2_in, b_in, b_out, iotas, e_in, e_out, chosen_ready, counted = (
        sem(n) for n in ("r_loaded", "w2_in", "b_in", "b_out", "iotas", "e_in", "e_out", "chosen_ready", "counted"))
    onehot, tabled, did, w_ready, id_ready, tf_ready = (
        sem(n) for n in ("onehot", "tabled", "route_did", "w_ready", "id_ready", "tf_ready"))
    block = ctx.enter_context(nc.Block())

    @block.sync
    def _(sp):
        sp.dma_start(bns[:], bn[0].partition_broadcast(P)).then_inc(loaded, 16)
        sp.dma_start(ebs[:], eb).then_inc(b_in, 16)
        sp.wait_ge(b_out, 1)
        for k in range(3):
            sp.dma_start(b3[k:k + 1, :], eb3[:, k]).then_inc(loaded, 16)
        for e in range(NE):
            sp.dma_start(w2s[:, e], w2[:, e]).then_inc(w2_in, 16)
        sp.wait_ge(loaded, 16 * 4)
        sp.wait_ge(w2_in, 16 * NE)

    @block.gpsimd
    def _(pool):
        for t, pattern, start, mult in ((order[:], [[-1, NE]], NE, 0), (iota_k[:], [[P, CHUNKS]], 0, 0),
                                        (iota_r[:], [[1, P]], 0, 0), (iota_t[:], [[1, TILES]], 0, 0),
                                        (token1[:], [[0, TOPK], [P, CHUNKS]], 1, 1), (spare[:], [[0, 1]], TOKENS + 1, 1)):
            pool.iota(t, pattern=pattern, base=start, channel_multiplier=mult,
                      allow_small_or_imprecise_dtypes=True).then_inc(iotas, 1)
        pool.memset(tab["gather"][:, TILES:], 0)
        pool.memset(tab["expert"][:, TILES:], 0).then_inc(iotas, 1)
        pool.wait_ge(iotas, 7)
        pool.wait_ge(tf_ready, 1)
        pool.tensor_tensor(hot_t[:, :, 0], hot_t[:, :, 0],
                           token1[:].rearrange("p k c -> p (k c)").unsqueeze(2).to_broadcast([P, CHOICES, TILES]),
                           ALU.mult).then_inc(id_ready, 1)

    @block.scalar
    def _(act):
        act.wait_ge(e_in, 1)
        act.activation(wts[:], wts[:], ACT.Exp).then_inc(e_out, 1)

    @block.vector
    def _(dve):
        steps = Steps(dve, did)
        do = steps.link

        def per_chunk(t):
            return t.unsqueeze(2).to_broadcast(te)

        def per_expert(t):
            return t[:].unsqueeze(1).to_broadcast(te)

        dve.wait_ge(b_in, 16)
        do(dve.tensor_copy(eb3[:, 0], ebs[:]))
        do(dve.tensor_tensor(eb_rest[:], ebs[:], eb3[:, 0], ALU.subtract))
        do(dve.tensor_copy(eb3[:, 1], eb_rest[:]))
        do(dve.tensor_tensor(eb_rest[:], eb_rest[:], eb3[:, 1], ALU.subtract))
        dve.tensor_copy(eb3[:, 2], eb_rest[:]).then_inc(b_out, 1)
        do(dve.tensor_reduce(top[:], scores[:], AX_X, ALU.max))
        dve.tensor_tensor(wts[:], scores[:], per_chunk(top[:]), ALU.subtract).then_inc(e_in, 1)
        dve.wait_ge(loaded, 16)
        do(dve.tensor_tensor(biased[:], scores[:], per_expert(bns), ALU.add))
        dve.wait_ge(iotas, 7)
        for k in range(TOPK):
            do(dve.tensor_reduce(top[:], biased[:], AX_X, ALU.max))
            do(dve.tensor_tensor(cand[:], biased[:], per_chunk(top[:]), ALU.is_equal))
            do(dve.tensor_tensor(cand[:], cand[:], per_expert(order), ALU.mult))
            do(dve.tensor_reduce(top[:], cand[:], AX_X, ALU.max))
            do(dve.tensor_tensor(pick[:, k], cand[:], per_chunk(top[:]), ALU.is_equal))
            if k == 0:
                do(dve.scalar_tensor_tensor(biased[:], pick[:, 0], -3e38, biased[:], ALU.mult, ALU.add))
        dve.tensor_tensor(chosen[:], pick[:, 0], pick[:, 1], ALU.add).then_inc(chosen_ready, 1)
        dve.wait_ge(e_out, 1)
        do(dve.tensor_reduce(total[:], wts[:], AX_X, ALU.add))
        do(dve.reciprocal(total[:], total[:]))
        do(dve.tensor_tensor(wts[:], wts[:], per_chunk(total[:]), ALU.mult))
        for k in range(TOPK):
            do(dve.tensor_tensor(cand[:], wts[:], pick[:, k], ALU.mult))
            do(dve.tensor_reduce(val[:, k], cand[:], AX_X, ALU.add))
        do(dve.tensor_tensor(total[:], val[:, 0], val[:, 1], ALU.add))
        do(dve.reciprocal(total[:], total[:]))
        do(dve.tensor_tensor(val[:], val[:], total[:].unsqueeze(1).to_broadcast([P, TOPK, CHUNKS]), ALU.mult))
        dve.wait_ge(counted, 1)
        do(dve.tensor_copy(before[0][:], pt[:, 0:CHUNKS * NE].rearrange("p (c e) -> p c e", e=NE)))
        src, far = 0, 1
        while far < CHUNKS:
            a, b = before[src], before[1 - src]
            steps.did(dve.tensor_copy(b[:, 0:far], a[:, 0:far]))
            do(dve.tensor_tensor(b[:, far:], a[:, far:], a[:, 0:CHUNKS - far], ALU.add))
            src, far = 1 - src, 2 * far
        upto_chunk = before[src]
        do(dve.tensor_tensor(many[:], upto_chunk[:, CHUNKS - 1].unsqueeze(2).to_broadcast([P, NE, CHUNKS]),
                             iota_k[:].unsqueeze(1).to_broadcast([P, NE, CHUNKS]), ALU.is_gt))
        do(dve.tensor_reduce(tiles[:], many[:], AX_X, ALU.add))
        do(dve.tensor_copy(upto[0][:], tiles[:]))
        s2, far = 0, 1
        while far < NE:
            a, b = upto[s2], upto[1 - s2]
            steps.did(dve.tensor_copy(b[:, 0:far], a[:, 0:far]))
            do(dve.tensor_tensor(b[:, far:], a[:, far:], a[:, 0:NE - far], ALU.add))
            s2, far = 1 - s2, 2 * far
        last_tile = upto[s2]
        do(dve.tensor_tensor(base[:], last_tile[:], tiles[:], ALU.subtract))
        do(dve.tensor_tensor(slot[:], upto_chunk[:], pt[:, 0:CHUNKS * NE].rearrange("p (c e) -> p c e", e=NE),
                             ALU.subtract))
        do(dve.tensor_tensor(slot[:], slot[:], pr[:, 0:CHUNKS * NE].rearrange("p (c e) -> p c e", e=NE), ALU.add))
        do(dve.scalar_tensor_tensor(slot[:], per_expert(base), float(P), slot[:], ALU.mult, ALU.add))
        for k in range(TOPK):
            do(dve.tensor_tensor(cand[:], slot[:], pick[:, k], ALU.mult))
            do(dve.tensor_reduce(slots[:, k], cand[:], AX_X, ALU.add))
        flat = slots[:].rearrange("p k c -> p (k c)")
        do(dve.tensor_copy(slot_i[:], flat))
        do(dve.tensor_scalar(tile_i[:], slot_i[:], P.bit_length() - 1, None, ALU.arith_shift_right))
        do(dve.tensor_scalar(row_i[:], slot_i[:], P - 1, None, ALU.bitwise_and))
        do(dve.tensor_copy(tile_f[:], tile_i[:]))
        do(dve.tensor_copy(row_f[:], row_i[:]))
        do(dve.tensor_tensor(hot_t[:, :, 0], iota_t[:].unsqueeze(1).to_broadcast([P, CHOICES, TILES]),
                             tile_f[:].unsqueeze(2).to_broadcast([P, CHOICES, TILES]), ALU.is_equal))
        dve.tensor_tensor(hot_t[:, :, 1], hot_t[:, :, 0],
                          val[:].rearrange("p k c -> p (k c)").unsqueeze(2).to_broadcast([P, CHOICES, TILES]),
                          ALU.mult).then_inc(tf_ready, 1)
        for a in range(CHOICES):
            if a >= RINGS:
                dve.wait_ge(tabled, a - RINGS + 1)
            dve.tensor_scalar(hot_r[:, a % RINGS], iota_r[:], row_f[:, a:a + 1], None, ALU.is_equal) \
                .then_inc(onehot, 1)
        do(dve.tensor_tensor(ex_t[:], last_tile[0:1].unsqueeze(1).to_broadcast([1, TILES, NE]),
                             iota_t[0:1].unsqueeze(2).to_broadcast([1, TILES, NE]), ALU.is_le))
        do(dve.tensor_reduce(ex_f[:], ex_t[:], AX_X, ALU.add))
        do(dve.tensor_scalar(tab["expert"][:, 0:TILES], ex_f[:], float(NE - 1), None, ALU.min))
        dve.wait_ge(tabled, CHOICES)
        do(dve.tensor_copy(named[:], pr[:, 0:2 * TILES].rearrange("p (j t) -> p j t", j=2)))
        do(dve.tensor_copy(tab["weight"][:], named[:, 1]))
        do(dve.tensor_scalar(tab["gather"][:, 0:TILES], named[:, 0], 1.0, 0.0, ALU.subtract, ALU.max))
        do(dve.tensor_scalar(empty[:], named[:, 0], 0.0, spare[:], ALU.is_equal, ALU.mult))
        do(dve.scalar_tensor_tensor(dest[:], named[:, 0], 1.0, empty[:], ALU.subtract, ALU.add))
        do(dve.tensor_copy(tab["scatter"][:], dest[:]))

    @block.tensor
    def _(pe):
        flat = chosen[:].rearrange("p c e -> p (c e)")
        pe.wait_ge(chosen_ready, 1)
        pe.matmul(pr[:, 0:CHUNKS * NE], lt[:], flat, start=True, stop=True)
        pe.matmul(pt[:, 0:CHUNKS * NE], ones[:], flat, start=True, stop=True).then_inc(counted, 1)
        pe.wait_ge(tf_ready, 1)
        pe.wait_ge(id_ready, 1)
        for a in range(CHOICES):
            pe.wait_ge(onehot, a + 1)
            pe.matmul(pr[:, 0:2 * TILES], hot_r[:, a % RINGS], hot_t[:, a].rearrange("p j t -> p (j t)"),
                      start=a == 0, stop=a == CHOICES - 1).then_inc(tabled, 1)


def experts(nc, ctx, consts, tab, w1s, w2s, b3, xf_dram, out):
    def sb(name, shape, dt=F32):
        return ctx.enter_context(nc.sbuf_tensor(name, shape, dt))

    def sem(name):
        return ctx.enter_context(nc.semaphore(name))

    def bank(name):
        return ctx.enter_context(nc.psum_tensor(name, [P, 512], F32))

    ident = consts["ident"]
    ones3 = sb("ones3", [3, P], BF16)
    scratch, scratched = sb("scratch_pool", [1, 2]), sem("scratched_pool")
    ig, isc = sb("ig", [P, UNROLL], U32), sb("isc", [P, 2], U32)
    wt = sb("wt", [P, 2])
    xg = sb("xg", [P, UNROLL, D])
    xt = sb("xt", [P, 2, DK, P])
    tg, sg, hh = sb("tg", [P, 2, HID]), sb("sg", [P, 2, HID]), sb("hh", [P, 2, HID])
    ht = sb("ht", [P, 2, FB, P])
    yw = sb("yw", [P, 2, D])
    pa_, pb_ = [bank("pha0"), bank("pha1")], [bank("phb0"), bank("phb1")]
    pxt, pht, pyy = bank("pxt"), bank("pht"), bank("pyy")

    (start, ig_ready, gathered, xt_full, xt_ready, h_full, tanh_ready, hh_ready, ht_full, ht_ready, y_full, wt_ready,
     yw_ready, is_ready, ones_ready, sg_ready) = (
        sem(n) for n in ("start", "ig_ready", "gathered_", "xt_full", "xt_ready", "h_full", "tanh_ready", "hh_ready",
                         "ht_full", "ht_ready", "y_full", "wt_ready", "yw_ready", "is_ready", "ones_ready",
                         "sg_ready"))
    gathered = [sem(f"gathered{k}") for k in range(UNROLL)]
    added = sem("added")
    block = ctx.enter_context(nc.Block())
    ROUNDS = TILES // UNROLL

    @block.gpsimd
    def _(pool):
        pool.memset(scratch[:], 0.0).then_inc(scratched, 1)
        pool.wait_ge(scratched, 1)

        def gather(i, j):
            k = j % UNROLL
            pool.tensor_copy(ig[:, k:k + 1], tab["gather"][:, bass.ds(UNROLL * i + j, 1)]).then_inc(ig_ready, 1)
            pool.wait_ge(ig_ready, UNROLL * i + (j + 1))
            wait_here(pool, scratch)
            pool.indirect_dma_start(xg[:, k], None, xf_dram, bass.IndirectOffsetOnAxis(ap=ig[:, k:k + 1], axis=0)) \
                .then_inc(gathered[k], 16)

        for j in range(AHEAD):
            gather(0, j)

        def body(i, last):
            for j in range(UNROLL):
                if not last or j + AHEAD < UNROLL:
                    pool.wait_ge(xt_full, UNROLL * i + (j + 1))
                    gather(i, j + AHEAD)
                pool.tensor_copy(isc[:, j % 2:j % 2 + 1], tab["scatter"][:, bass.ds(UNROLL * i + j, 1)]) \
                    .then_inc(is_ready, 1)
                pool.wait_ge(is_ready, UNROLL * i + (j + 1))
                pool.wait_ge(yw_ready, UNROLL * i + (j + 1))
                if not (isinstance(i, int) and i == 0 and j == 0):
                    pool.wait_ge(added, 16 * UNROLL * i + 16 * j)
                wait_here(pool, scratch)
                pool.indirect_dma_start(out, bass.IndirectOffsetOnAxis(ap=isc[:, j % 2:j % 2 + 1], axis=0),
                                        yw[:, j % 2], None, compute_op=ALU.add).then_inc(added, 16)

        body(0, False)
        with pool.Fori(1, ROUNDS - 1) as i:
            body(i, False)
        body(ROUNDS - 1, True)
        pool.wait_ge(added, 16 * TILES)

    @block.scalar
    def _(act):
        def xt_copy(i, j):
            act.wait_ge(xt_full, UNROLL * i + (j + 2))
            act.activation(xt[:, j % 2].rearrange("p d t -> p (d t)"), pxt[:, 0:D], ACT.Identity) \
                .then_inc(xt_ready, 1)

        def tanh(i, j):
            act.wait_ge(h_full, UNROLL * i + (j + 1))
            act.activation(tg[:, j % 2], pa_[j % 2][:], ACT.Tanh, scale=0.5).then_inc(tanh_ready, 1)

        def ht_copy(i, j):
            act.wait_ge(ht_full, UNROLL * i + (j + 1))
            act.activation(ht[:, j % 2].rearrange("p f t -> p (f t)"), pht[:], ACT.Identity).then_inc(ht_ready, 1)

        xt_copy(0, 0)
        xt_copy(0, 1)
        tanh(0, 0)

        def body(i, last):
            for j in range(UNROLL):
                if not last or j + 2 < UNROLL:
                    xt_copy(i, j + 2)
                if not last or j + 1 < UNROLL:
                    tanh(i, j + 1)
                ht_copy(i, j)

        with act.Fori(0, ROUNDS - 1) as i:
            body(i, False)
        body(ROUNDS - 1, True)

    @block.vector
    def _(dve):
        dve.memset(ones3[:], 1.0).then_inc(ones_ready, 1)

        def swiglu(i, j):
            b = j % 2
            dve.wait_ge(tanh_ready, UNROLL * i + (j + 1))
            dve.scalar_tensor_tensor(sg[:, b], tg[:, b], 1.0, pa_[b][:], ALU.add, ALU.mult).then_inc(sg_ready, 1)
            dve.wait_ge(sg_ready, UNROLL * i + (j + 1))
            dve.scalar_tensor_tensor(hh[:, b], sg[:, b], 0.5, pb_[b][:], ALU.mult, ALU.mult).then_inc(hh_ready, 1)

        def weigh(i, j):
            b = j % 2
            dve.tensor_copy(wt[:, b:b + 1], tab["weight"][:, bass.ds(UNROLL * i + j, 1)]).then_inc(wt_ready, 1)
            dve.wait_ge(wt_ready, UNROLL * i + (j + 1))
            dve.wait_ge(y_full, UNROLL * i + (j + 1))
            if not (isinstance(i, int) and i == 0 and j < 2):
                dve.wait_ge(added, 16 * UNROLL * i + 16 * (j - 1))
            dve.tensor_scalar(yw[:, b], pyy[:, 0:D], wt[:, b:b + 1], None, ALU.mult).then_inc(yw_ready, 1)

        swiglu(0, 0)

        def body(i, last, first=False):
            for j in range(UNROLL):
                if not last or j + 1 < UNROLL:
                    swiglu(i, j + 1)
                weigh(i, j)

        body(0, False)
        with dve.Fori(1, ROUNDS - 1) as i:
            body(i, False)
        body(ROUNDS - 1, True)

    @block.tensor
    def _(pe):
        pe.sem_inc(xt_full, 1)
        pe.wait_ge(ones_ready, 1)

        def transpose_x(i, j, guard=True):
            k = j % UNROLL
            pe.wait_ge(gathered[k], 16 * i + 16 * (j // UNROLL + 1))
            if guard:
                pe.wait_ge(xt_ready, UNROLL * i + j)
            for d in range(DK):
                ins = pe.transpose(pxt[:, d * P:(d + 1) * P], xg[:, k, d * P:(d + 1) * P], ident[:])
            ins.then_inc(xt_full, 1)

        def expert(i, j):
            return pe.value_load(tab["expert"][0:1, bass.ds(UNROLL * i + j, 1)], min_val=0, max_val=NE - 1)

        def up(i, j, guard=True):
            b = j % 2
            e = expert(i, j)
            if guard:
                pe.wait_ge(hh_ready, UNROLL * i + (j - 1))
            pe.wait_ge(xt_ready, UNROLL * i + (j + 1))
            for half, dst in enumerate((pa_[b], pb_[b])):
                pe.matmul(dst[:], ones3[:], b3[:, bass.ds(e * EB + half * HID, HID)], start=True, stop=False)
                for d in range(DK):
                    ins = pe.matmul(dst[:], xt[:, b, d],
                                    w1s[:, bass.ds(e, 1), d, half * HID:(half + 1) * HID]
                                    .rearrange("p a n -> p (a n)"), start=False, stop=d == DK - 1)
            ins.then_inc(h_full, 1)

        def transpose_h(i, j):
            b = j % 2
            pe.wait_ge(hh_ready, UNROLL * i + (j + 1))
            if not (isinstance(i, int) and i == 0 and j == 0):
                pe.wait_ge(ht_ready, UNROLL * i + j)
            for f in range(FB):
                ins = pe.transpose(pht[:, f * P:(f + 1) * P], hh[:, b, f * P:(f + 1) * P], ident[:])
            ins.then_inc(ht_full, 1)

        def down(i, j):
            b = j % 2
            e = expert(i, j)
            if not (isinstance(i, int) and i == 0 and j == 0):
                pe.wait_ge(yw_ready, UNROLL * i + j)
            pe.matmul(pyy[:, 0:D], ones3[:], b3[:, bass.ds(e * EB + 2 * HID, D)], start=True, stop=False)
            pe.wait_ge(ht_ready, UNROLL * i + (j + 1))
            for f in range(FB):
                ins = pe.matmul(pyy[:, 0:D], ht[:, b, f], w2s[:, bass.ds(e, 1), f].rearrange("p a n -> p (a n)"),
                                start=False, stop=f == FB - 1)
            ins.then_inc(y_full, 1)

        transpose_x(0, 0, guard=False)
        up(0, 0, guard=False)
        transpose_x(0, 1)

        def body(i, last):
            for j in range(UNROLL):
                if not last or j + 2 < UNROLL:
                    transpose_x(i, j + 2)
                if not last or j + 1 < UNROLL:
                    up(i, j + 1, guard=not (isinstance(i, int) and i == 0 and j == 0))
                transpose_h(i, j)
                down(i, j)

        body(0, False)
        with pe.Fori(1, ROUNDS - 1) as i:
            body(i, False)
        body(ROUNDS - 1, True)


def kernel(**inputs):
    import numpy as np
    import concourse.bacc as bacc
    from concourse.bass_utils import run_bass_kernel_spmd

    def arr(name):
        return np.asarray(inputs["L0_" + name])

    def blocks(w):
        return w.reshape(-1, P, w.shape[-1]).transpose(1, 0, 2)

    b_in = arr("attn_b_in")
    n_b = 2 * INNER
    laid = {
        "x": arr("attn_input_tensor").reshape(TOKENS, D),
        "win": blocks(arr("attn_W_in")), "wout": blocks(arr("attn_W_out")),
        "gam": arr("attn_ln_gamma").reshape(DK, P).T, "bet": arr("attn_ln_beta").reshape(DK, P).T,
        "bz": b_in[:INNER].reshape(FB, P).T,
        "bbc": b_in[n_b:n_b + 2 * STATE].reshape(2, STATE).T,
        "bx": b_in[INNER:n_b].reshape(1, INNER),
        "bdt": np.concatenate([b_in[n_b:n_b + STATE], b_in[PROJ - HEADS:]]).reshape(1, -1),
        "alog": arr("attn_A_log").reshape(1, HEADS), "dskip": arr("attn_D_skip").reshape(1, HEADS),
        "dtb": arr("attn_dt_bias").reshape(1, HEADS), "bout": arr("attn_b_out").reshape(1, D),
        "wr": blocks(arr("ffn_Wr").T), "br": arr("ffn_br").reshape(1, NE), "bn": arr("ffn_biases_N").reshape(1, NE),
        "w1": arr("ffn_Wl1").reshape(NE, DK, P, 2 * HID).transpose(2, 0, 1, 3),
        "w2": arr("ffn_Wl2").reshape(NE, FB, P, D).transpose(2, 0, 1, 3),
        "eb": np.concatenate([arr("ffn_bl1"), arr("ffn_bl2")], axis=1).reshape(P, NE * EB // P),
    }
    laid = {k: np.ascontiguousarray(v) for k, v in laid.items()}
    nc = bacc.Bacc("TRN2", target_bir_lowering=False, num_devices=1)
    aps = {k: nc.dram_tensor("in_" + k, v.shape, mybir.dt.from_np(v.dtype), kind="ExternalInput").ap()
           for k, v in laid.items()}
    out = nc.dram_tensor("out_rows", (TOKENS + P, D), F32, kind="ExternalOutput").ap()
    build(nc, out=out, **aps)
    r = run_bass_kernel_spmd(nc, [{"in_" + k: v for k, v in laid.items()}], core_ids=[0])
    return r.results[0]["out_rows"][:TOKENS].reshape(BATCH, SEQ, D)
```

```python
from contextlib import ExitStack

import concourse.bass as bass
from concourse import mybir

ALU = mybir.AluOpType
ACT = mybir.ActivationFunctionType
F32 = mybir.dt.float32
F32R = mybir.dt.float32r
BF16 = mybir.dt.bfloat16
I32 = mybir.dt.int32
U32 = mybir.dt.uint32
AX_X = mybir.AxisListType.X

P = 128
D = 256
DK = D // P
INNER = 512
FB = INNER // P
HEADS = 8
HD = INNER // HEADS
STATE = 64
PROJ = 2 * INNER + 2 * STATE + HEADS
BATCH, SEQ = 4, 1024
TOKENS = BATCH * SEQ
CHUNKS = TOKENS // P
CPS = SEQ // P
GC = 4
GT_ = GC * P
EPS = 1e-5
NE = 8
HID = 512
TOPK = 2
CHOICES = TOPK * CHUNKS
TILES = (TOPK * TOKENS + NE * (P - 1)) // P + 1
EB = 2 * HID + D
UNROLL = 4
AHEAD = 3
TPAD = TILES + AHEAD + 1
GROUP_PRODUCTS = ["u0", "u1", "bd", "cb", "z0", "cum", "z1", "z2", "z3"]
RING = len(GROUP_PRODUCTS)


class Steps:

    def __init__(self, eng, sem, base=0, per_round=0, r=0):
        self.eng, self.sem, self.base, self.per_round, self.r, self.n = eng, sem, base, per_round, r, 0

    def did(self, ins):
        self.n += 1
        ins.then_inc(self.sem, 1)
        return self.n

    def wait(self, n=None):
        n = self.n if n is None else n
        self.eng.wait_ge(self.sem, self.per_round * self.r + (self.base + n) if self.per_round else self.base + n)

    def link(self, ins):
        self.wait(self.did(ins))


def wait_here(eng, scratch):
    eng.tensor_tensor(scratch[:, 0:1], scratch[:, 1:2], scratch[:, 1:2], ALU.add)


def split_matmul(pe, dst, lhs, rhs, start, stop):
    pe.matmul(dst, lhs[1], rhs[0], start=start, stop=False)
    pe.matmul(dst, lhs[0], rhs[1], start=False, stop=False)
    return pe.matmul(dst, lhs[0], rhs[0], start=False, stop=stop)


def build(nc, x, win, wout, gam, bet, bz, bcb, bx, bdt, alog, dskip, dtb, bout, wr, br, bn, w1, w2, eb, out):
    xf_dram = nc.dram_tensor("xf_dram", (TOKENS, D), F32, kind="Internal").ap()
    with ExitStack() as ctx:
        def sb(name, shape, dt=F32, c=ctx):
            return c.enter_context(nc.sbuf_tensor(name, shape, dt))

        consts = {
            "ident": sb("ident", [P, P]), "le": sb("le", [P, P]), "gt": sb("gt", [P, P]),
            "lt": sb("lt", [P, P]), "ones": sb("ones", [P, P]), "half": sb("half", [P, 8]),
        }
        scores = sb("scores", [P, CHUNKS, NE])
        with ExitStack() as c:
            mamba(nc, c, consts, scores, xf_dram, x, win, wout, gam, bet, bz, bcb, bx, bdt, alog, dskip, dtb,
                  bout, wr, out)
        w1s = sb("w1s", [P, NE, DK, 2 * HID])
        w2s = sb("w2s", [P, NE, FB, D])
        b3 = sb("b3", [3, NE * EB], BF16)
        tab = {
            "gather": sb("gather", [P, TPAD], U32), "scatter": sb("scatter", [P, TILES], U32),
            "weight": sb("weight", [P, TILES]), "expert": sb("expert", [1, TPAD], I32),
        }
        with ExitStack() as c:
            route(nc, c, consts, scores, tab, w1s, w2s, b3, w1, w2, eb, br, bn)
        with ExitStack() as c:
            experts(nc, c, consts, tab, w1s, w2s, b3, xf_dram, out)


def mamba(nc, ctx, consts, scores, xf_dram, x, win, wout, gam, bet, bz, bcb, bx, bdt, alog, dskip, dtb, bout,
          wr, out):
    def sb(name, shape, dt=F32):
        return ctx.enter_context(nc.sbuf_tensor(name, shape, dt))

    def sem(name):
        return ctx.enter_context(nc.semaphore(name))

    def bank(name):
        return ctx.enter_context(nc.psum_tensor(name, [P, 512], F32))

    ident, le, gt, lt, ones, half = (consts[k] for k in ("ident", "le", "gt", "lt", "ones", "half"))
    winp = [sb(f"win_{n}", [P, DK, PROJ], F32R) for n in ("high", "low")]
    wouts = sb("wouts", [P, FB, D])
    win_bd = sb("win_bd", [P, DK, STATE + HEADS])
    gtr = sb("gtr", [P, P], F32R)
    wrs = sb("wrs", [P, DK, NE])
    gams, bets = sb("gams", [P, DK]), sb("bets", [P, DK])
    bzs, bzh = sb("bzs", [P, FB]), sb("bzh", [P, FB])
    bcbs = sb("bcbs", [2 * STATE, 1])
    bxs = sb("bxs", [P, INNER])
    bdts, dtbs = sb("bdts", [P, STATE + HEADS]), sb("dtbs", [P, HEADS])
    alogs, nega, dsk = sb("alogs", [P, HEADS]), sb("nega", [P, HEADS]), sb("dsk", [P, HEADS])
    bouts = sb("bouts", [P, D])
    scratch, scratched = sb("scratch", [1, 2]), sem("scratched")
    xi, xr = sb("xi", [P, 2, GC, D]), sb("xr", [P, 2, GC, D])
    x1, u0 = sb("x1", [P, GC, D]), sb("u0", [P, GC, D])
    st = sb("st", [P, GC, 6])
    mv1, mv2 = sb("mv1", [P, GC, 2]), sb("mv2", [P, GC, 2])
    ve1, ve2, rs1, rs2 = (sb(n, [P, GC]) for n in ("ve1", "ve2", "rs1", "rs2"))
    ut = sb("ut", [P, DK, GT_])
    utp = [sb(f"ut_{n}", [P, 2, DK, GT_], F32R) for n in ("high", "low")]
    zh, th = sb("zh", [P, 2, GT_]), sb("th", [P, 2, GT_])
    sil = sb("sil", [P, 2, FB, GT_])
    bt, ct = sb("bt", [STATE, 2, GT_]), sb("ct", [STATE, 2, GT_])
    bd = sb("bd", [P, 2, GC, STATE + HEADS])
    spa, spe, spl, spr = (sb(n, [P, GC, HEADS]) for n in ("spa", "spe", "spl", "spr"))
    dt, aa = sb("dt", [P, 2, GC, HEADS]), sb("aa", [P, 2, GC, HEADS])
    aap = [sb(f"aa_{n}", [P, 2, GC, HEADS], F32R) for n in ("high", "low")]
    ex = sb("ex", [P, 2, 3, GC, HEADS])
    xs, dtx, wx, dxs, y = (sb(n, [P, 2, INNER]) for n in ("xs", "dtx", "wx", "dxs", "y"))
    ya = sb("ya", [P, INNER])
    gT = sb("gT", [P, 2, INNER])
    segr = [sb(f"segr_{n}", [P, HEADS, P], F32R) for n in ("high", "low")]
    lm = sb("lm", [P, 2, HEADS, P])
    gm = sb("gm", [P, 2, P])
    hst = sb("hst", [STATE, 2, INNER])
    xp, xf, xft = sb("xp", [P, 2, D]), sb("xf", [P, 2, D]), sb("xft", [P, 2, DK, P])
    st3, mv3, ve3, rs3 = sb("st3", [P, 6]), sb("mv3", [P, 2]), sb("ve3", [P, 1]), sb("rs3", [P, 1])

    pa = [bank("pa0"), bank("pa1")]
    ps = [bank("ps0"), bank("ps1")]
    px, pg, py, po = bank("px"), bank("pg"), bank("py"), bank("po")

    raw = sil[:].rearrange("p a f t -> p (a f t)")
    win_raw = raw[:, 0:DK * PROJ].rearrange("p (d n) -> p d n", d=DK)

    c_const, c_load, masks = sem("c_const"), sem("c_load"), sem("masks")
    cleared, nega_ready, high_ready, parts_ready, ul_ready = (
        sem(n) for n in ("cleared", "nega_ready", "high_ready", "parts_ready", "ul_ready"))
    x_in, xp_stored, xf_stored = ([sem(f"{n}{k}") for k in range(2)] for n in ("x_in", "xp_stored", "xf_stored"))
    stats1, rstd1, x1_ready, xr_ready, stats2, rstd2, u0_ready = (
        sem(n) for n in ("stats1", "rstd1", "x1_ready", "xr_ready", "stats2", "rstd2", "u0_ready"))
    a_full, a_free, bd_ready, sp_ready, a_ready, sil_ready = (
        sem(n) for n in ("a_full", "a_free", "bd_ready", "sp_ready", "a_ready", "sil_ready"))
    segr_ready, seg_full, l_ready, g_full, gm_ready, m_ready = (
        sem(n) for n in ("segr_ready", "seg_full", "l_ready", "g_full", "gm_ready", "m_ready"))
    x_full, xs_ready, dtx_ready, wx_ready, dxs_ready = (
        sem(n) for n in ("x_full", "xs_ready", "dtx_ready", "wx_ready", "dxs_ready"))
    n_full, st_ready, yi_full, ye_full, y_ready, yt_full, gate_ready, o_full, xp_ready = (
        sem(n) for n in ("n_full", "st_ready", "yi_full", "ye_full", "y_ready", "yt_full", "gate_ready", "o_full",
                         "xp_ready"))
    stats3, rstd3, xf_ready, xft_full, xft_ready, sc_full, sc_ready = (
        sem(n) for n in ("stats3", "rstd3", "xf_ready", "xft_full", "xft_ready", "sc_full", "sc_ready"))
    dve_did, act_did, pool_did = sem("dve_did"), sem("act_did"), sem("pool_did")

    xg_dram = x.rearrange("(g c p) d -> g p c d", p=P, c=GC)
    zero_rows = out[TOKENS:TOKENS + P, :]
    NLOADS = 14

    def par(c):
        return c % 2

    def gpar(c):
        return (c // GC) % 2, c % GC

    def cnt(s, c):
        return s * CPS + (c + 1)

    def gcnt(s, g, per=1):
        return s * (2 * per) + per * (g + 1)

    def states(s, n):
        return s * (CPS - 1) + (n // CPS) * (CPS - 1) + (n % CPS + 1)

    FIRST, ROUND = range(2), range(2, CPS + 2)

    def here(n, end):
        return 0 <= n and not (end and n >= CPS)

    def group_here(g, end):
        return not (end and g >= 2)

    block = ctx.enter_context(nc.Block())

    @block.sync
    def _(sp):
        def load_x(g_dram, half_):
            sp.dma_start(xi[:, half_], g_dram).then_inc(x_in[half_], 16)

        def row(a):
            return a.partition_broadcast(P)

        load_x(xg_dram[0], 0)
        for dst, src in ((gams[:], gam), (bets[:], bet), (win_raw, win), (bzs[:], bz), (bcbs[:], bcb),
                         (bdts[:], row(bdt[0])), (dtbs[:], row(dtb[0])), (bxs[:], row(bx[0])),
                         (alogs[:], row(alog[0])), (dsk[:], row(dskip[0])), (bouts[:], row(bout[0])),
                         (wrs[:], wr), (wouts[:], wout), (win_bd[:], win[:, :, PROJ - STATE - HEADS:])):
            sp.dma_start(dst, src).then_inc(c_load, 16)
        load_x(xg_dram[1], 1)
        sp.wait_ge(cleared, 1)
        sp.dma_start(zero_rows, wx[:, 0, 0:D]).then_inc(c_const, 16)

        def body(s, last):
            for c in range(CPS + 2):
                if c % GC == 0 and c < CPS and not last:
                    g = c // GC
                    sp.wait_ge(xr_ready, gcnt(s, g))
                    load_x(xg_dram[bass.ds(2 * s + (g + 2), 1)].rearrange("a p c d -> (a p) c d"), g)
                if 1 <= c <= CPS:
                    n = c - 1
                    sp.wait_ge(xp_ready, cnt(s, n))
                    sp.dma_start(out[bass.ds(s * SEQ + n * P, P), :], xp[:, par(n)]) \
                        .then_inc(xp_stored[par(n)], 16)
                    sp.wait_ge(xf_ready, cnt(s, n))
                    sp.dma_start(xf_dram[bass.ds(s * SEQ + n * P, P), :], xf[:, par(n)]) \
                        .then_inc(xf_stored[par(n)], 16)

        with sp.Fori(0, BATCH - 1) as s:
            body(s, False)
        body(BATCH - 1, True)
        for k in range(2):
            sp.wait_ge(xp_stored[k], 16 * (CHUNKS // 2 + 1))
            sp.wait_ge(xf_stored[k], 16 * (CHUNKS // 2 + 1))
        sp.wait_ge(c_const, 16)

    @block.gpsimd
    def _(pool):
        steps0 = Steps(pool, masks)
        pool.memset(wx[:, 0, 0:D], 0.0).then_inc(cleared, 1)
        for t, v in ((ident, 0.0), (le, 1.0), (gt, 1.0), (lt, 1.0), (ones, 1.0), (half, -0.5)):
            steps0.did(pool.memset(t[:], v))
        steps0.wait()
        for t, op, base, mult, step, fill in ((ident, ALU.not_equal, 0, 1, -1, 1.0), (le, ALU.is_ge, 0, -1, 1, 0.0),
                                              (gt, ALU.is_gt, 0, 1, -1, 0.0), (lt, ALU.is_gt, 0, -1, 1, 0.0)):
            steps0.did(pool.affine_select(out=t[:], in_=t[:], compare_op=op, fill=fill, base=base,
                                          pattern=[[step, P]], channel_multiplier=mult))
        steps0.wait()

        def rstd(dst, src, n, ready, value, done):
            pool.wait_ge(ready, value)
            pool.tensor_tensor(dst, src, half[:, 0:n], ALU.pow).then_inc(done, 1)

        def residual(s, g, steps, a, b):
            h = g % 2
            pool.wait_ge(x1_ready, gcnt(s, g))
            steps.link(pool.tensor_tensor(xr[:, h, a:b], xi[:, h, a:b], x1[:, a:b], ALU.add))
            ins = pool.tensor_tensor(xr[:, h, a:b], xr[:, h, a:b],
                                     bouts[:].unsqueeze(1).to_broadcast([P, b - a, D]), ALU.add)
            if b == GC:
                ins.then_inc(xr_ready, 1)

        def segment(s, n):
            h, k = gpar(n)
            pool.wait_ge(a_ready, gcnt(s, n // GC))
            if n:
                pool.wait_ge(seg_full, cnt(s, n - 1))
            for part in range(2):
                ins = pool.tensor_tensor(segr[part][:], le[:].unsqueeze(1).to_broadcast([P, HEADS, P]),
                                         aap[part][:, h, k].bitcast(F32).unsqueeze(2).to_broadcast([P, HEADS, P]),
                                         ALU.mult)
            ins.then_inc(segr_ready, 1)

        def heads(t):
            return t.rearrange("p (h d) -> p h d", h=HEADS)

        def per_head(t):
            return t.unsqueeze(2).to_broadcast([P, HEADS, HD])

        def scaled(s, n):
            h, k = gpar(n)
            pool.wait_ge(xs_ready, cnt(s, n))
            pool.tensor_tensor(heads(dtx[:, par(n)]), heads(xs[:, par(n)]), per_head(dt[:, h, k]), ALU.mult) \
                .then_inc(dtx_ready, 1)
            pool.tensor_tensor(heads(dxs[:, par(n)]), heads(xs[:, par(n)]), per_head(dsk[:]), ALU.mult) \
                .then_inc(dxs_ready, 1)
            pool.wait_ge(a_free, gcnt(s, n // GC - 1, RING) + (GROUP_PRODUCTS.index("cum") + 3))
            pool.wait_ge(dtx_ready, cnt(s, n))
            pool.tensor_tensor(heads(wx[:, par(n)]), heads(dtx[:, par(n)]), per_head(ex[:, h, 1, k]), ALU.mult) \
                .then_inc(wx_ready, 1)

        POOL_LINKS = 4
        steps = Steps(pool, pool_did)
        rstd(rs1[:], ve1[:], GC, stats1, 1, rstd1)
        pool.wait_ge(c_load, 16 * NLOADS)
        residual(0, 0, steps, 0, GC)
        rstd(rs2[:], ve2[:], GC, stats2, 1, rstd2)
        segment(0, 0)
        rstd(rs1[:], ve1[:], GC, stats1, 2, rstd1)
        pool.wait_ge(c_const, 16)
        scaled(0, 0)
        segment(0, 1)
        rstd(rs2[:], ve2[:], GC, stats2, 2, rstd2)

        def step(s, c, end, steps):
            k, g = c % GC, c // GC + 1
            if here(c + 1, end):
                scaled(s, c + 1)
            if here(c - 1, end):
                rstd(rs3[:], ve3[:], 1, stats3, cnt(s, c - 1), rstd3)
            if here(c + 2, end):
                segment(s, c + 2)
            if k == 3 and group_here(g + 1, end):
                rstd(rs2[:], ve2[:], GC, stats2, gcnt(s, g + 1), rstd2)
            if k in (1, 2) and group_here(g, end):
                residual(s, g, steps, 2 * (k - 1), 2 * k)
            if k == 2 and group_here(g + 1, end):
                rstd(rs1[:], ve1[:], GC, stats1, gcnt(s, g + 1), rstd1)

        for c in FIRST:
            step(0, c, False, steps)
        base = steps.n
        with pool.Fori(0, BATCH - 1) as s:
            steps = Steps(pool, pool_did, base=base, per_round=POOL_LINKS, r=s)
            for c in ROUND:
                step(s, c, False, steps)
            assert steps.n == POOL_LINKS
        steps = Steps(pool, pool_did, base=base, per_round=POOL_LINKS, r=BATCH - 1)
        for c in ROUND:
            step(BATCH - 1, c, True, steps)

    @block.scalar
    def _(act):
        act.sem_inc(a_free, 2)
        act.sem_inc(xft_ready, 1)
        act.sem_inc(sc_ready, 1)
        for k in range(2):
            act.sem_inc(xp_stored[k], 16)
            act.sem_inc(xf_stored[k], 16)
        act.wait_ge(c_load, 16 * NLOADS)
        act.mul(bzh[:], bzs[:], 0.5).then_inc(act_did, 1)
        act.activation(nega[:], alogs[:], ACT.Exp).then_inc(nega_ready, 1)
        act.wait_ge(act_did, 1)
        act.activation(winp[0][:], win_raw, ACT.Identity).then_inc(high_ready, 1)
        act.wait_ge(masks, 10)
        act.activation(gtr[:], gt[:], ACT.Identity).then_inc(high_ready, 1)

        def group(s, g, parts):
            h = g % 2
            for k, what in enumerate(GROUP_PRODUCTS):
                if what not in parts:
                    continue
                src = pa[k % 2]
                if what != "bd":
                    act.wait_ge(a_full, gcnt(s, g - 1, RING) + (k + 1))
                if what in ("u0", "u1"):
                    d = int(what[1])
                    act.activation(ut[:, d], src[:], ACT.Identity, bias=bets[:, d:d + 1],
                                   scale=gams[:, d:d + 1])
                    act.activation(utp[0][:, h, d], src[:], ACT.Identity, bias=bets[:, d:d + 1],
                                   scale=gams[:, d:d + 1]).then_inc(a_free, 1)
                elif what == "bd":
                    act.wait_ge(bd_ready, gcnt(s, g))
                    act.activation(spa[:], bd[:, h, :, STATE:], ACT.Abs).then_inc(act_did, 1)
                    act.activation(spr[:], bd[:, h, :, STATE:], ACT.Relu).then_inc(a_free, 1)
                    act.wait_ge(act_did, gcnt(s, g - 1, 2) + 2)
                    act.activation(spe[:], spa[:], ACT.Exp, scale=-1.0).then_inc(act_did, 1)
                    act.wait_ge(act_did, gcnt(s, g - 1, 2) + 3)
                    act.activation(spl[:], spe[:], ACT.Ln, bias=1.0).then_inc(sp_ready, 1)
                elif what == "cb":
                    act.activation(ct[:, h], src[0:STATE, :], ACT.Identity, bias=bcbs[0:STATE])
                    act.activation(bt[:, h], src[STATE:2 * STATE, :], ACT.Identity, bias=bcbs[STATE:2 * STATE]) \
                        .then_inc(a_free, 1)
                elif what == "cum":
                    act.activation(ex[:, h].rearrange("p a c n -> p (a c n)"), src[:, 0:3 * GC * HEADS], ACT.Exp) \
                        .then_inc(a_free, 1)
                else:
                    f = int(what[1])
                    act.wait_ge(sil_ready, gcnt(s, g - 1, FB) + (f + 1))
                    act.activation(zh[:, f % 2], src[:], ACT.Identity, bias=bzh[:, f:f + 1], scale=0.5)
                    act.activation(th[:, f % 2], src[:], ACT.Tanh, bias=bzh[:, f:f + 1], scale=0.5) \
                        .then_inc(a_free, 1)

        def decay(s, n):
            act.wait_ge(seg_full, cnt(s, n))
            act.activation(lm[:, par(n), 0:4], ps[0][:].rearrange("p (h i) -> p h i", h=4), ACT.Exp)
            act.activation(lm[:, par(n), 4:8], ps[1][:].rearrange("p (h i) -> p h i", h=4), ACT.Exp) \
                .then_inc(l_ready, 1)

        def turned(s, n):
            act.wait_ge(xft_full, cnt(s, n))
            act.activation(xft[:, par(n)].rearrange("p d t -> p (d t)"), ps[0][:, 0:D], ACT.Identity) \
                .then_inc(xft_ready, 1)

        def score(s, n):
            act.wait_ge(sc_full, cnt(s, n))
            act.activation(scores[:, bass.ds(s * CPS + n, 1)], ps[1][:, 0:NE].unsqueeze(1), ACT.Identity) \
                .then_inc(sc_ready, 1)

        group(0, 0, GROUP_PRODUCTS)
        decay(0, 0)

        def step(s, c, end):
            k, g = c % GC, c // GC + 1

            def place(name):
                if group_here(g, end):
                    group(s, g, [what for what in PLACES[k].get(name, ()) if what != "bd"])

            place("first")
            if here(c + 1, end):
                decay(s, c + 1)
            place("a")
            if here(c - 2, end):
                turned(s, c - 2)
            place("b")
            if here(c - 2, end):
                score(s, c - 2)
            if k == 1 and group_here(g, end):
                group(s, g, ["bd"])
            place("c")

        for c in FIRST:
            step(0, c, False)
        with act.Fori(0, BATCH - 1) as s:
            for c in ROUND:
                step(s, c, False)
        for c in ROUND:
            step(BATCH - 1, c, True)

    @block.vector
    def _(dve):
        dve.memset(scratch[:], 0.0).then_inc(scratched, 1)
        dve.wait_ge(scratched, 1)
        dve.sem_inc(sil_ready, 2)
        dve.wait_ge(nega_ready, 1)
        dve.wait_ge(masks, 10)

        def stats(src, ve, mv, steps, done):
            n = [steps.did(dve.bn_stats(st[:, k], src[:, k])) for k in range(GC)]
            steps.wait(n[-1])
            wait_here(dve, scratch)
            for k in range(GC):
                m = steps.did(dve.bn_aggr(mv[:, k], st[:, k]))
            steps.wait(m)
            dve.tensor_scalar(ve[:], mv[:, :, 1], EPS, None, ALU.add).then_inc(done, 1)

        def normalise(dst, src, mv, rs, done):
            for k in range(GC):
                ins = dve.tensor_scalar(dst[:, k], src[:, k], mv[:, k, 0:1], rs[:, k:k + 1], ALU.subtract, ALU.mult)
            ins.then_inc(done, 1)

        def first_stats(s, g, steps):
            dve.wait_ge(x_in[g % 2], 16 * s + 16 * (g // 2 + 1))
            stats(xi[:, g % 2], ve1, mv1, steps, stats1)

        def first_norm(s, g, steps):
            dve.wait_ge(rstd1, gcnt(s, g))
            if not (isinstance(s, int) and 2 * s + g == 0):
                dve.wait_ge(xr_ready, gcnt(s, g - 1))
            normalise(x1, xi[:, g % 2], mv1, rs1, x1_ready)
            dve.wait_ge(x1_ready, gcnt(s, g))
            stats(x1, ve2, mv2, steps, stats2)

        def second_norm(s, g):
            dve.wait_ge(rstd2, gcnt(s, g))
            if not (isinstance(s, int) and 2 * s + g == 0):
                dve.wait_ge(a_full, gcnt(s, g - 2, RING) + 2)
            normalise(u0, x1, mv2, rs2, u0_ready)

        def low_u(s, g):
            for d in range(DK):
                dve.wait_ge(a_free, gcnt(s, g - 1, RING) + (d + 3))
                dve.tensor_tensor(utp[1][:, g % 2, d], ut[:, d], utp[0][:, g % 2, d].bitcast(F32), ALU.subtract) \
                    .then_inc(ul_ready, 1)

        def steps_dt(s, g, steps):
            h = g % 2
            dve.wait_ge(sp_ready, gcnt(s, g))
            steps.link(dve.tensor_tensor(dt[:, h], spr[:], spl[:], ALU.add))
            steps.link(dve.scalar_tensor_tensor(aa[:, h], dt[:, h], -1.0,
                                                nega[:].unsqueeze(1).to_broadcast([P, GC, HEADS]), ALU.mult, ALU.mult))
            steps.link(dve.tensor_copy(aap[0][:, h], aa[:, h]))
            dve.tensor_tensor(aap[1][:, h], aa[:, h], aap[0][:, h].bitcast(F32), ALU.subtract).then_inc(a_ready, 1)

        def by_token(s, g):
            n = GC * (STATE + HEADS)
            dve.wait_ge(a_full, gcnt(s, g - 1, RING) + (GROUP_PRODUCTS.index("bd") + 1))
            dve.tensor_tensor(bd[:, g % 2], pa[0][:, 0:n].rearrange("p (c n) -> p c n", c=GC),
                              bdts[:].unsqueeze(1).to_broadcast([P, GC, STATE + HEADS]), ALU.add).then_inc(bd_ready, 1)

        def silu(s, g, f):
            dve.wait_ge(a_free, gcnt(s, g - 1, RING) + (GROUP_PRODUCTS.index(f"z{f}") + 3))
            dve.scalar_tensor_tensor(sil[:, g % 2, f], th[:, f % 2], 1.0, zh[:, f % 2], ALU.add, ALU.mult) \
                .then_inc(sil_ready, 1)

        def inner_x(s, n):
            dve.wait_ge(x_full, cnt(s, n))
            dve.tensor_tensor(xs[:, par(n)], px[:], bxs[:], ALU.add).then_inc(xs_ready, 1)

        def masked(s, n):
            dve.wait_ge(g_full, cnt(s, n))
            dve.tensor_tensor(gm[:, par(n)], pg[:, 0:P], le[:], ALU.mult).then_inc(gm_ready, 1)

        def mixing(s, n):
            dve.wait_ge(gm_ready, cnt(s, n))
            dve.wait_ge(l_ready, cnt(s, n))
            dve.tensor_tensor(lm[:, par(n)], lm[:, par(n)],
                              gm[:, par(n)].unsqueeze(1).to_broadcast([P, HEADS, P]), ALU.mult).then_inc(m_ready, 1)

        def state(s, n, steps):
            h, k = gpar(n)
            dve.wait_ge(n_full, states(s, n))
            if n % CPS == 0:
                dve.tensor_copy(hst[:, 1], pg[0:STATE, :]).then_inc(st_ready, 1)
                return
            new = hst[:, par(n + 1)]
            dve.wait_ge(st_ready, states(s, n - 1))
            steps.link(dve.tensor_tensor(new.rearrange("p (h d) -> p h d", h=HEADS),
                                         hst[:, par(n)].rearrange("p (h d) -> p h d", h=HEADS),
                                         ex[0:STATE, h, 2, k].unsqueeze(2).to_broadcast([STATE, HEADS, HD]), ALU.mult))
            dve.tensor_tensor(new, new, pg[0:STATE, :], ALU.add).then_inc(st_ready, 1)

        def gate(s, n):
            h, k = gpar(n)
            dve.wait_ge(yt_full, cnt(s, n))
            dve.wait_ge(sil_ready, gcnt(s, n // GC, FB) + 2)
            dve.tensor_tensor(gT[:, par(n)].rearrange("p (f t) -> p f t", f=FB),
                              py[:].rearrange("p (f t) -> p f t", f=FB), sil[:, h, :, k * P:(k + 1) * P], ALU.mult) \
                .then_inc(gate_ready, 1)

        def residual(s, n, steps):
            h, k = gpar(n)
            dve.wait_ge(o_full, cnt(s, n))
            dve.wait_ge(xp_stored[par(n)], s * (8 * CPS) + 16 * (n // 2 + 1))
            dve.tensor_tensor(xp[:, par(n)], po[:, 0:D], xr[:, h, k], ALU.add).then_inc(xp_ready, 1)
            dve.wait_ge(xp_ready, cnt(s, n))
            a = steps.did(dve.bn_stats(st3[:], xp[:, par(n)]))
            steps.wait(a)
            wait_here(dve, scratch)
            steps.link(dve.bn_aggr(mv3[:], st3[:]))
            dve.tensor_scalar(ve3[:], mv3[:, 1:2], EPS, None, ALU.add).then_inc(stats3, 1)

        def last_norm(s, n):
            dve.wait_ge(rstd3, cnt(s, n))
            dve.wait_ge(xf_stored[par(n)], s * (8 * CPS) + 16 * (n // 2 + 1))
            dve.tensor_scalar(xf[:, par(n)], xp[:, par(n)], mv3[:, 0:1], rs3[:], ALU.subtract, ALU.mult) \
                .then_inc(xf_ready, 1)

        def output(s, n, steps):
            h, k = gpar(n)
            dve.wait_ge(yi_full, cnt(s, n))
            dve.wait_ge(dxs_ready, cnt(s, n))
            yy = y[:, par(n)]
            if n % CPS:
                steps.did(dve.tensor_tensor(yy, py[:], dxs[:, par(n)], ALU.add))
                dve.wait_ge(ye_full, states(s, n - 1))
                steps.link(dve.tensor_tensor(ya[:].rearrange("p (h d) -> p h d", h=HEADS),
                                             po[:].rearrange("p (h d) -> p h d", h=HEADS),
                                             ex[:, h, 0, k].unsqueeze(2).to_broadcast([P, HEADS, HD]), ALU.mult))
                dve.tensor_tensor(yy, yy, ya[:], ALU.add).then_inc(y_ready, 1)
            else:
                dve.tensor_tensor(yy, py[:], dxs[:, par(n)], ALU.add).then_inc(y_ready, 1)

        steps = Steps(dve, dve_did)
        dve.wait_ge(high_ready, 1)
        dve.tensor_tensor(winp[1][:], win_raw, winp[0][:].bitcast(F32), ALU.subtract).then_inc(parts_ready, 1)
        first_stats(0, 0, steps)
        first_norm(0, 0, steps)
        second_norm(0, 0)
        low_u(0, 0)
        dve.wait_ge(parts_ready, 1)
        steps.link(dve.tensor_tensor(bdts[:, STATE:], bdts[:, STATE:], dtbs[:], ALU.add))
        by_token(0, 0)
        silu(0, 0, 0)
        steps_dt(0, 0, steps)
        for f in range(1, FB):
            silu(0, 0, f)
        inner_x(0, 0)
        masked(0, 0)
        mixing(0, 0)
        first_stats(0, 1, steps)
        first_norm(0, 1, steps)

        def step(s, c, end, steps):
            k, g = c % GC, c // GC + 1
            if here(c, end):
                output(s, c, steps)
                if c % CPS != CPS - 1:
                    state(s, c, steps)
            if here(c + 1, end):
                inner_x(s, c + 1)
            if here(c, end):
                if k == 0 and c:
                    silu(s, g - 1, 2)
                    silu(s, g - 1, 3)
                gate(s, c)
            if here(c + 1, end):
                masked(s, c + 1)
                mixing(s, c + 1)
            if here(c - 1, end):
                residual(s, c - 1, steps)
            if k == 1 and group_here(g, end):
                by_token(s, g)
                low_u(s, g)
            if k == 2 and group_here(g, end):
                steps_dt(s, g, steps)
            if k == 3 and group_here(g + 1, end):
                first_norm(s, g + 1, steps)
            if here(c - 1, end):
                last_norm(s, c - 1)
            if k == 2 and group_here(g + 1, end):
                first_stats(s, g + 1, steps)
            if k == 0 and group_here(g, end):
                second_norm(s, g)
            if k == 2 and group_here(g, end):
                silu(s, g, 0)
            if k == 3 and group_here(g, end):
                silu(s, g, 1)

        for c in FIRST:
            step(0, c, False, steps)
        base = steps.n
        DVE_STEPS = 2 * (4 * GC + 3) + (CPS - 2) + 2 * CPS + 2 * (CPS - 1)
        with dve.Fori(0, BATCH - 1) as s:
            steps = Steps(dve, dve_did, base=base, per_round=DVE_STEPS, r=s)
            for c in ROUND:
                step(s, c, False, steps)
            assert steps.n == DVE_STEPS
        steps = Steps(dve, dve_did, base=base, per_round=DVE_STEPS, r=BATCH - 1)
        for c in ROUND:
            step(BATCH - 1, c, True, steps)

    @block.tensor
    def _(pe):
        pe.wait_ge(masks, 10)
        pe.wait_ge(high_ready, 2)
        pe.wait_ge(parts_ready, 1)

        def group(s, g, parts):
            h = g % 2
            for k, what in enumerate(GROUP_PRODUCTS):
                if what not in parts:
                    continue
                dst = pa[k % 2]
                pe.wait_ge(a_free, gcnt(s, g - 1, RING) + max(k + 1, 2))
                if what in ("u0", "u1"):
                    d = int(what[1])
                    pe.wait_ge(u0_ready, gcnt(s, g))
                    for c in range(GC):
                        ins = pe.transpose(dst[:, c * P:(c + 1) * P], u0[:, c, d * P:(d + 1) * P], ident[:])
                elif what == "bd":
                    pe.wait_ge(a_free, gcnt(s, g - 1, RING) + 4)
                    n0 = STATE + HEADS
                    for c in range(GC):
                        for d in range(DK):
                            ins = pe.matmul(dst[:, c * n0:(c + 1) * n0], ut[:, d, c * P:(c + 1) * P], win_bd[:, d],
                                            start=d == 0, stop=d == DK - 1)
                elif what == "cb":
                    pe.wait_ge(ul_ready, gcnt(s, g, 2))
                    for d in range(DK):
                        ins = split_matmul(pe, dst[:], [w[:, d, 2 * INNER:2 * INNER + 2 * STATE] for w in winp],
                                           [u[:, h, d] for u in utp], d == 0, d == DK - 1)
                elif what == "cum":
                    pe.wait_ge(a_ready, gcnt(s, g))
                    n = GC * HEADS
                    for j, m in enumerate((le, gt, ones)):
                        ins = pe.matmul(dst[:, j * n:(j + 1) * n], m[:], aa[:, h].rearrange("p c n -> p (c n)"),
                                        start=True, stop=True)
                else:
                    f = int(what[1])
                    for d in range(DK):
                        ins = split_matmul(pe, dst[:], [w[:, d, f * P:(f + 1) * P] for w in winp],
                                           [u[:, h, d] for u in utp], d == 0, d == DK - 1)
                ins.then_inc(a_full, 1)

        def inner_x(s, n):
            h, k = gpar(n)
            if n:
                pe.wait_ge(xs_ready, cnt(s, n - 1))
            for d in range(DK):
                ins = split_matmul(pe, px[:], [u[:, h, d, k * P:(k + 1) * P] for u in utp],
                                   [w[:, d, INNER:2 * INNER] for w in winp], d == 0, d == DK - 1)
            ins.then_inc(x_full, 1)

        def segment_sums(s, n):
            pe.wait_ge(segr_ready, cnt(s, n))
            if n:
                pe.wait_ge(l_ready, cnt(s, n - 1))
                pe.wait_ge(xft_ready, s * CPS + (max(n - 3, 0) + 1))
                pe.wait_ge(sc_ready, s * CPS + (max(n - 3, 0) + 1))
            for j in range(2):
                for part in (1, 0):
                    ins = pe.matmul(ps[j][:], gtr[:], segr[part][:, 4 * j:4 * j + 4].rearrange("p h i -> p (h i)"),
                                    start=part == 1, stop=part == 0)
            ins.then_inc(seg_full, 1)

        def scores_cb(s, n):
            h, k = gpar(n)
            pe.wait_ge(a_free, gcnt(s, n // GC - 1, RING) + (GROUP_PRODUCTS.index("cb") + 3))
            if n % CPS:
                pe.wait_ge(st_ready, states(s, n - 1))
            elif n:
                pe.wait_ge(gm_ready, cnt(s, n - 1))
            pe.matmul(pg[:, 0:P], bt[:, h, k * P:(k + 1) * P], ct[:, h, k * P:(k + 1) * P], start=True, stop=True) \
                .then_inc(g_full, 1)

        def new_state(s, n):
            h, k = gpar(n)
            pe.wait_ge(wx_ready, cnt(s, n))
            pe.wait_ge(gm_ready, cnt(s, n))
            pe.matmul(pg[0:STATE, :], bd[:, h, k, 0:STATE], wx[:, par(n)], start=True, stop=True).then_inc(n_full, 1)

        def transposed(s, n):
            pe.wait_ge(y_ready, cnt(s, n))
            for f in range(FB):
                ins = pe.transpose(py[:, f * P:(f + 1) * P], y[:, par(n), f * P:(f + 1) * P], ident[:])
            ins.then_inc(yt_full, 1)

        def out_proj(s, n):
            pe.wait_ge(gate_ready, cnt(s, n))
            if (n + 1) % CPS == 0:
                pe.wait_ge(xp_ready, cnt(s, n - 1))
            for f in range(FB):
                ins = pe.matmul(po[:, 0:D], gT[:, par(n), f * P:(f + 1) * P], wouts[:, f], start=f == 0,
                                stop=f == FB - 1)
            ins.then_inc(o_full, 1)

        def within(s, n):
            pe.wait_ge(m_ready, cnt(s, n))
            pe.wait_ge(dtx_ready, cnt(s, n))
            if n:
                pe.wait_ge(gate_ready, cnt(s, n - 1))
            for hh in range(HEADS):
                ins = pe.matmul(py[:, hh * HD:(hh + 1) * HD], lm[:, par(n), hh], dtx[:, par(n), hh * HD:(hh + 1) * HD],
                                start=True, stop=True)
            ins.then_inc(yi_full, 1)

        def across(s, n):
            h, k = gpar(n)
            pe.wait_ge(st_ready, states(s, n - 1))
            if n >= 2:
                pe.wait_ge(xp_ready, cnt(s, n - 2))
            pe.matmul(po[:], ct[:, h, k * P:(k + 1) * P], hst[:, par(n)], start=True, stop=True).then_inc(ye_full, 1)

        def turn_xf(s, n, exps):
            pe.wait_ge(xf_ready, cnt(s, n))
            pe.wait_ge(l_ready, cnt(s, exps))
            pe.wait_ge(sc_ready, s * CPS + (n + 1))
            for d in range(DK):
                ins = pe.transpose(ps[0][:, d * P:(d + 1) * P], xf[:, par(n), d * P:(d + 1) * P], ident[:])
            ins.then_inc(xft_full, 1)

        def router(s, n):
            pe.wait_ge(xft_ready, s * CPS + (n + 2))
            for d in range(DK):
                ins = pe.matmul(ps[1][:, 0:NE], xft[:, par(n), d], wrs[:, d], start=d == 0, stop=d == DK - 1)
            ins.then_inc(sc_full, 1)

        group(0, 0, GROUP_PRODUCTS)
        inner_x(0, 0)
        segment_sums(0, 0)
        scores_cb(0, 0)
        within(0, 0)

        def step(s, c, end):
            k, g = c % GC, c // GC + 1

            def place(name):
                if group_here(g, end):
                    group(s, g, PLACES[k].get(name, ()))

            if here(c, end) and c % CPS != CPS - 1:
                new_state(s, c)
            if here(c + 1, end):
                inner_x(s, c + 1)
            place("first")
            if here(c + 1, end):
                segment_sums(s, c + 1)
            if here(c, end):
                transposed(s, c)
            place("a")
            if here(c + 1, end):
                scores_cb(s, c + 1)
            if here(c - 1, end):
                out_proj(s, c - 1)
            if here(c - 2, end):
                turn_xf(s, c - 2, c + 1 if here(c + 1, end) else CPS - 1)
            place("b")
            if here(c - 2, end):
                router(s, c - 2)
            if here(c + 1, end):
                within(s, c + 1)
                if (c + 1) % CPS:
                    across(s, c + 1)
            place("c")

        for c in FIRST:
            step(0, c, False)
        with pe.Fori(0, BATCH - 1) as s:
            for c in ROUND:
                step(s, c, False)
        for c in ROUND:
            step(BATCH - 1, c, True)


PLACES = [{}, {"first": ["u0", "u1"], "a": ["bd"]}, {"a": ["cb"], "b": ["z0"], "c": ["cum"]},
          {"a": ["z1"], "b": ["z2"], "c": ["z3"]}]


def route(nc, ctx, consts, scores, tab, w1s, w2s, b3, w1, w2, eb, br, bn):
    def sb(name, shape, dt=F32):
        return ctx.enter_context(nc.sbuf_tensor(name, shape, dt))

    def sem(name):
        return ctx.enter_context(nc.semaphore(name))

    lt, ones = consts["lt"], consts["ones"]
    te = [P, CHUNKS, NE]
    brs, bns = sb("brs", [P, NE]), sb("bns", [P, NE])
    ebs, eb_rest, eb3 = sb("ebs", [P, NE * EB // P]), sb("eb_rest", [P, NE * EB // P]), \
        sb("eb3", [P, 3, NE * EB // P], BF16)
    top, wts, biased, cand = sb("top", [P, CHUNKS]), sb("wts", te), sb("biased", te), sb("cand", te)
    pick = sb("pick", [P, TOPK, CHUNKS, NE])
    order = sb("order", [P, NE])
    val = sb("val", [P, TOPK, CHUNKS])
    total = sb("total", [P, CHUNKS])
    chosen = sb("chosen", te)
    before = [sb("before0", te), sb("before1", te)]
    many, iota_k = sb("many", [P, NE, CHUNKS]), sb("iota_k", [P, CHUNKS])
    tiles = sb("tiles", [P, NE])
    upto = [sb("upto0", [P, NE]), sb("upto1", [P, NE])]
    base = sb("base", [P, NE])
    slot, slots = sb("slot", te), sb("slots", [P, TOPK, CHUNKS])
    slot_i, tile_i, row_i = (sb(n, [P, CHOICES], I32) for n in ("slot_i", "tile_i", "row_i"))
    tile_f, row_f = sb("tile_f", [P, CHOICES]), sb("row_f", [P, CHOICES])
    iota_r, iota_t = sb("iota_r", [P, P]), sb("iota_t", [P, TILES])
    token1 = sb("token1", [P, TOPK, CHUNKS])
    spare = sb("spare", [P, 1])
    hot_t = sb("hot_t", [P, CHOICES, 2, TILES])
    RINGS = 4
    hot_r = sb("hot_r", [P, RINGS, P])
    named = sb("named", [P, 2, TILES])
    empty, dest = sb("empty", [P, TILES]), sb("dest", [P, TILES])
    ex_t, ex_f = sb("ex_t", [1, TILES, NE]), sb("ex_f", [1, TILES])
    pr = ctx.enter_context(nc.psum_tensor("pr", [P, 512], F32))
    pt = ctx.enter_context(nc.psum_tensor("pt", [P, 512], F32))

    rows_in, loaded, w_in, b_in, b_out, iotas, e_in, e_out, chosen_ready, counted = (
        sem(n) for n in ("rows_in", "r_loaded", "w_in", "b_in", "b_out", "iotas", "e_in", "e_out", "chosen_ready", "counted"))
    onehot, tabled, did, w_ready, id_ready, tf_ready = (
        sem(n) for n in ("onehot", "tabled", "route_did", "w_ready", "id_ready", "tf_ready"))
    block = ctx.enter_context(nc.Block())

    @block.sync
    def _(sp):
        sp.dma_start(brs[:], br[0].partition_broadcast(P)).then_inc(rows_in, 16)
        sp.dma_start(bns[:], bn[0].partition_broadcast(P)).then_inc(rows_in, 16)
        sp.dma_start(ebs[:], eb).then_inc(b_in, 16)
        for e in range(NE):
            sp.dma_start(w1s[:, e], w1[:, e]).then_inc(w_in, 16)
            sp.dma_start(w2s[:, e], w2[:, e]).then_inc(w_in, 16)
        sp.wait_ge(b_out, 1)
        for k in range(3):
            sp.dma_start(b3[k:k + 1, :], eb3[:, k]).then_inc(loaded, 16)
        sp.wait_ge(loaded, 16 * 3)
        sp.wait_ge(w_in, 16 * 2 * NE)

    @block.gpsimd
    def _(pool):
        for t, pattern, start, mult in ((order[:], [[-1, NE]], NE, 0), (iota_k[:], [[P, CHUNKS]], 0, 0),
                                        (iota_r[:], [[1, P]], 0, 0), (iota_t[:], [[1, TILES]], 0, 0),
                                        (token1[:], [[0, TOPK], [P, CHUNKS]], 1, 1), (spare[:], [[0, 1]], TOKENS + 1, 1)):
            pool.iota(t, pattern=pattern, base=start, channel_multiplier=mult,
                      allow_small_or_imprecise_dtypes=True).then_inc(iotas, 1)
        pool.memset(tab["gather"][:, TILES:], 0)
        pool.memset(tab["expert"][:, TILES:], 0).then_inc(iotas, 1)
        pool.wait_ge(iotas, 7)
        pool.wait_ge(tf_ready, 1)
        pool.tensor_tensor(hot_t[:, :, 0], hot_t[:, :, 0],
                           token1[:].rearrange("p k c -> p (k c)").unsqueeze(2).to_broadcast([P, CHOICES, TILES]),
                           ALU.mult).then_inc(id_ready, 1)

    @block.scalar
    def _(act):
        act.wait_ge(e_in, 1)
        act.activation(wts[:], wts[:], ACT.Exp).then_inc(e_out, 1)

    @block.vector
    def _(dve):
        steps = Steps(dve, did)
        do = steps.link

        def per_chunk(t):
            return t.unsqueeze(2).to_broadcast(te)

        def per_expert(t):
            return t[:].unsqueeze(1).to_broadcast(te)

        dve.wait_ge(b_in, 16)
        do(dve.tensor_copy(eb3[:, 0], ebs[:]))
        do(dve.tensor_tensor(eb_rest[:], ebs[:], eb3[:, 0], ALU.subtract))
        do(dve.tensor_copy(eb3[:, 1], eb_rest[:]))
        do(dve.tensor_tensor(eb_rest[:], eb_rest[:], eb3[:, 1], ALU.subtract))
        dve.tensor_copy(eb3[:, 2], eb_rest[:]).then_inc(b_out, 1)
        dve.wait_ge(rows_in, 32)
        do(dve.tensor_tensor(scores[:], scores[:], per_expert(brs), ALU.add))
        do(dve.tensor_reduce(top[:], scores[:], AX_X, ALU.max))
        dve.tensor_tensor(wts[:], scores[:], per_chunk(top[:]), ALU.subtract).then_inc(e_in, 1)
        do(dve.tensor_tensor(biased[:], scores[:], per_expert(bns), ALU.add))
        dve.wait_ge(iotas, 7)
        for k in range(TOPK):
            do(dve.tensor_reduce(top[:], biased[:], AX_X, ALU.max))
            do(dve.tensor_tensor(cand[:], biased[:], per_chunk(top[:]), ALU.is_equal))
            do(dve.tensor_tensor(cand[:], cand[:], per_expert(order), ALU.mult))
            do(dve.tensor_reduce(top[:], cand[:], AX_X, ALU.max))
            do(dve.tensor_tensor(pick[:, k], cand[:], per_chunk(top[:]), ALU.is_equal))
            if k == 0:
                do(dve.scalar_tensor_tensor(biased[:], pick[:, 0], -3e38, biased[:], ALU.mult, ALU.add))
        dve.tensor_tensor(chosen[:], pick[:, 0], pick[:, 1], ALU.add).then_inc(chosen_ready, 1)
        dve.wait_ge(e_out, 1)
        do(dve.tensor_reduce(total[:], wts[:], AX_X, ALU.add))
        do(dve.reciprocal(total[:], total[:]))
        do(dve.tensor_tensor(wts[:], wts[:], per_chunk(total[:]), ALU.mult))
        for k in range(TOPK):
            do(dve.tensor_tensor(cand[:], wts[:], pick[:, k], ALU.mult))
            do(dve.tensor_reduce(val[:, k], cand[:], AX_X, ALU.add))
        do(dve.tensor_tensor(total[:], val[:, 0], val[:, 1], ALU.add))
        do(dve.reciprocal(total[:], total[:]))
        do(dve.tensor_tensor(val[:], val[:], total[:].unsqueeze(1).to_broadcast([P, TOPK, CHUNKS]), ALU.mult))
        dve.wait_ge(counted, 1)
        do(dve.tensor_copy(before[0][:], pt[:, 0:CHUNKS * NE].rearrange("p (c e) -> p c e", e=NE)))
        src, far = 0, 1
        while far < CHUNKS:
            a, b = before[src], before[1 - src]
            steps.did(dve.tensor_copy(b[:, 0:far], a[:, 0:far]))
            do(dve.tensor_tensor(b[:, far:], a[:, far:], a[:, 0:CHUNKS - far], ALU.add))
            src, far = 1 - src, 2 * far
        upto_chunk = before[src]
        do(dve.tensor_tensor(many[:], upto_chunk[:, CHUNKS - 1].unsqueeze(2).to_broadcast([P, NE, CHUNKS]),
                             iota_k[:].unsqueeze(1).to_broadcast([P, NE, CHUNKS]), ALU.is_gt))
        do(dve.tensor_reduce(tiles[:], many[:], AX_X, ALU.add))
        do(dve.tensor_copy(upto[0][:], tiles[:]))
        s2, far = 0, 1
        while far < NE:
            a, b = upto[s2], upto[1 - s2]
            steps.did(dve.tensor_copy(b[:, 0:far], a[:, 0:far]))
            do(dve.tensor_tensor(b[:, far:], a[:, far:], a[:, 0:NE - far], ALU.add))
            s2, far = 1 - s2, 2 * far
        last_tile = upto[s2]
        do(dve.tensor_tensor(base[:], last_tile[:], tiles[:], ALU.subtract))
        do(dve.tensor_tensor(slot[:], upto_chunk[:], pt[:, 0:CHUNKS * NE].rearrange("p (c e) -> p c e", e=NE),
                             ALU.subtract))
        do(dve.tensor_tensor(slot[:], slot[:], pr[:, 0:CHUNKS * NE].rearrange("p (c e) -> p c e", e=NE), ALU.add))
        do(dve.scalar_tensor_tensor(slot[:], per_expert(base), float(P), slot[:], ALU.mult, ALU.add))
        for k in range(TOPK):
            do(dve.tensor_tensor(cand[:], slot[:], pick[:, k], ALU.mult))
            do(dve.tensor_reduce(slots[:, k], cand[:], AX_X, ALU.add))
        flat = slots[:].rearrange("p k c -> p (k c)")
        do(dve.tensor_copy(slot_i[:], flat))
        do(dve.tensor_scalar(tile_i[:], slot_i[:], P.bit_length() - 1, None, ALU.arith_shift_right))
        do(dve.tensor_scalar(row_i[:], slot_i[:], P - 1, None, ALU.bitwise_and))
        do(dve.tensor_copy(tile_f[:], tile_i[:]))
        do(dve.tensor_copy(row_f[:], row_i[:]))
        do(dve.tensor_tensor(hot_t[:, :, 0], iota_t[:].unsqueeze(1).to_broadcast([P, CHOICES, TILES]),
                             tile_f[:].unsqueeze(2).to_broadcast([P, CHOICES, TILES]), ALU.is_equal))
        dve.tensor_tensor(hot_t[:, :, 1], hot_t[:, :, 0],
                          val[:].rearrange("p k c -> p (k c)").unsqueeze(2).to_broadcast([P, CHOICES, TILES]),
                          ALU.mult).then_inc(tf_ready, 1)
        for a in range(CHOICES):
            if a >= RINGS:
                dve.wait_ge(tabled, a - RINGS + 1)
            dve.tensor_scalar(hot_r[:, a % RINGS], iota_r[:], row_f[:, a:a + 1], None, ALU.is_equal) \
                .then_inc(onehot, 1)
        do(dve.tensor_tensor(ex_t[:], last_tile[0:1].unsqueeze(1).to_broadcast([1, TILES, NE]),
                             iota_t[0:1].unsqueeze(2).to_broadcast([1, TILES, NE]), ALU.is_le))
        do(dve.tensor_reduce(ex_f[:], ex_t[:], AX_X, ALU.add))
        do(dve.tensor_scalar(tab["expert"][:, 0:TILES], ex_f[:], float(NE - 1), None, ALU.min))
        dve.wait_ge(tabled, CHOICES)
        do(dve.tensor_copy(named[:], pr[:, 0:2 * TILES].rearrange("p (j t) -> p j t", j=2)))
        do(dve.tensor_copy(tab["weight"][:], named[:, 1]))
        do(dve.tensor_scalar(tab["gather"][:, 0:TILES], named[:, 0], 1.0, 0.0, ALU.subtract, ALU.max))
        do(dve.tensor_scalar(empty[:], named[:, 0], 0.0, spare[:], ALU.is_equal, ALU.mult))
        do(dve.scalar_tensor_tensor(dest[:], named[:, 0], 1.0, empty[:], ALU.subtract, ALU.add))
        do(dve.tensor_copy(tab["scatter"][:], dest[:]))

    @block.tensor
    def _(pe):
        flat = chosen[:].rearrange("p c e -> p (c e)")
        pe.wait_ge(chosen_ready, 1)
        pe.matmul(pr[:, 0:CHUNKS * NE], lt[:], flat, start=True, stop=True)
        pe.matmul(pt[:, 0:CHUNKS * NE], ones[:], flat, start=True, stop=True).then_inc(counted, 1)
        pe.wait_ge(tf_ready, 1)
        pe.wait_ge(id_ready, 1)
        for a in range(CHOICES):
            pe.wait_ge(onehot, a + 1)
            pe.matmul(pr[:, 0:2 * TILES], hot_r[:, a % RINGS], hot_t[:, a].rearrange("p j t -> p (j t)"),
                      start=a == 0, stop=a == CHOICES - 1).then_inc(tabled, 1)


def experts(nc, ctx, consts, tab, w1s, w2s, b3, xf_dram, out):
    def sb(name, shape, dt=F32):
        return ctx.enter_context(nc.sbuf_tensor(name, shape, dt))

    def sem(name):
        return ctx.enter_context(nc.semaphore(name))

    def bank(name):
        return ctx.enter_context(nc.psum_tensor(name, [P, 512], F32))

    ident = consts["ident"]
    ones3 = sb("ones3", [3, P], BF16)
    scratch, scratched = sb("scratch_pool", [1, 2]), sem("scratched_pool")
    ig, isc = sb("ig", [P, UNROLL], U32), sb("isc", [P, 2], U32)
    wt = sb("wt", [P, 2])
    xg = sb("xg", [P, UNROLL, D])
    xt = sb("xt", [P, 2, DK, P])
    tg, sg, hh = sb("tg", [P, 2, HID]), sb("sg", [P, 2, HID]), sb("hh", [P, 2, HID])
    ht = sb("ht", [P, 2, FB, P])
    yw = sb("yw", [P, 2, D])
    pa_, pb_ = [bank("pha0"), bank("pha1")], [bank("phb0"), bank("phb1")]
    pxt, pht, pyy = bank("pxt"), bank("pht"), bank("pyy")

    (start, ig_ready, gathered, xt_full, xt_ready, a_full, h_full, tanh_ready, hh_ready, ht_full, ht_ready, y_full, wt_ready,
     yw_ready, is_ready, ones_ready, sg_ready) = (
        sem(n) for n in ("start", "ig_ready", "gathered_", "xt_full", "xt_ready", "e_a_full", "h_full", "tanh_ready", "hh_ready",
                         "ht_full", "ht_ready", "y_full", "wt_ready", "yw_ready", "is_ready", "ones_ready",
                         "sg_ready"))
    gathered = [sem(f"gathered{k}") for k in range(UNROLL)]
    added = sem("added")
    block = ctx.enter_context(nc.Block())
    ROUNDS = TILES // UNROLL

    @block.gpsimd
    def _(pool):
        pool.memset(scratch[:], 0.0).then_inc(scratched, 1)
        pool.wait_ge(scratched, 1)

        def gather(i, j):
            k = j % UNROLL
            pool.tensor_copy(ig[:, k:k + 1], tab["gather"][:, bass.ds(UNROLL * i + j, 1)]).then_inc(ig_ready, 1)
            pool.wait_ge(ig_ready, UNROLL * i + (j + 1))
            wait_here(pool, scratch)
            pool.indirect_dma_start(xg[:, k], None, xf_dram, bass.IndirectOffsetOnAxis(ap=ig[:, k:k + 1], axis=0)) \
                .then_inc(gathered[k], 16)

        for j in range(AHEAD):
            gather(0, j)

        def body(i, last):
            for j in range(UNROLL):
                if not last or j + AHEAD < UNROLL:
                    pool.wait_ge(xt_full, UNROLL * i + (j + 1))
                    gather(i, j + AHEAD)
                pool.tensor_copy(isc[:, j % 2:j % 2 + 1], tab["scatter"][:, bass.ds(UNROLL * i + j, 1)]) \
                    .then_inc(is_ready, 1)
                pool.wait_ge(is_ready, UNROLL * i + (j + 1))
                pool.wait_ge(yw_ready, UNROLL * i + (j + 1))
                if not (isinstance(i, int) and i == 0 and j == 0):
                    pool.wait_ge(added, 16 * UNROLL * i + 16 * j)
                wait_here(pool, scratch)
                pool.indirect_dma_start(out, bass.IndirectOffsetOnAxis(ap=isc[:, j % 2:j % 2 + 1], axis=0),
                                        yw[:, j % 2], None, compute_op=ALU.add).then_inc(added, 16)

        body(0, False)
        with pool.Fori(1, ROUNDS - 1) as i:
            body(i, False)
        body(ROUNDS - 1, True)
        pool.wait_ge(added, 16 * TILES)

    @block.scalar
    def _(act):
        def xt_copy(i, j):
            act.wait_ge(xt_full, UNROLL * i + (j + 2))
            act.activation(xt[:, j % 2].rearrange("p d t -> p (d t)"), pxt[:, 0:D], ACT.Identity) \
                .then_inc(xt_ready, 1)

        def tanh(i, j):
            act.wait_ge(a_full, UNROLL * i + (j + 1))
            act.activation(tg[:, j % 2], pa_[j % 2][:], ACT.Tanh, scale=0.5).then_inc(tanh_ready, 1)

        def ht_copy(i, j):
            act.wait_ge(ht_full, UNROLL * i + (j + 1))
            act.activation(ht[:, j % 2].rearrange("p f t -> p (f t)"), pht[:], ACT.Identity).then_inc(ht_ready, 1)

        xt_copy(0, 0)
        xt_copy(0, 1)
        tanh(0, 0)

        def body(i, last):
            for j in range(UNROLL):
                if not last or j + 2 < UNROLL:
                    xt_copy(i, j + 2)
                if not last or j + 1 < UNROLL:
                    tanh(i, j + 1)
                ht_copy(i, j)

        with act.Fori(0, ROUNDS - 1) as i:
            body(i, False)
        body(ROUNDS - 1, True)

    @block.vector
    def _(dve):
        dve.memset(ones3[:], 1.0).then_inc(ones_ready, 1)

        def swiglu(i, j):
            b = j % 2
            dve.wait_ge(tanh_ready, UNROLL * i + (j + 1))
            dve.scalar_tensor_tensor(sg[:, b], tg[:, b], 1.0, pa_[b][:], ALU.add, ALU.mult).then_inc(sg_ready, 1)
            dve.wait_ge(sg_ready, UNROLL * i + (j + 1))
            dve.wait_ge(h_full, UNROLL * i + (j + 1))
            dve.scalar_tensor_tensor(hh[:, b], sg[:, b], 0.5, pb_[b][:], ALU.mult, ALU.mult).then_inc(hh_ready, 1)

        def weigh(i, j):
            b = j % 2
            dve.tensor_copy(wt[:, b:b + 1], tab["weight"][:, bass.ds(UNROLL * i + j, 1)]).then_inc(wt_ready, 1)
            dve.wait_ge(wt_ready, UNROLL * i + (j + 1))
            dve.wait_ge(y_full, UNROLL * i + (j + 1))
            if not (isinstance(i, int) and i == 0 and j < 2):
                dve.wait_ge(added, 16 * UNROLL * i + 16 * (j - 1))
            dve.tensor_scalar(yw[:, b], pyy[:, 0:D], wt[:, b:b + 1], None, ALU.mult).then_inc(yw_ready, 1)

        swiglu(0, 0)

        def body(i, last, first=False):
            for j in range(UNROLL):
                if not last or j + 1 < UNROLL:
                    swiglu(i, j + 1)
                weigh(i, j)

        body(0, False)
        with dve.Fori(1, ROUNDS - 1) as i:
            body(i, False)
        body(ROUNDS - 1, True)

    @block.tensor
    def _(pe):
        pe.sem_inc(xt_full, 1)
        pe.wait_ge(ones_ready, 1)

        def transpose_x(i, j, guard=True):
            k = j % UNROLL
            pe.wait_ge(gathered[k], 16 * i + 16 * (j // UNROLL + 1))
            if guard:
                pe.wait_ge(xt_ready, UNROLL * i + j)
            for d in range(DK):
                ins = pe.transpose(pxt[:, d * P:(d + 1) * P], xg[:, k, d * P:(d + 1) * P], ident[:])
            ins.then_inc(xt_full, 1)

        def expert(i, j):
            return pe.value_load(tab["expert"][0:1, bass.ds(UNROLL * i + j, 1)], min_val=0, max_val=NE - 1)

        def up(i, j, half, guard=True):
            b = j % 2
            e = expert(i, j)
            if guard:
                pe.wait_ge(hh_ready, UNROLL * i + (j - 1))
            pe.wait_ge(xt_ready, UNROLL * i + (j + 1))
            dst = (pa_[b], pb_[b])[half]
            pe.matmul(dst[:], ones3[:], b3[:, bass.ds(e * EB + half * HID, HID)], start=True, stop=False)
            for d in range(DK):
                ins = pe.matmul(dst[:], xt[:, b, d],
                                w1s[:, bass.ds(e, 1), d, half * HID:(half + 1) * HID]
                                .rearrange("p a n -> p (a n)"), start=False, stop=d == DK - 1)
            ins.then_inc((a_full, h_full)[half], 1)

        def transpose_h(i, j):
            b = j % 2
            pe.wait_ge(hh_ready, UNROLL * i + (j + 1))
            if not (isinstance(i, int) and i == 0 and j == 0):
                pe.wait_ge(ht_ready, UNROLL * i + j)
            for f in range(FB):
                ins = pe.transpose(pht[:, f * P:(f + 1) * P], hh[:, b, f * P:(f + 1) * P], ident[:])
            ins.then_inc(ht_full, 1)

        def down(i, j):
            b = j % 2
            e = expert(i, j)
            if not (isinstance(i, int) and i == 0 and j == 0):
                pe.wait_ge(yw_ready, UNROLL * i + j)
            pe.matmul(pyy[:, 0:D], ones3[:], b3[:, bass.ds(e * EB + 2 * HID, D)], start=True, stop=False)
            pe.wait_ge(ht_ready, UNROLL * i + (j + 1))
            for f in range(FB):
                ins = pe.matmul(pyy[:, 0:D], ht[:, b, f], w2s[:, bass.ds(e, 1), f].rearrange("p a n -> p (a n)"),
                                start=False, stop=f == FB - 1)
            ins.then_inc(y_full, 1)

        transpose_x(0, 0, guard=False)
        up(0, 0, 0, guard=False)
        up(0, 0, 1, guard=False)
        transpose_x(0, 1)

        def body(i, last):
            for j in range(UNROLL):
                if not last or j + 2 < UNROLL:
                    transpose_x(i, j + 2)
                more, guard = not last or j + 1 < UNROLL, not (isinstance(i, int) and i == 0 and j == 0)
                if more:
                    up(i, j + 1, 0, guard)
                transpose_h(i, j)
                if more:
                    up(i, j + 1, 1, guard)
                down(i, j)

        body(0, False)
        with pe.Fori(1, ROUNDS - 1) as i:
            body(i, False)
        body(ROUNDS - 1, True)


def kernel(**inputs):
    import numpy as np
    import concourse.bacc as bacc
    from concourse.bass_utils import run_bass_kernel_spmd

    def arr(name):
        return np.asarray(inputs["L0_" + name])

    def blocks(w):
        return w.reshape(-1, P, w.shape[-1]).transpose(1, 0, 2)

    b_in, w_in = arr("attn_b_in"), arr("attn_W_in")
    n_b = 2 * INNER
    w_in = np.concatenate([w_in[:, :n_b], w_in[:, n_b + STATE:n_b + 2 * STATE], w_in[:, n_b:n_b + STATE],
                           w_in[:, n_b + 2 * STATE:]], axis=1)
    laid = {
        "x": arr("attn_input_tensor").reshape(TOKENS, D),
        "win": blocks(w_in), "wout": blocks(arr("attn_W_out")),
        "gam": arr("attn_ln_gamma").reshape(DK, P).T, "bet": arr("attn_ln_beta").reshape(DK, P).T,
        "bz": b_in[:INNER].reshape(FB, P).T,
        "bcb": np.concatenate([b_in[n_b + STATE:n_b + 2 * STATE], b_in[n_b:n_b + STATE]]).reshape(2 * STATE, 1),
        "bx": b_in[INNER:n_b].reshape(1, INNER),
        "bdt": np.concatenate([b_in[n_b:n_b + STATE], b_in[PROJ - HEADS:]]).reshape(1, -1),
        "alog": arr("attn_A_log").reshape(1, HEADS), "dskip": arr("attn_D_skip").reshape(1, HEADS),
        "dtb": arr("attn_dt_bias").reshape(1, HEADS), "bout": arr("attn_b_out").reshape(1, D),
        "wr": blocks(arr("ffn_Wr").T), "br": arr("ffn_br").reshape(1, NE), "bn": arr("ffn_biases_N").reshape(1, NE),
        "w1": arr("ffn_Wl1").reshape(NE, DK, P, 2 * HID).transpose(2, 0, 1, 3),
        "w2": arr("ffn_Wl2").reshape(NE, FB, P, D).transpose(2, 0, 1, 3),
        "eb": np.concatenate([arr("ffn_bl1"), arr("ffn_bl2")], axis=1).reshape(P, NE * EB // P),
    }
    laid = {k: np.ascontiguousarray(v) for k, v in laid.items()}
    nc = bacc.Bacc("TRN2", target_bir_lowering=False, num_devices=1)
    aps = {k: nc.dram_tensor("in_" + k, v.shape, mybir.dt.from_np(v.dtype), kind="ExternalInput").ap()
           for k, v in laid.items()}
    out = nc.dram_tensor("out_rows", (TOKENS + P, D), F32, kind="ExternalOutput").ap()
    build(nc, out=out, **aps)
    r = run_bass_kernel_spmd(nc, [{"in_" + k: v for k, v in laid.items()}], core_ids=[0])
    return r.results[0]["out_rows"][:TOKENS].reshape(BATCH, SEQ, D)
```

```python
from contextlib import ExitStack

import concourse.bass as bass
from concourse import mybir

ALU = mybir.AluOpType
ACT = mybir.ActivationFunctionType
F32 = mybir.dt.float32
F32R = mybir.dt.float32r
BF16 = mybir.dt.bfloat16
F16 = mybir.dt.float16
I32 = mybir.dt.int32
U32 = mybir.dt.uint32
AX_X = mybir.AxisListType.X

P = 128
D = 256
DK = D // P
INNER = 512
FB = INNER // P
HEADS = 8
HD = INNER // HEADS
STATE = 64
PROJ = 2 * INNER + 2 * STATE + HEADS
BATCH, SEQ = 4, 1024
TOKENS = BATCH * SEQ
CHUNKS = TOKENS // P
CPS = SEQ // P
GC = 4
GT_ = GC * P
EPS = 1e-5
NE = 8
HID = 512
TOPK = 2
CHOICES = TOPK * CHUNKS
TILES = (TOPK * TOKENS + NE * (P - 1)) // P + 1
EW1 = DK * 2 * HID
EW = EW1 + FB * D
PIECE = EW // 2
PIECES = NE * EW // PIECE
RAWS = 3
LOW = 64.0
UNROLL = 8
AHEAD = 4
TPAD = TILES + AHEAD + 1
GROUP_PRODUCTS = ["u0", "u1", "bd", "cb", "z0", "cum", "z1", "z2", "z3"]
RING = len(GROUP_PRODUCTS)


class Steps:

    def __init__(self, eng, sem, base=0, per_round=0, r=0):
        self.eng, self.sem, self.base, self.per_round, self.r, self.n = eng, sem, base, per_round, r, 0

    def did(self, ins):
        self.n += 1
        ins.then_inc(self.sem, 1)
        return self.n

    def wait(self, n=None):
        n = self.n if n is None else n
        self.eng.wait_ge(self.sem, self.per_round * self.r + (self.base + n) if self.per_round else self.base + n)

    def link(self, ins):
        self.wait(self.did(ins))


def wait_here(eng, scratch):
    eng.tensor_tensor(scratch[:, 0:1], scratch[:, 1:2], scratch[:, 1:2], ALU.add)


def split_matmul(pe, dst, lhs, rhs, start, stop):
    pe.matmul(dst, lhs[1], rhs[0], start=start, stop=False)
    pe.matmul(dst, lhs[0], rhs[1], start=False, stop=False)
    return pe.matmul(dst, lhs[0], rhs[0], start=False, stop=stop)


def build(nc, x, win, wout, gam, bet, bz, bcb, bx, bdt, alog, dskip, dtb, bout, wr, br, bn, we, b1, b2, out):
    xf_dram = nc.dram_tensor("xf_dram", (TOKENS, D), F32, kind="Internal").ap()
    with ExitStack() as ctx:
        def sb(name, shape, dt=F32, c=ctx):
            return c.enter_context(nc.sbuf_tensor(name, shape, dt))

        squares = sb("squares", [P, 4 * P])
        consts = {"ident": sb("ident", [P, P]), "half": sb("half", [P, 8]), "squares": squares}
        consts.update({name: squares[:, k * P:(k + 1) * P] for k, name in enumerate(("le", "gt", "lt", "ones"))})
        scores = sb("scores", [P, CHUNKS, NE])
        router_rows = brs, bns, ebs = sb("brs", [P, NE]), sb("bns", [P, NE]), sb("ebs", [P, NE * D // P])
        with ExitStack() as c:
            mamba(nc, c, consts, scores, router_rows, br, bn, b2, xf_dram, x, win, wout, gam, bet, bz, bcb, bx,
                  bdt, alog, dskip, dtb, bout, wr, out)
        wh, wl = sb("wh", [P, NE * EW], F32R), sb("wl", [P, NE * EW], F16)
        rows = sb("rows", [P, NE * 2 * HID])
        rows_in = ctx.enter_context(nc.semaphore("rows_in"))
        b3 = sb("b3", [3, NE * D], BF16)
        tab = {
            "gather": sb("gather", [P, TPAD], U32), "scatter": sb("scatter", [P, TILES], U32),
            "weight": sb("weight", [P, TILES]), "expert": sb("expert", [1, TPAD], I32),
        }
        with ExitStack() as c:
            route(nc, c, consts, scores, router_rows, tab, wh, wl, rows, rows_in, b3, we, b1)
        with ExitStack() as c:
            experts(nc, c, consts, tab, wh, wl, rows, rows_in, b3, xf_dram, out)


def mamba(nc, ctx, consts, scores, router_rows, br, bn, b2, xf_dram, x, win, wout, gam, bet, bz, bcb, bx, bdt, alog,
          dskip, dtb, bout, wr, out):
    def sb(name, shape, dt=F32):
        return ctx.enter_context(nc.sbuf_tensor(name, shape, dt))

    def sem(name):
        return ctx.enter_context(nc.semaphore(name))

    def bank(name):
        return ctx.enter_context(nc.psum_tensor(name, [P, 512], F32))

    ident, le, gt, lt, ones, half = (consts[k] for k in ("ident", "le", "gt", "lt", "ones", "half"))
    winp = [sb(f"win_{n}", [P, DK, PROJ], F32R) for n in ("high", "low")]
    wouts = sb("wouts", [P, FB, D])
    win_bd = sb("win_bd", [P, DK, STATE + HEADS])
    gtr = sb("gtr", [P, P], F32R)
    wrs = sb("wrs", [P, DK, NE])
    gams, bets = sb("gams", [P, DK]), sb("bets", [P, DK])
    bzs, bzh = sb("bzs", [P, FB]), sb("bzh", [P, FB])
    bcbs = sb("bcbs", [2 * STATE, 1])
    bxs = sb("bxs", [P, INNER])
    bdts, dtbs = sb("bdts", [P, STATE + HEADS]), sb("dtbs", [P, HEADS])
    alogs, nega, dsk = sb("alogs", [P, HEADS]), sb("nega", [P, HEADS]), sb("dsk", [P, HEADS])
    bouts = sb("bouts", [P, D])
    scratch, scratched = sb("scratch", [1, 2]), sem("scratched")
    xi, xr = sb("xi", [P, 2, GC, D]), sb("xr", [P, 2, GC, D])
    x1, u0 = sb("x1", [P, GC, D]), sb("u0", [P, GC, D])
    st = sb("st", [P, GC, 6])
    mv1, mv2 = sb("mv1", [P, GC, 2]), sb("mv2", [P, GC, 2])
    ve1, ve2, rs1, rs2 = (sb(n, [P, GC]) for n in ("ve1", "ve2", "rs1", "rs2"))
    ut = sb("ut", [P, DK, GT_])
    utp = [sb(f"ut_{n}", [P, 2, DK, GT_], F32R) for n in ("high", "low")]
    zh, th = sb("zh", [P, 2, GT_]), sb("th", [P, 2, GT_])
    sil = sb("sil", [P, 2, FB, GT_])
    bt, ct = sb("bt", [STATE, 2, GT_]), sb("ct", [STATE, 2, GT_])
    bd = sb("bd", [P, 2, GC, STATE + HEADS])
    spa, spe, spl, spr = (sb(n, [P, GC, HEADS]) for n in ("spa", "spe", "spl", "spr"))
    dt, aa = sb("dt", [P, 2, GC, HEADS]), sb("aa", [P, 2, GC, HEADS])
    aap = [sb(f"aa_{n}", [P, 2, GC, HEADS], F32R) for n in ("high", "low")]
    ex = sb("ex", [P, 2, 3, GC, HEADS])
    xs, dtx, wx, dxs, y = (sb(n, [P, 2, INNER]) for n in ("xs", "dtx", "wx", "dxs", "y"))
    ya = sb("ya", [P, INNER])
    gT = sb("gT", [P, 2, INNER])
    segr = [sb(f"segr_{n}", [P, HEADS, P], F32R) for n in ("high", "low")]
    lm = sb("lm", [P, 2, HEADS, P])
    gm = sb("gm", [P, 2, P])
    hst = sb("hst", [STATE, 2, INNER])
    xp, xf, xft = sb("xp", [P, 2, D]), sb("xf", [P, 2, D]), sb("xft", [P, 2, DK, P])
    st3, mv3, ve3, rs3 = sb("st3", [P, 6]), sb("mv3", [P, 2]), sb("ve3", [P, 1]), sb("rs3", [P, 1])

    pa = [bank("pa0"), bank("pa1")]
    ps = [bank("ps0"), bank("ps1")]
    px, pg, py, po = bank("px"), bank("pg"), bank("py"), bank("po")

    raw = sil[:].rearrange("p a f t -> p (a f t)")
    win_raw = raw[:, 0:DK * PROJ].rearrange("p (d n) -> p d n", d=DK)

    c_const, c_load, c_rows, masks = sem("c_const"), sem("c_load"), sem("c_rows"), sem("masks")
    cleared, nega_ready, high_ready, parts_ready, ul_ready = (
        sem(n) for n in ("cleared", "nega_ready", "high_ready", "parts_ready", "ul_ready"))
    x_in, xp_stored, xf_stored = ([sem(f"{n}{k}") for k in range(2)] for n in ("x_in", "xp_stored", "xf_stored"))
    stats1, rstd1, x1_ready, xr_ready, stats2, rstd2, u0_ready = (
        sem(n) for n in ("stats1", "rstd1", "x1_ready", "xr_ready", "stats2", "rstd2", "u0_ready"))
    a_full, a_free, bd_ready, sp_ready, a_ready, sil_ready = (
        sem(n) for n in ("a_full", "a_free", "bd_ready", "sp_ready", "a_ready", "sil_ready"))
    segr_ready, seg_full, l_ready, g_full, gm_ready, m_ready = (
        sem(n) for n in ("segr_ready", "seg_full", "l_ready", "g_full", "gm_ready", "m_ready"))
    x_full, xs_ready, dtx_ready, wx_ready, dxs_ready = (
        sem(n) for n in ("x_full", "xs_ready", "dtx_ready", "wx_ready", "dxs_ready"))
    n_full, st_ready, yi_full, ye_full, y_ready, yt_full, gate_ready, o_full, xp_ready = (
        sem(n) for n in ("n_full", "st_ready", "yi_full", "ye_full", "y_ready", "yt_full", "gate_ready", "o_full",
                         "xp_ready"))
    stats3, rstd3, xf_ready, xft_full, xft_ready, sc_full, sc_ready = (
        sem(n) for n in ("stats3", "rstd3", "xf_ready", "xft_full", "xft_ready", "sc_full", "sc_ready"))
    dve_did, act_did, pool_did = sem("dve_did"), sem("act_did"), sem("pool_did")

    xg_dram = x.rearrange("(g c p) d -> g p c d", p=P, c=GC)
    zero_rows = out[TOKENS:TOKENS + P, :]
    NLOADS = 14

    def par(c):
        return c % 2

    def gpar(c):
        return (c // GC) % 2, c % GC

    def cnt(s, c):
        return s * CPS + (c + 1)

    def gcnt(s, g, per=1):
        return s * (2 * per) + per * (g + 1)

    def states(s, n):
        return s * (CPS - 1) + (n // CPS) * (CPS - 1) + (n % CPS + 1)

    FIRST, ROUND = range(2), range(2, CPS + 2)

    def here(n, end):
        return 0 <= n and not (end and n >= CPS)

    def group_here(g, end):
        return not (end and g >= 2)

    block = ctx.enter_context(nc.Block())

    @block.sync
    def _(sp):
        def load_x(g_dram, half_):
            sp.dma_start(xi[:, half_], g_dram).then_inc(x_in[half_], 16)

        def row(a):
            return a.partition_broadcast(P)

        load_x(xg_dram[0], 0)
        for dst, src in ((gams[:], gam), (bets[:], bet), (win_raw, win), (bzs[:], bz), (bcbs[:], bcb),
                         (bdts[:], row(bdt[0])), (dtbs[:], row(dtb[0])), (bxs[:], row(bx[0])),
                         (alogs[:], row(alog[0])), (dsk[:], row(dskip[0])), (bouts[:], row(bout[0])),
                         (wrs[:], wr), (wouts[:], wout), (win_bd[:], win[:, :, PROJ - STATE - HEADS:])):
            sp.dma_start(dst, src).then_inc(c_load, 16)
        load_x(xg_dram[1], 1)
        for dst, src in zip(router_rows, (row(br[0]), row(bn[0]), b2)):
            sp.dma_start(dst[:], src).then_inc(c_rows, 16)
        sp.wait_ge(cleared, 1)
        sp.dma_start(zero_rows, wx[:, 0, 0:D]).then_inc(c_const, 16)

        def body(s, last):
            for c in range(CPS + 2):
                if c % GC == 0 and c < CPS and not last:
                    g = c // GC
                    sp.wait_ge(xr_ready, gcnt(s, g))
                    load_x(xg_dram[bass.ds(2 * s + (g + 2), 1)].rearrange("a p c d -> (a p) c d"), g)
                if 1 <= c <= CPS:
                    n = c - 1
                    sp.wait_ge(xp_ready, cnt(s, n))
                    sp.dma_start(out[bass.ds(s * SEQ + n * P, P), :], xp[:, par(n)]) \
                        .then_inc(xp_stored[par(n)], 16)
                    sp.wait_ge(xf_ready, cnt(s, n))
                    sp.dma_start(xf_dram[bass.ds(s * SEQ + n * P, P), :], xf[:, par(n)]) \
                        .then_inc(xf_stored[par(n)], 16)

        with sp.Fori(0, BATCH - 1) as s:
            body(s, False)
        body(BATCH - 1, True)
        for k in range(2):
            sp.wait_ge(xp_stored[k], 16 * (CHUNKS // 2 + 1))
            sp.wait_ge(xf_stored[k], 16 * (CHUNKS // 2 + 1))
        sp.wait_ge(c_const, 16)
        sp.wait_ge(c_rows, 16 * 3)

    @block.gpsimd
    def _(pool):
        steps0 = Steps(pool, masks)
        pool.memset(wx[:, 0, 0:D], 0.0).then_inc(cleared, 1)
        for t, v in ((ident, 0.0), (le, 1.0), (gt, 1.0), (lt, 1.0), (ones, 1.0), (half, -0.5)):
            steps0.did(pool.memset(t[:], v))
        steps0.wait()
        for t, op, base, mult, step, fill in ((ident, ALU.not_equal, 0, 1, -1, 1.0), (le, ALU.is_ge, 0, -1, 1, 0.0),
                                              (gt, ALU.is_gt, 0, 1, -1, 0.0), (lt, ALU.is_gt, 0, -1, 1, 0.0)):
            steps0.did(pool.affine_select(out=t[:], in_=t[:], compare_op=op, fill=fill, base=base,
                                          pattern=[[step, P]], channel_multiplier=mult))
        steps0.wait()

        def rstd(dst, src, n, ready, value, done):
            pool.wait_ge(ready, value)
            pool.tensor_tensor(dst, src, half[:, 0:n], ALU.pow).then_inc(done, 1)

        def residual(s, g, steps, a, b):
            h = g % 2
            pool.wait_ge(x1_ready, gcnt(s, g))
            steps.link(pool.tensor_tensor(xr[:, h, a:b], xi[:, h, a:b], x1[:, a:b], ALU.add))
            ins = pool.tensor_tensor(xr[:, h, a:b], xr[:, h, a:b],
                                     bouts[:].unsqueeze(1).to_broadcast([P, b - a, D]), ALU.add)
            if b == GC:
                ins.then_inc(xr_ready, 1)

        def segment(s, n):
            h, k = gpar(n)
            pool.wait_ge(a_ready, gcnt(s, n // GC))
            if n:
                pool.wait_ge(seg_full, cnt(s, n - 1))
            for part in range(2):
                ins = pool.tensor_tensor(segr[part][:], le[:].unsqueeze(1).to_broadcast([P, HEADS, P]),
                                         aap[part][:, h, k].bitcast(F32).unsqueeze(2).to_broadcast([P, HEADS, P]),
                                         ALU.mult)
            ins.then_inc(segr_ready, 1)

        def heads(t):
            return t.rearrange("p (h d) -> p h d", h=HEADS)

        def per_head(t):
            return t.unsqueeze(2).to_broadcast([P, HEADS, HD])

        def scaled(s, n):
            h, k = gpar(n)
            pool.wait_ge(xs_ready, cnt(s, n))
            pool.tensor_tensor(heads(dtx[:, par(n)]), heads(xs[:, par(n)]), per_head(dt[:, h, k]), ALU.mult) \
                .then_inc(dtx_ready, 1)
            pool.tensor_tensor(heads(dxs[:, par(n)]), heads(xs[:, par(n)]), per_head(dsk[:]), ALU.mult) \
                .then_inc(dxs_ready, 1)
            pool.wait_ge(a_free, gcnt(s, n // GC - 1, RING) + (GROUP_PRODUCTS.index("cum") + 3))
            pool.wait_ge(dtx_ready, cnt(s, n))
            pool.tensor_tensor(heads(wx[:, par(n)]), heads(dtx[:, par(n)]), per_head(ex[:, h, 1, k]), ALU.mult) \
                .then_inc(wx_ready, 1)

        POOL_LINKS = 4
        steps = Steps(pool, pool_did)
        rstd(rs1[:], ve1[:], GC, stats1, 1, rstd1)
        rstd(rs2[:], ve2[:], GC, stats2, 1, rstd2)
        pool.wait_ge(c_load, 16 * NLOADS)
        residual(0, 0, steps, 0, GC)
        rstd(rs1[:], ve1[:], GC, stats1, 2, rstd1)
        rstd(rs2[:], ve2[:], GC, stats2, 2, rstd2)
        segment(0, 0)
        pool.wait_ge(c_const, 16)
        scaled(0, 0)
        segment(0, 1)

        def step(s, c, end, steps):
            k, g = c % GC, c // GC + 1
            if here(c + 1, end):
                scaled(s, c + 1)
            if here(c - 1, end):
                rstd(rs3[:], ve3[:], 1, stats3, cnt(s, c - 1), rstd3)
            if here(c + 2, end):
                segment(s, c + 2)
            if k == 3 and group_here(g + 1, end):
                rstd(rs2[:], ve2[:], GC, stats2, gcnt(s, g + 1), rstd2)
            if k in (1, 2) and group_here(g, end):
                residual(s, g, steps, 2 * (k - 1), 2 * k)
            if k == 2 and group_here(g + 1, end):
                rstd(rs1[:], ve1[:], GC, stats1, gcnt(s, g + 1), rstd1)

        for c in FIRST:
            step(0, c, False, steps)
        base = steps.n
        with pool.Fori(0, BATCH - 1) as s:
            steps = Steps(pool, pool_did, base=base, per_round=POOL_LINKS, r=s)
            for c in ROUND:
                step(s, c, False, steps)
            assert steps.n == POOL_LINKS
        steps = Steps(pool, pool_did, base=base, per_round=POOL_LINKS, r=BATCH - 1)
        for c in ROUND:
            step(BATCH - 1, c, True, steps)

    @block.scalar
    def _(act):
        act.sem_inc(a_free, 2)
        act.sem_inc(xft_ready, 1)
        act.sem_inc(sc_ready, 1)
        for k in range(2):
            act.sem_inc(xp_stored[k], 16)
            act.sem_inc(xf_stored[k], 16)
        act.wait_ge(c_load, 16 * NLOADS)
        act.mul(bzh[:], bzs[:], 0.5).then_inc(act_did, 1)
        act.activation(nega[:], alogs[:], ACT.Exp).then_inc(nega_ready, 1)
        act.wait_ge(act_did, 1)
        act.activation(winp[0][:], win_raw, ACT.Identity).then_inc(high_ready, 1)
        act.wait_ge(masks, 10)
        act.activation(gtr[:], gt[:], ACT.Identity).then_inc(high_ready, 1)

        def group(s, g, parts):
            h = g % 2
            for k, what in enumerate(GROUP_PRODUCTS):
                if what not in parts:
                    continue
                src = pa[k % 2]
                if what != "bd":
                    act.wait_ge(a_full, gcnt(s, g - 1, RING) + (k + 1))
                if what in ("u0", "u1"):
                    d = int(what[1])
                    act.activation(ut[:, d], src[:], ACT.Identity, bias=bets[:, d:d + 1],
                                   scale=gams[:, d:d + 1])
                    act.activation(utp[0][:, h, d], src[:], ACT.Identity, bias=bets[:, d:d + 1],
                                   scale=gams[:, d:d + 1]).then_inc(a_free, 1)
                elif what == "bd":
                    act.wait_ge(bd_ready, gcnt(s, g))
                    act.activation(spa[:], bd[:, h, :, STATE:], ACT.Abs).then_inc(act_did, 1)
                    act.activation(spr[:], bd[:, h, :, STATE:], ACT.Relu).then_inc(a_free, 1)
                    act.wait_ge(act_did, gcnt(s, g - 1, 2) + 2)
                    act.activation(spe[:], spa[:], ACT.Exp, scale=-1.0).then_inc(act_did, 1)
                    act.wait_ge(act_did, gcnt(s, g - 1, 2) + 3)
                    act.activation(spl[:], spe[:], ACT.Ln, bias=1.0).then_inc(sp_ready, 1)
                elif what == "cb":
                    act.activation(ct[:, h], src[0:STATE, :], ACT.Identity, bias=bcbs[0:STATE])
                    act.activation(bt[:, h], src[STATE:2 * STATE, :], ACT.Identity, bias=bcbs[STATE:2 * STATE]) \
                        .then_inc(a_free, 1)
                elif what == "cum":
                    act.activation(ex[:, h].rearrange("p a c n -> p (a c n)"), src[:, 0:3 * GC * HEADS], ACT.Exp) \
                        .then_inc(a_free, 1)
                else:
                    f = int(what[1])
                    act.wait_ge(sil_ready, gcnt(s, g - 1, FB) + (f + 1))
                    act.activation(zh[:, f % 2], src[:], ACT.Identity, bias=bzh[:, f:f + 1], scale=0.5)
                    act.activation(th[:, f % 2], src[:], ACT.Tanh, bias=bzh[:, f:f + 1], scale=0.5) \
                        .then_inc(a_free, 1)

        def decay(s, n):
            act.wait_ge(seg_full, cnt(s, n))
            act.activation(lm[:, par(n), 0:4], ps[0][:].rearrange("p (h i) -> p h i", h=4), ACT.Exp)
            act.activation(lm[:, par(n), 4:8], ps[1][:].rearrange("p (h i) -> p h i", h=4), ACT.Exp) \
                .then_inc(l_ready, 1)

        def turned(s, n):
            act.wait_ge(xft_full, cnt(s, n))
            act.activation(xft[:, par(n)].rearrange("p d t -> p (d t)"), ps[0][:, 0:D], ACT.Identity) \
                .then_inc(xft_ready, 1)

        def score(s, n):
            act.wait_ge(sc_full, cnt(s, n))
            act.activation(scores[:, bass.ds(s * CPS + n, 1)], ps[1][:, 0:NE].unsqueeze(1), ACT.Identity) \
                .then_inc(sc_ready, 1)

        group(0, 0, GROUP_PRODUCTS)
        decay(0, 0)

        def step(s, c, end):
            k, g = c % GC, c // GC + 1

            def place(name):
                if group_here(g, end):
                    group(s, g, [what for what in PLACES[k].get(name, ()) if what != "bd"])

            place("first")
            if here(c + 1, end):
                decay(s, c + 1)
            place("a")
            if here(c - 2, end):
                turned(s, c - 2)
            place("b")
            if here(c - 2, end):
                score(s, c - 2)
            if k == 1 and group_here(g, end):
                group(s, g, ["bd"])
            place("c")

        for c in FIRST:
            step(0, c, False)
        with act.Fori(0, BATCH - 1) as s:
            for c in ROUND:
                step(s, c, False)
        for c in ROUND:
            step(BATCH - 1, c, True)

    @block.vector
    def _(dve):
        dve.memset(scratch[:], 0.0).then_inc(scratched, 1)
        dve.wait_ge(scratched, 1)
        dve.sem_inc(sil_ready, 2)

        def stats(src, ve, mv, steps, done):
            n = [steps.did(dve.bn_stats(st[:, k], src[:, k])) for k in range(GC)]
            steps.wait(n[-1])
            wait_here(dve, scratch)
            for k in range(GC):
                m = steps.did(dve.bn_aggr(mv[:, k], st[:, k]))
            steps.wait(m)
            dve.tensor_scalar(ve[:], mv[:, :, 1], EPS, None, ALU.add).then_inc(done, 1)

        def normalise(dst, src, mv, rs, done):
            for k in range(GC):
                ins = dve.tensor_scalar(dst[:, k], src[:, k], mv[:, k, 0:1], rs[:, k:k + 1], ALU.subtract, ALU.mult)
            ins.then_inc(done, 1)

        def first_stats(s, g, steps):
            dve.wait_ge(x_in[g % 2], 16 * s + 16 * (g // 2 + 1))
            stats(xi[:, g % 2], ve1, mv1, steps, stats1)

        def first_norm(s, g, steps):
            dve.wait_ge(rstd1, gcnt(s, g))
            if not (isinstance(s, int) and 2 * s + g == 0):
                dve.wait_ge(xr_ready, gcnt(s, g - 1))
            normalise(x1, xi[:, g % 2], mv1, rs1, x1_ready)
            dve.wait_ge(x1_ready, gcnt(s, g))
            stats(x1, ve2, mv2, steps, stats2)

        def second_norm(s, g):
            dve.wait_ge(rstd2, gcnt(s, g))
            if not (isinstance(s, int) and 2 * s + g == 0):
                dve.wait_ge(a_full, gcnt(s, g - 2, RING) + 2)
            normalise(u0, x1, mv2, rs2, u0_ready)

        def low_u(s, g):
            for d in range(DK):
                dve.wait_ge(a_free, gcnt(s, g - 1, RING) + (d + 3))
                dve.tensor_tensor(utp[1][:, g % 2, d], ut[:, d], utp[0][:, g % 2, d].bitcast(F32), ALU.subtract) \
                    .then_inc(ul_ready, 1)

        def steps_dt(s, g, steps):
            h = g % 2
            dve.wait_ge(sp_ready, gcnt(s, g))
            steps.link(dve.tensor_tensor(dt[:, h], spr[:], spl[:], ALU.add))
            steps.link(dve.scalar_tensor_tensor(aa[:, h], dt[:, h], -1.0,
                                                nega[:].unsqueeze(1).to_broadcast([P, GC, HEADS]), ALU.mult, ALU.mult))
            steps.link(dve.tensor_copy(aap[0][:, h], aa[:, h]))
            dve.tensor_tensor(aap[1][:, h], aa[:, h], aap[0][:, h].bitcast(F32), ALU.subtract).then_inc(a_ready, 1)

        def by_token(s, g):
            n = GC * (STATE + HEADS)
            dve.wait_ge(a_full, gcnt(s, g - 1, RING) + (GROUP_PRODUCTS.index("bd") + 1))
            dve.tensor_tensor(bd[:, g % 2], pa[0][:, 0:n].rearrange("p (c n) -> p c n", c=GC),
                              bdts[:].unsqueeze(1).to_broadcast([P, GC, STATE + HEADS]), ALU.add).then_inc(bd_ready, 1)

        def silu(s, g, f):
            dve.wait_ge(a_free, gcnt(s, g - 1, RING) + (GROUP_PRODUCTS.index(f"z{f}") + 3))
            dve.scalar_tensor_tensor(sil[:, g % 2, f], th[:, f % 2], 1.0, zh[:, f % 2], ALU.add, ALU.mult) \
                .then_inc(sil_ready, 1)

        def inner_x(s, n):
            dve.wait_ge(x_full, cnt(s, n))
            dve.tensor_tensor(xs[:, par(n)], px[:], bxs[:], ALU.add).then_inc(xs_ready, 1)

        def masked(s, n):
            dve.wait_ge(g_full, cnt(s, n))
            dve.tensor_tensor(gm[:, par(n)], pg[:, 0:P], le[:], ALU.mult).then_inc(gm_ready, 1)

        def mixing(s, n):
            dve.wait_ge(gm_ready, cnt(s, n))
            dve.wait_ge(l_ready, cnt(s, n))
            dve.tensor_tensor(lm[:, par(n)], lm[:, par(n)],
                              gm[:, par(n)].unsqueeze(1).to_broadcast([P, HEADS, P]), ALU.mult).then_inc(m_ready, 1)

        def state(s, n, steps):
            h, k = gpar(n)
            dve.wait_ge(n_full, states(s, n))
            if n % CPS == 0:
                dve.tensor_copy(hst[:, 1], pg[0:STATE, :]).then_inc(st_ready, 1)
                return
            new = hst[:, par(n + 1)]
            dve.wait_ge(st_ready, states(s, n - 1))
            steps.link(dve.tensor_tensor(new.rearrange("p (h d) -> p h d", h=HEADS),
                                         hst[:, par(n)].rearrange("p (h d) -> p h d", h=HEADS),
                                         ex[0:STATE, h, 2, k].unsqueeze(2).to_broadcast([STATE, HEADS, HD]), ALU.mult))
            dve.tensor_tensor(new, new, pg[0:STATE, :], ALU.add).then_inc(st_ready, 1)

        def gate(s, n):
            h, k = gpar(n)
            dve.wait_ge(yt_full, cnt(s, n))
            dve.wait_ge(sil_ready, gcnt(s, n // GC, FB) + 2)
            dve.tensor_tensor(gT[:, par(n)].rearrange("p (f t) -> p f t", f=FB),
                              py[:].rearrange("p (f t) -> p f t", f=FB), sil[:, h, :, k * P:(k + 1) * P], ALU.mult) \
                .then_inc(gate_ready, 1)

        def residual(s, n, steps):
            h, k = gpar(n)
            dve.wait_ge(o_full, cnt(s, n))
            dve.wait_ge(xp_stored[par(n)], s * (8 * CPS) + 16 * (n // 2 + 1))
            dve.tensor_tensor(xp[:, par(n)], po[:, 0:D], xr[:, h, k], ALU.add).then_inc(xp_ready, 1)
            dve.wait_ge(xp_ready, cnt(s, n))
            a = steps.did(dve.bn_stats(st3[:], xp[:, par(n)]))
            steps.wait(a)
            wait_here(dve, scratch)
            steps.link(dve.bn_aggr(mv3[:], st3[:]))
            dve.tensor_scalar(ve3[:], mv3[:, 1:2], EPS, None, ALU.add).then_inc(stats3, 1)

        def last_norm(s, n):
            dve.wait_ge(rstd3, cnt(s, n))
            dve.wait_ge(xf_stored[par(n)], s * (8 * CPS) + 16 * (n // 2 + 1))
            dve.tensor_scalar(xf[:, par(n)], xp[:, par(n)], mv3[:, 0:1], rs3[:], ALU.subtract, ALU.mult) \
                .then_inc(xf_ready, 1)

        def output(s, n, steps):
            h, k = gpar(n)
            dve.wait_ge(yi_full, cnt(s, n))
            dve.wait_ge(dxs_ready, cnt(s, n))
            yy = y[:, par(n)]
            if n % CPS:
                steps.did(dve.tensor_tensor(yy, py[:], dxs[:, par(n)], ALU.add))
                dve.wait_ge(ye_full, states(s, n - 1))
                steps.link(dve.tensor_tensor(ya[:].rearrange("p (h d) -> p h d", h=HEADS),
                                             po[:].rearrange("p (h d) -> p h d", h=HEADS),
                                             ex[:, h, 0, k].unsqueeze(2).to_broadcast([P, HEADS, HD]), ALU.mult))
                dve.tensor_tensor(yy, yy, ya[:], ALU.add).then_inc(y_ready, 1)
            else:
                dve.tensor_tensor(yy, py[:], dxs[:, par(n)], ALU.add).then_inc(y_ready, 1)

        steps = Steps(dve, dve_did)
        first_stats(0, 0, steps)
        first_norm(0, 0, steps)
        second_norm(0, 0)
        dve.wait_ge(nega_ready, 1)
        dve.wait_ge(masks, 10)
        dve.wait_ge(high_ready, 1)
        dve.tensor_tensor(winp[1][:], win_raw, winp[0][:].bitcast(F32), ALU.subtract).then_inc(parts_ready, 1)
        dve.wait_ge(parts_ready, 1)
        steps.link(dve.tensor_tensor(bdts[:, STATE:], bdts[:, STATE:], dtbs[:], ALU.add))
        low_u(0, 0)
        by_token(0, 0)
        first_stats(0, 1, steps)
        steps_dt(0, 0, steps)
        first_norm(0, 1, steps)
        silu(0, 0, 0)
        for f in range(1, FB):
            silu(0, 0, f)
        inner_x(0, 0)
        masked(0, 0)
        mixing(0, 0)

        def step(s, c, end, steps):
            k, g = c % GC, c // GC + 1
            if here(c, end):
                output(s, c, steps)
                if c % CPS != CPS - 1:
                    state(s, c, steps)
            if here(c + 1, end):
                inner_x(s, c + 1)
            if here(c, end):
                if k == 0 and c:
                    silu(s, g - 1, 2)
                    silu(s, g - 1, 3)
                gate(s, c)
            if here(c + 1, end):
                masked(s, c + 1)
                mixing(s, c + 1)
            if here(c - 1, end):
                residual(s, c - 1, steps)
            if k == 1 and group_here(g, end):
                by_token(s, g)
                low_u(s, g)
            if k == 2 and group_here(g, end):
                steps_dt(s, g, steps)
            if k == 3 and group_here(g + 1, end):
                first_norm(s, g + 1, steps)
            if here(c - 1, end):
                last_norm(s, c - 1)
            if k == 2 and group_here(g + 1, end):
                first_stats(s, g + 1, steps)
            if k == 0 and group_here(g, end):
                second_norm(s, g)
            if k == 2 and group_here(g, end):
                silu(s, g, 0)
            if k == 3 and group_here(g, end):
                silu(s, g, 1)

        for c in FIRST:
            step(0, c, False, steps)
        base = steps.n
        DVE_STEPS = 2 * (4 * GC + 3) + (CPS - 2) + 2 * CPS + 2 * (CPS - 1)
        with dve.Fori(0, BATCH - 1) as s:
            steps = Steps(dve, dve_did, base=base, per_round=DVE_STEPS, r=s)
            for c in ROUND:
                step(s, c, False, steps)
            assert steps.n == DVE_STEPS
        steps = Steps(dve, dve_did, base=base, per_round=DVE_STEPS, r=BATCH - 1)
        for c in ROUND:
            step(BATCH - 1, c, True, steps)

    @block.tensor
    def _(pe):
        pe.wait_ge(masks, 10)

        def group(s, g, parts):
            h = g % 2
            for k, what in enumerate(GROUP_PRODUCTS):
                if what not in parts:
                    continue
                dst = pa[k % 2]
                pe.wait_ge(a_free, gcnt(s, g - 1, RING) + max(k + 1, 2))
                if what in ("u0", "u1"):
                    d = int(what[1])
                    pe.wait_ge(u0_ready, gcnt(s, g))
                    for c in range(GC):
                        ins = pe.transpose(dst[:, c * P:(c + 1) * P], u0[:, c, d * P:(d + 1) * P], ident[:])
                elif what == "bd":
                    pe.wait_ge(a_free, gcnt(s, g - 1, RING) + 4)
                    n0 = STATE + HEADS
                    for c in range(GC):
                        for d in range(DK):
                            ins = pe.matmul(dst[:, c * n0:(c + 1) * n0], ut[:, d, c * P:(c + 1) * P], win_bd[:, d],
                                            start=d == 0, stop=d == DK - 1)
                elif what == "cb":
                    pe.wait_ge(ul_ready, gcnt(s, g, 2))
                    for d in range(DK):
                        ins = split_matmul(pe, dst[:], [w[:, d, 2 * INNER:2 * INNER + 2 * STATE] for w in winp],
                                           [u[:, h, d] for u in utp], d == 0, d == DK - 1)
                elif what == "cum":
                    pe.wait_ge(a_ready, gcnt(s, g))
                    n = GC * HEADS
                    for j, m in enumerate((le, gt, ones)):
                        ins = pe.matmul(dst[:, j * n:(j + 1) * n], m[:], aa[:, h].rearrange("p c n -> p (c n)"),
                                        start=True, stop=True)
                else:
                    f = int(what[1])
                    for d in range(DK):
                        ins = split_matmul(pe, dst[:], [w[:, d, f * P:(f + 1) * P] for w in winp],
                                           [u[:, h, d] for u in utp], d == 0, d == DK - 1)
                ins.then_inc(a_full, 1)

        def inner_x(s, n):
            h, k = gpar(n)
            if n:
                pe.wait_ge(xs_ready, cnt(s, n - 1))
            for d in range(DK):
                ins = split_matmul(pe, px[:], [u[:, h, d, k * P:(k + 1) * P] for u in utp],
                                   [w[:, d, INNER:2 * INNER] for w in winp], d == 0, d == DK - 1)
            ins.then_inc(x_full, 1)

        def segment_sums(s, n):
            pe.wait_ge(segr_ready, cnt(s, n))
            if n:
                pe.wait_ge(l_ready, cnt(s, n - 1))
                pe.wait_ge(xft_ready, s * CPS + (max(n - 3, 0) + 1))
                pe.wait_ge(sc_ready, s * CPS + (max(n - 3, 0) + 1))
            for j in range(2):
                for part in (1, 0):
                    ins = pe.matmul(ps[j][:], gtr[:], segr[part][:, 4 * j:4 * j + 4].rearrange("p h i -> p (h i)"),
                                    start=part == 1, stop=part == 0)
            ins.then_inc(seg_full, 1)

        def scores_cb(s, n):
            h, k = gpar(n)
            pe.wait_ge(a_free, gcnt(s, n // GC - 1, RING) + (GROUP_PRODUCTS.index("cb") + 3))
            if n % CPS:
                pe.wait_ge(st_ready, states(s, n - 1))
            elif n:
                pe.wait_ge(gm_ready, cnt(s, n - 1))
            pe.matmul(pg[:, 0:P], bt[:, h, k * P:(k + 1) * P], ct[:, h, k * P:(k + 1) * P], start=True, stop=True) \
                .then_inc(g_full, 1)

        def new_state(s, n):
            h, k = gpar(n)
            pe.wait_ge(wx_ready, cnt(s, n))
            pe.wait_ge(gm_ready, cnt(s, n))
            pe.matmul(pg[0:STATE, :], bd[:, h, k, 0:STATE], wx[:, par(n)], start=True, stop=True).then_inc(n_full, 1)

        def transposed(s, n):
            pe.wait_ge(y_ready, cnt(s, n))
            for f in range(FB):
                ins = pe.transpose(py[:, f * P:(f + 1) * P], y[:, par(n), f * P:(f + 1) * P], ident[:])
            ins.then_inc(yt_full, 1)

        def out_proj(s, n):
            pe.wait_ge(gate_ready, cnt(s, n))
            if (n + 1) % CPS == 0:
                pe.wait_ge(xp_ready, cnt(s, n - 1))
            for f in range(FB):
                ins = pe.matmul(po[:, 0:D], gT[:, par(n), f * P:(f + 1) * P], wouts[:, f], start=f == 0,
                                stop=f == FB - 1)
            ins.then_inc(o_full, 1)

        def within(s, n):
            pe.wait_ge(m_ready, cnt(s, n))
            pe.wait_ge(dtx_ready, cnt(s, n))
            if n:
                pe.wait_ge(gate_ready, cnt(s, n - 1))
            for hh in range(HEADS):
                ins = pe.matmul(py[:, hh * HD:(hh + 1) * HD], lm[:, par(n), hh], dtx[:, par(n), hh * HD:(hh + 1) * HD],
                                start=True, stop=True)
            ins.then_inc(yi_full, 1)

        def across(s, n):
            h, k = gpar(n)
            pe.wait_ge(st_ready, states(s, n - 1))
            if n >= 2:
                pe.wait_ge(xp_ready, cnt(s, n - 2))
            pe.matmul(po[:], ct[:, h, k * P:(k + 1) * P], hst[:, par(n)], start=True, stop=True).then_inc(ye_full, 1)

        def turn_xf(s, n, exps):
            pe.wait_ge(xf_ready, cnt(s, n))
            pe.wait_ge(l_ready, cnt(s, exps))
            pe.wait_ge(sc_ready, s * CPS + (n + 1))
            for d in range(DK):
                ins = pe.transpose(ps[0][:, d * P:(d + 1) * P], xf[:, par(n), d * P:(d + 1) * P], ident[:])
            ins.then_inc(xft_full, 1)

        def router(s, n):
            pe.wait_ge(xft_ready, s * CPS + (n + 2))
            for d in range(DK):
                ins = pe.matmul(ps[1][:, 0:NE], xft[:, par(n), d], wrs[:, d], start=d == 0, stop=d == DK - 1)
            ins.then_inc(sc_full, 1)

        group(0, 0, ["u0", "u1"])
        pe.wait_ge(c_load, 16 * NLOADS)
        group(0, 0, ["bd"])
        pe.wait_ge(high_ready, 2)
        pe.wait_ge(parts_ready, 1)
        group(0, 0, GROUP_PRODUCTS[GROUP_PRODUCTS.index("bd") + 1:])
        inner_x(0, 0)
        segment_sums(0, 0)
        scores_cb(0, 0)
        within(0, 0)

        def step(s, c, end):
            k, g = c % GC, c // GC + 1

            def place(name):
                if group_here(g, end):
                    group(s, g, PLACES[k].get(name, ()))

            if here(c, end) and c % CPS != CPS - 1:
                new_state(s, c)
            if here(c + 1, end):
                inner_x(s, c + 1)
            place("first")
            if here(c + 1, end):
                segment_sums(s, c + 1)
            if here(c, end):
                transposed(s, c)
            if here(c + 1, end):
                scores_cb(s, c + 1)
            place("a")
            if here(c - 1, end):
                out_proj(s, c - 1)
            if here(c - 2, end):
                turn_xf(s, c - 2, c + 1 if here(c + 1, end) else CPS - 1)
            place("b")
            if here(c - 2, end):
                router(s, c - 2)
            if here(c + 1, end):
                within(s, c + 1)
                if (c + 1) % CPS:
                    across(s, c + 1)
            place("c")

        for c in FIRST:
            step(0, c, False)
        with pe.Fori(0, BATCH - 1) as s:
            for c in ROUND:
                step(s, c, False)
        for c in ROUND:
            step(BATCH - 1, c, True)


PLACES = [{}, {"a": ["u0", "u1"], "b": ["bd"]}, {"a": ["cb"], "b": ["z0"], "c": ["cum"]},
          {"b": ["z1", "z2"], "c": ["z3"]}]


def route(nc, ctx, consts, scores, router_rows, tab, wh, wl, rows, rows_in, b3, we, b1):
    def sb(name, shape, dt=F32):
        return ctx.enter_context(nc.sbuf_tensor(name, shape, dt))

    def sem(name):
        return ctx.enter_context(nc.semaphore(name))

    lt, ones = consts["lt"], consts["ones"]
    te = [P, CHUNKS, NE]
    early = NE * 2 * HID - (RAWS - 1) * PIECE
    raw = [sb("raw", [P, PIECE])[:]] + [rows[:, early + k * PIECE:early + (k + 1) * PIECE] for k in range(RAWS - 1)]
    brs, bns, ebs = router_rows
    eb_rest, eb3 = sb("eb_rest", [P, NE * D // P]), \
        sb("eb3", [P, 3, NE * D // P], BF16)
    top, wts, biased, cand = sb("top", [P, CHUNKS]), sb("wts", te), sb("biased", te), sb("cand", te)
    pick = sb("pick", [P, TOPK, CHUNKS, NE])
    order = sb("order", [P, NE])
    val = sb("val", [P, TOPK, CHUNKS])
    total = sb("total", [P, CHUNKS])
    chosen = sb("chosen", te)
    before = [wts, chosen]
    many, iota_k = cand[:].rearrange("p c e -> p (c e)").rearrange("p (e c) -> p e c", e=NE), \
        sb("iota_k", [P, CHUNKS])
    tiles = sb("tiles", [P, NE])
    upto = [sb("upto0", [P, NE]), sb("upto1", [P, NE])]
    base = sb("base", [P, NE])
    slot, slots = biased, sb("slots", [P, TOPK, CHUNKS])
    slot_i, tile_i, row_i = (sb(n, [P, CHOICES], I32) for n in ("slot_i", "tile_i", "row_i"))
    tile_f, row_f = sb("tile_f", [P, CHOICES]), slots[:].rearrange("p k c -> p (k c)")
    iota_r, iota_t = sb("iota_r", [P, P]), sb("iota_t", [P, TILES])
    token1 = sb("token1", [P, TOPK, CHUNKS])
    spare = sb("spare", [P, 1])
    RINGS = 4
    hot_t = sb("hot_t", [P, RINGS, 2, TILES])
    hot_r = sb("hot_r", [P, RINGS, P])
    named = cand[:].rearrange("p c e -> p (c e)")[:, 0:2 * TILES].rearrange("p (j t) -> p j t", j=2)
    empty, dest = (biased[:].rearrange("p c e -> p (c e)")[:, k * TILES:(k + 1) * TILES] for k in range(2))
    ex_t = hot_t[0:1].rearrange("p r j t -> p (r j t)").rearrange("p (t e) -> p t e", e=NE)
    ex_f = sb("ex_f", [1, TILES])
    pr = ctx.enter_context(nc.psum_tensor("pr", [P, 512], F32))
    pt = ctx.enter_context(nc.psum_tensor("pt", [P, 512], F32))

    w_in = [sem(f"w_in{k}") for k in range(RAWS)]
    wh_ready, rest_ready, wl_ready = (sem(n) for n in ("wh_ready", "rest_ready", "wl_ready"))
    loaded, b_out, iotas, e_in, e_out, chosen_ready, counted = (
        sem(n) for n in ("r_loaded", "b_out", "iotas", "e_in", "e_out", "chosen_ready", "counted"))
    onehot, tabled, did = sem("onehot"), sem("tabled"), sem("route_did")
    block = ctx.enter_context(nc.Block())

    @block.sync
    def _(sp):
        for n in range(PIECES):
            if n >= RAWS:
                sp.wait_ge(wl_ready, n - RAWS + 1)
            sp.dma_start(raw[n % RAWS], we[:, n * PIECE:(n + 1) * PIECE]).then_inc(w_in[n % RAWS], 16)
            if n == PIECES // 2:
                sp.wait_ge(b_out, 1)
                for k in range(3):
                    sp.dma_start(b3[k:k + 1, :], eb3[:, k]).then_inc(loaded, 16)
        sp.dma_start(rows[:, 0:early], b1[0, 0:early].partition_broadcast(P)).then_inc(loaded, 16)
        sp.wait_ge(loaded, 16 * (3 + 1))
        sp.wait_ge(wl_ready, PIECES)
        sp.dma_start(rows[:, early:], b1[0, early:].partition_broadcast(P)).then_inc(rows_in, 16)

    @block.gpsimd
    def _(pool):
        for t, pattern, start, mult in ((order[:], [[-1, NE]], NE, 0), (iota_k[:], [[P, CHUNKS]], 0, 0),
                                        (iota_r[:], [[1, P]], 0, 0), (iota_t[:], [[1, TILES]], 0, 0),
                                        (token1[:], [[0, TOPK], [P, CHUNKS]], 1, 1), (spare[:], [[0, 1]], TOKENS + 1, 1)):
            pool.iota(t, pattern=pattern, base=start, channel_multiplier=mult,
                      allow_small_or_imprecise_dtypes=True).then_inc(iotas, 1)
        pool.memset(tab["gather"][:, TILES:], 0)
        pool.memset(tab["expert"][:, TILES:], 0).then_inc(iotas, 1)
        for n in range(PIECES):
            pool.wait_ge(wh_ready, n + 1)
            piece = raw[n % RAWS]
            pool.tensor_tensor(piece, piece, wh[:, n * PIECE:(n + 1) * PIECE].bitcast(F32), ALU.subtract) \
                .then_inc(rest_ready, 1)

    @block.scalar
    def _(act):
        def high(n):
            act.wait_ge(w_in[n % RAWS], 16 * (n // RAWS + 1))
            act.activation(wh[:, n * PIECE:(n + 1) * PIECE], raw[n % RAWS], ACT.Identity).then_inc(wh_ready, 1)

        def low(n):
            act.wait_ge(rest_ready, n + 1)
            act.activation(wl[:, n * PIECE:(n + 1) * PIECE], raw[n % RAWS], ACT.Identity, scale=LOW) \
                .then_inc(wl_ready, 1)

        for n in range(PIECES):
            high(n)
            if n == 1:
                act.wait_ge(e_in, 1)
                act.activation(wts[:], wts[:], ACT.Exp).then_inc(e_out, 1)
            if n:
                low(n - 1)
        low(PIECES - 1)

    @block.vector
    def _(dve):
        steps = Steps(dve, did)
        do = steps.link

        def per_chunk(t):
            return t.unsqueeze(2).to_broadcast(te)

        def per_expert(t):
            return t[:].unsqueeze(1).to_broadcast(te)

        do(dve.tensor_tensor(scores[:], scores[:], per_expert(brs), ALU.add))
        do(dve.tensor_reduce(top[:], scores[:], AX_X, ALU.max))
        dve.tensor_tensor(wts[:], scores[:], per_chunk(top[:]), ALU.subtract).then_inc(e_in, 1)
        do(dve.tensor_tensor(biased[:], scores[:], per_expert(bns), ALU.add))
        dve.wait_ge(iotas, 7)
        for k in range(TOPK):
            do(dve.tensor_reduce(top[:], biased[:], AX_X, ALU.max))
            do(dve.tensor_tensor(cand[:], biased[:], per_chunk(top[:]), ALU.is_equal))
            do(dve.tensor_tensor(cand[:], cand[:], per_expert(order), ALU.mult))
            do(dve.tensor_reduce(top[:], cand[:], AX_X, ALU.max))
            do(dve.tensor_tensor(pick[:, k], cand[:], per_chunk(top[:]), ALU.is_equal))
            if k == 0:
                do(dve.scalar_tensor_tensor(biased[:], pick[:, 0], -3e38, biased[:], ALU.mult, ALU.add))
        dve.tensor_tensor(chosen[:], pick[:, 0], pick[:, 1], ALU.add).then_inc(chosen_ready, 1)
        dve.wait_ge(e_out, 1)
        do(dve.tensor_reduce(total[:], wts[:], AX_X, ALU.add))
        do(dve.reciprocal(total[:], total[:]))
        do(dve.tensor_tensor(wts[:], wts[:], per_chunk(total[:]), ALU.mult))
        for k in range(TOPK):
            do(dve.tensor_tensor(cand[:], wts[:], pick[:, k], ALU.mult))
            do(dve.tensor_reduce(val[:, k], cand[:], AX_X, ALU.add))
        do(dve.tensor_tensor(total[:], val[:, 0], val[:, 1], ALU.add))
        do(dve.reciprocal(total[:], total[:]))
        do(dve.tensor_tensor(val[:], val[:], total[:].unsqueeze(1).to_broadcast([P, TOPK, CHUNKS]), ALU.mult))
        dve.wait_ge(counted, 1)
        do(dve.tensor_copy(before[0][:], pt[:, 0:CHUNKS * NE].rearrange("p (c e) -> p c e", e=NE)))
        src, far = 0, 1
        while far < CHUNKS:
            a, b = before[src], before[1 - src]
            steps.did(dve.tensor_copy(b[:, 0:far], a[:, 0:far]))
            do(dve.tensor_tensor(b[:, far:], a[:, far:], a[:, 0:CHUNKS - far], ALU.add))
            src, far = 1 - src, 2 * far
        upto_chunk = before[src]
        do(dve.tensor_tensor(many, upto_chunk[:, CHUNKS - 1].unsqueeze(2).to_broadcast([P, NE, CHUNKS]),
                             iota_k[:].unsqueeze(1).to_broadcast([P, NE, CHUNKS]), ALU.is_gt))
        do(dve.tensor_reduce(tiles[:], many, AX_X, ALU.add))
        do(dve.tensor_copy(upto[0][:], tiles[:]))
        s2, far = 0, 1
        while far < NE:
            a, b = upto[s2], upto[1 - s2]
            steps.did(dve.tensor_copy(b[:, 0:far], a[:, 0:far]))
            do(dve.tensor_tensor(b[:, far:], a[:, far:], a[:, 0:NE - far], ALU.add))
            s2, far = 1 - s2, 2 * far
        last_tile = upto[s2]
        do(dve.tensor_tensor(base[:], last_tile[:], tiles[:], ALU.subtract))
        do(dve.tensor_tensor(slot[:], upto_chunk[:], pt[:, 0:CHUNKS * NE].rearrange("p (c e) -> p c e", e=NE),
                             ALU.subtract))
        do(dve.tensor_tensor(slot[:], slot[:], pr[:, 0:CHUNKS * NE].rearrange("p (c e) -> p c e", e=NE), ALU.add))
        do(dve.scalar_tensor_tensor(slot[:], per_expert(base), float(P), slot[:], ALU.mult, ALU.add))
        for k in range(TOPK):
            do(dve.tensor_tensor(cand[:], slot[:], pick[:, k], ALU.mult))
            do(dve.tensor_reduce(slots[:, k], cand[:], AX_X, ALU.add))
        flat = slots[:].rearrange("p k c -> p (k c)")
        do(dve.tensor_copy(slot_i[:], flat))
        do(dve.tensor_scalar(tile_i[:], slot_i[:], P.bit_length() - 1, None, ALU.arith_shift_right))
        do(dve.tensor_scalar(row_i[:], slot_i[:], P - 1, None, ALU.bitwise_and))
        do(dve.tensor_copy(tile_f[:], tile_i[:]))
        do(dve.tensor_copy(row_f, row_i[:]))
        do(dve.tensor_copy(eb3[:, 0], ebs[:]))
        do(dve.tensor_tensor(eb_rest[:], ebs[:], eb3[:, 0], ALU.subtract))
        do(dve.tensor_copy(eb3[:, 1], eb_rest[:]))
        do(dve.tensor_tensor(eb_rest[:], eb_rest[:], eb3[:, 1], ALU.subtract))
        dve.tensor_copy(eb3[:, 2], eb_rest[:]).then_inc(b_out, 1)
        number, weight = token1[:].rearrange("p k c -> p (k c)"), val[:].rearrange("p k c -> p (k c)")
        for a in range(CHOICES):
            if a >= RINGS:
                dve.wait_ge(tabled, a - RINGS + 1)
            dve.tensor_scalar(hot_r[:, a % RINGS], iota_r[:], row_f[:, a:a + 1], None, ALU.is_equal)
            for j, value in enumerate((number, weight)):
                ins = dve.tensor_scalar(hot_t[:, a % RINGS, j], iota_t[:], tile_f[:, a:a + 1], value[:, a:a + 1],
                                        ALU.is_equal, ALU.mult)
            ins.then_inc(onehot, 1)
        dve.wait_ge(tabled, CHOICES)
        do(dve.tensor_tensor(ex_t, last_tile[0:1].unsqueeze(1).to_broadcast([1, TILES, NE]),
                             iota_t[0:1].unsqueeze(2).to_broadcast([1, TILES, NE]), ALU.is_le))
        do(dve.tensor_reduce(ex_f[:], ex_t, AX_X, ALU.add))
        do(dve.tensor_scalar(tab["expert"][:, 0:TILES], ex_f[:], float(NE - 1), None, ALU.min))
        do(dve.tensor_copy(named, pr[:, 0:2 * TILES].rearrange("p (j t) -> p j t", j=2)))
        do(dve.tensor_copy(tab["weight"][:], named[:, 1]))
        do(dve.tensor_scalar(tab["gather"][:, 0:TILES], named[:, 0], 1.0, 0.0, ALU.subtract, ALU.max))
        do(dve.tensor_scalar(empty, named[:, 0], 0.0, spare[:], ALU.is_equal, ALU.mult))
        do(dve.scalar_tensor_tensor(dest, named[:, 0], 1.0, empty, ALU.subtract, ALU.add))
        do(dve.tensor_copy(tab["scatter"][:], dest))

    @block.tensor
    def _(pe):
        flat = chosen[:].rearrange("p c e -> p (c e)")
        pe.wait_ge(chosen_ready, 1)
        pe.matmul(pr[:, 0:CHUNKS * NE], lt[:], flat, start=True, stop=True)
        pe.matmul(pt[:, 0:CHUNKS * NE], ones[:], flat, start=True, stop=True).then_inc(counted, 1)
        for a in range(CHOICES):
            pe.wait_ge(onehot, a + 1)
            pe.matmul(pr[:, 0:2 * TILES], hot_r[:, a % RINGS], hot_t[:, a % RINGS].rearrange("p j t -> p (j t)"),
                      start=a == 0, stop=a == CHOICES - 1).then_inc(tabled, 1)


def experts(nc, ctx, consts, tab, wh, wl, rows, rows_in, b3, xf_dram, out):
    def sb(name, shape, dt=F32):
        return ctx.enter_context(nc.sbuf_tensor(name, shape, dt))

    def sem(name):
        return ctx.enter_context(nc.semaphore(name))

    def bank(name):
        return ctx.enter_context(nc.psum_tensor(name, [P, 512], F32))

    ident = consts["ident"]
    ones3 = sb("ones3", [3, P], BF16)
    scratch, scratched = sb("scratch_pool", [1, 2]), sem("scratched_pool")
    ig, isc = sb("ig", [P, AHEAD], U32), sb("isc", [P, 2], U32)
    wt = sb("wt", [P, 2])
    xg = sb("xg", [P, AHEAD, D])
    xth, xtl, xts = sb("xth", [P, 2, D], F32R), sb("xtl", [P, 2, D], F32R), sb("xts", [P, 2, D], F16)
    hth, htl, hts = sb("hth", [P, HID], F32R), sb("htl", [P, HID], F32R), sb("hts", [P, HID], F16)
    ga, up_, hh = sb("ga", [P, HID]), sb("up_", [P, HID]), sb("hh", [P, HID])
    tg = consts["squares"]
    yw = sb("yw", [P, 2, D])
    pa_, pb_ = [bank("pha0"), bank("pha1")], [bank("phb0"), bank("phb1")]
    pxt, pht, pyy = bank("pxt"), bank("pht"), bank("pyy")

    (ig_ready, xt_full, xth_ready, xts_ready, xtl_ready, a_full, h_full, tanh_ready, hh_ready, ht_full, hth_ready,
     hts_ready, htl_ready, y_full, wt_ready, yw_ready, is_ready, ones_ready, sg_ready, ga_ready,
     up_ready) = (
        sem(n) for n in ("ig_ready", "xt_full", "xth_ready", "xts_ready", "xtl_ready", "e_a_full", "h_full",
                         "tanh_ready", "hh_ready", "ht_full", "hth_ready", "hts_ready", "htl_ready", "y_full",
                         "wt_ready", "yw_ready", "is_ready", "ones_ready", "sg_ready", "ga_ready", "up_ready"))
    gathered = [sem(f"gathered{k}") for k in range(AHEAD)]
    added = sem("added")
    block = ctx.enter_context(nc.Block())
    ROUNDS = TILES // UNROLL

    @block.gpsimd
    def _(pool):
        pool.memset(scratch[:], 0.0).then_inc(scratched, 1)
        pool.wait_ge(scratched, 1)

        def gather(i, j):
            k = j % AHEAD
            pool.tensor_copy(ig[:, k:k + 1], tab["gather"][:, bass.ds(UNROLL * i + j, 1)]).then_inc(ig_ready, 1)
            pool.wait_ge(ig_ready, UNROLL * i + (j + 1))
            wait_here(pool, scratch)
            pool.indirect_dma_start(xg[:, k], None, xf_dram, bass.IndirectOffsetOnAxis(ap=ig[:, k:k + 1], axis=0)) \
                .then_inc(gathered[k], 16)

        for j in range(AHEAD):
            gather(0, j)

        def body(i, last):
            for j in range(UNROLL):
                if not last or j + AHEAD < UNROLL:
                    pool.wait_ge(xt_full, UNROLL * i + (j + 2))
                    gather(i, j + AHEAD)
                pool.tensor_copy(isc[:, j % 2:j % 2 + 1], tab["scatter"][:, bass.ds(UNROLL * i + j, 1)]) \
                    .then_inc(is_ready, 1)
                pool.wait_ge(is_ready, UNROLL * i + (j + 1))
                pool.wait_ge(yw_ready, UNROLL * i + (j + 1))
                if not (isinstance(i, int) and i == 0 and j == 0):
                    pool.wait_ge(added, 16 * UNROLL * i + 16 * j)
                wait_here(pool, scratch)
                pool.indirect_dma_start(out, bass.IndirectOffsetOnAxis(ap=isc[:, j % 2:j % 2 + 1], axis=0),
                                        yw[:, j % 2], None, compute_op=ALU.add).then_inc(added, 16)

        body(0, False)
        with pool.Fori(1, ROUNDS - 1) as i:
            body(i, False)
        body(ROUNDS - 1, True)
        pool.wait_ge(added, 16 * TILES)

    @block.scalar
    def _(act):
        def xt_copy(i, j):
            b = j % 2
            act.wait_ge(xt_full, UNROLL * i + (j + 2))
            act.activation(xts[:, b], pxt[:, 0:D], ACT.Identity, scale=1.0 / LOW).then_inc(xts_ready, 1)
            act.activation(xth[:, b], pxt[:, 0:D], ACT.Identity).then_inc(xth_ready, 1)

        def tanh(i, j):
            act.wait_ge(ga_ready, UNROLL * i + (j + 1))
            act.activation(tg[:], ga[:], ACT.Tanh, scale=0.5).then_inc(tanh_ready, 1)

        def ht_copy(i, j):
            act.wait_ge(ht_full, UNROLL * i + (j + 1))
            act.activation(hts[:], pht[:], ACT.Identity, scale=1.0 / LOW).then_inc(hts_ready, 1)
            act.activation(hth[:], pht[:], ACT.Identity).then_inc(hth_ready, 1)

        xt_copy(0, 0)
        xt_copy(0, 1)
        tanh(0, 0)

        def body(i, last):
            for j in range(UNROLL):
                if not last or j + 2 < UNROLL:
                    xt_copy(i, j + 2)
                ht_copy(i, j)
                if not last or j + 1 < UNROLL:
                    tanh(i, j + 1)

        with act.Fori(0, ROUNDS - 1) as i:
            body(i, False)
        body(ROUNDS - 1, True)

    @block.vector
    def _(dve):
        dve.memset(ones3[:], 1.0).then_inc(ones_ready, 1)

        def low_x(i, j):
            dve.wait_ge(xth_ready, UNROLL * i + (j + 1))
            dve.tensor_tensor(xtl[:, j % 2], pxt[:, 0:D], xth[:, j % 2].bitcast(F32), ALU.subtract) \
                .then_inc(xtl_ready, 1)

        def low_h(i, j):
            dve.wait_ge(hth_ready, UNROLL * i + (j + 1))
            dve.tensor_tensor(htl[:], pht[:], hth[:].bitcast(F32), ALU.subtract).then_inc(htl_ready, 1)

        def expert(i, j):
            return dve.value_load(tab["expert"][0:1, bass.ds(UNROLL * i + j, 1)], min_val=0, max_val=NE - 1)

        def biased(i, j, half, e):
            bank, dst, full, ready = ((pa_, ga, a_full, ga_ready), (pb_, up_, h_full, up_ready))[half]
            dve.wait_ge(full, UNROLL * i + (j + 1))
            if not (isinstance(i, int) and i == 0 and j == 0):
                dve.wait_ge(hh_ready, UNROLL * i + j)
            dve.tensor_tensor(dst[:], bank[j % 2][:], rows[:, bass.ds(e * 2 * HID + half * HID, HID)], ALU.add) \
                .then_inc(ready, 1)

        def gated(i, j):
            dve.wait_ge(tanh_ready, UNROLL * i + (j + 1))
            dve.scalar_tensor_tensor(ga[:], tg[:], 1.0, ga[:], ALU.add, ALU.mult).then_inc(sg_ready, 1)
            dve.wait_ge(sg_ready, UNROLL * i + (j + 1))
            dve.wait_ge(up_ready, UNROLL * i + (j + 1))
            dve.scalar_tensor_tensor(hh[:], ga[:], 0.5, up_[:], ALU.mult, ALU.mult).then_inc(hh_ready, 1)

        def weigh(i, j):
            b = j % 2
            dve.tensor_copy(wt[:, b:b + 1], tab["weight"][:, bass.ds(UNROLL * i + j, 1)]).then_inc(wt_ready, 1)
            dve.wait_ge(wt_ready, UNROLL * i + (j + 1))
            dve.wait_ge(y_full, UNROLL * i + (j + 1))
            if not (isinstance(i, int) and i == 0 and j < 2):
                dve.wait_ge(added, 16 * UNROLL * i + 16 * (j - 1))
            dve.tensor_scalar(yw[:, b], pyy[:, 0:D], wt[:, b:b + 1], None, ALU.mult).then_inc(yw_ready, 1)

        low_x(0, 0)
        first = expert(0, 0)
        dve.wait_ge(rows_in, 16)
        biased(0, 0, 0, first)
        low_x(0, 1)
        biased(0, 0, 1, first)
        gated(0, 0)

        def body(i, last):
            for j in range(UNROLL):
                more = not last or j + 1 < UNROLL
                ahead = expert(i, j + 1) if more else None
                if not last or j + 2 < UNROLL:
                    low_x(i, j + 2)
                if more:
                    biased(i, j + 1, 0, ahead)
                low_h(i, j)
                if more:
                    biased(i, j + 1, 1, ahead)
                    gated(i, j + 1)
                weigh(i, j)

        body(0, False)
        with dve.Fori(1, ROUNDS - 1) as i:
            body(i, False)
        body(ROUNDS - 1, True)

    @block.tensor
    def _(pe):
        pe.sem_inc(xt_full, 1)
        pe.wait_ge(ones_ready, 1)

        def transpose_x(i, j, guard=True):
            k = j % AHEAD
            pe.wait_ge(gathered[k], 16 * (UNROLL // AHEAD) * i + 16 * (j // AHEAD + 1))
            if guard:
                pe.wait_ge(xtl_ready, UNROLL * i + j)
            for d in range(DK):
                ins = pe.transpose(pxt[:, d * P:(d + 1) * P], xg[:, k, d * P:(d + 1) * P], ident[:])
            ins.then_inc(xt_full, 1)

        def expert(i, j):
            return pe.value_load(tab["expert"][0:1, bass.ds(UNROLL * i + j, 1)], min_val=0, max_val=NE - 1)

        def up(i, j, half, e, guard=True):
            b = j % 2
            if guard:
                pe.wait_ge(hh_ready, UNROLL * i + (j - 1))
            pe.wait_ge(xth_ready, UNROLL * i + (j + 1))
            pe.wait_ge(xtl_ready, UNROLL * i + (j + 1))
            dst = (pa_[b], pb_[b])[half]
            for d in range(DK):
                here, at = slice(d * P, (d + 1) * P), bass.ds(e * EW + (d * 2 * HID + half * HID), HID)
                pe.matmul(dst[:], xts[:, b, here], wl[:, at], start=d == 0, stop=False)
                pe.matmul(dst[:], xtl[:, b, here], wh[:, at], start=False, stop=False)
                ins = pe.matmul(dst[:], xth[:, b, here], wh[:, at], start=False, stop=d == DK - 1)
            ins.then_inc((a_full, h_full)[half], 1)

        def transpose_h(i, j):
            b = j % 2
            pe.wait_ge(hh_ready, UNROLL * i + (j + 1))
            if not (isinstance(i, int) and i == 0 and j == 0):
                pe.wait_ge(htl_ready, UNROLL * i + j)
            for f in range(FB):
                ins = pe.transpose(pht[:, f * P:(f + 1) * P], hh[:, f * P:(f + 1) * P], ident[:])
            ins.then_inc(ht_full, 1)

        def down(i, j, e):
            b = j % 2
            if not (isinstance(i, int) and i == 0 and j == 0):
                pe.wait_ge(yw_ready, UNROLL * i + j)
            pe.matmul(pyy[:, 0:D], ones3[:], b3[:, bass.ds(e * D, D)], start=True, stop=False)
            for part, weights, ready in ((hts, wl, hts_ready), (hth, wh, hth_ready), (htl, wh, htl_ready)):
                pe.wait_ge(ready, UNROLL * i + (j + 1))
                for f in range(FB):
                    ins = pe.matmul(pyy[:, 0:D], part[:, f * P:(f + 1) * P],
                                    weights[:, bass.ds(e * EW + (EW1 + f * D), D)], start=False,
                                    stop=part is htl and f == FB - 1)
            ins.then_inc(y_full, 1)

        transpose_x(0, 0, guard=False)
        first = expert(0, 0)
        up(0, 0, 0, first, guard=False)
        transpose_x(0, 1)
        up(0, 0, 1, first, guard=False)

        def body(i, last):
            ahead = expert(i, 1)
            for j in range(UNROLL):
                more, guard = not last or j + 1 < UNROLL, not (isinstance(i, int) and i == 0 and j == 0)
                if not last or j + 2 < UNROLL:
                    transpose_x(i, j + 2)
                if more:
                    up(i, j + 1, 0, ahead, guard)
                here = expert(i, j)
                transpose_h(i, j)
                if more:
                    up(i, j + 1, 1, ahead, guard)
                if j + 1 < UNROLL and (not last or j + 2 < UNROLL):
                    ahead = expert(i, j + 2)
                down(i, j, here)

        body(0, False)
        with pe.Fori(1, ROUNDS - 1) as i:
            body(i, False)
        body(ROUNDS - 1, True)


def kernel(**inputs):
    import numpy as np
    import concourse.bacc as bacc
    from concourse.bass_utils import run_bass_kernel_spmd

    def arr(name):
        return np.asarray(inputs["L0_" + name])

    def blocks(w):
        return w.reshape(-1, P, w.shape[-1]).transpose(1, 0, 2)

    b_in, w_in = arr("attn_b_in"), arr("attn_W_in")
    n_b = 2 * INNER
    w_in = np.concatenate([w_in[:, :n_b], w_in[:, n_b + STATE:n_b + 2 * STATE], w_in[:, n_b:n_b + STATE],
                           w_in[:, n_b + 2 * STATE:]], axis=1)
    laid = {
        "x": arr("attn_input_tensor").reshape(TOKENS, D),
        "win": blocks(w_in), "wout": blocks(arr("attn_W_out")),
        "gam": arr("attn_ln_gamma").reshape(DK, P).T, "bet": arr("attn_ln_beta").reshape(DK, P).T,
        "bz": b_in[:INNER].reshape(FB, P).T,
        "bcb": np.concatenate([b_in[n_b + STATE:n_b + 2 * STATE], b_in[n_b:n_b + STATE]]).reshape(2 * STATE, 1),
        "bx": b_in[INNER:n_b].reshape(1, INNER),
        "bdt": np.concatenate([b_in[n_b:n_b + STATE], b_in[PROJ - HEADS:]]).reshape(1, -1),
        "alog": arr("attn_A_log").reshape(1, HEADS), "dskip": arr("attn_D_skip").reshape(1, HEADS),
        "dtb": arr("attn_dt_bias").reshape(1, HEADS), "bout": arr("attn_b_out").reshape(1, D),
        "wr": blocks(arr("ffn_Wr").T), "br": arr("ffn_br").reshape(1, NE), "bn": arr("ffn_biases_N").reshape(1, NE),
        "we": np.concatenate([arr("ffn_Wl1").reshape(NE, DK, P, 2 * HID).transpose(2, 0, 1, 3).reshape(P, NE, EW1),
                              arr("ffn_Wl2").reshape(NE, FB, P, D).transpose(2, 0, 1, 3).reshape(P, NE, FB * D)],
                             axis=2).reshape(P, NE * EW),
        "b1": arr("ffn_bl1").reshape(1, NE * 2 * HID), "b2": arr("ffn_bl2").reshape(P, NE * D // P),
    }
    laid = {k: np.ascontiguousarray(v) for k, v in laid.items()}
    nc = bacc.Bacc("TRN2", target_bir_lowering=False, num_devices=1)
    aps = {k: nc.dram_tensor("in_" + k, v.shape, mybir.dt.from_np(v.dtype), kind="ExternalInput").ap()
           for k, v in laid.items()}
    out = nc.dram_tensor("out_rows", (TOKENS + P, D), F32, kind="ExternalOutput").ap()
    build(nc, out=out, **aps)
    r = run_bass_kernel_spmd(nc, [{"in_" + k: v for k, v in laid.items()}], core_ids=[0])
    return r.results[0]["out_rows"][:TOKENS].reshape(BATCH, SEQ, D)
```
